# Optimizing a Trainium2 kernel written in Bass

```python
import numpy as np
import jax
import jax.numpy as jnp

def _softmax(x, axis=-1):
    return jax.nn.softmax(x, axis=axis)

def _gelu(x):
    return jax.nn.gelu(x, approximate=True)

def _silu(x):
    return jax.nn.silu(x)

def _sigmoid(x):
    return jax.nn.sigmoid(x)

def _layernorm(x, axis=-1, eps=1e-05):
    m = jnp.mean(x, axis=axis, keepdims=True)
    v = jnp.var(x, axis=axis, keepdims=True)
    return (x - m) / jnp.sqrt(v + eps)

def _scatter_add(tgt, idx, src, axis=0):
    return tgt.at[idx].add(src)

def _segment_sum(src, seg, n):
    return jax.ops.segment_sum(src, seg, n)
kernel_name = 'mk_gnn_resnorm_d4_gnn_r32_faa80c'

def setup_inputs(seed: int=0):
    np.random.seed(seed)
    _w = jnp.asarray

    def _rec_inputs():
        import jax
        import jax.numpy as jnp
        _gk = jax.random.key(seed)
        x = -8.776e-05 + 1 * jax.random.normal(jax.random.fold_in(_gk, 1), (3125, 128), jnp.float32)
        src = jax.random.randint(jax.random.fold_in(_gk, 2), (100000,), 0, 3125, jnp.int32)
        dst = jnp.minimum((3125 * jax.random.uniform(jax.random.fold_in(_gk, 3), (100000,)) ** 2.0).astype(jnp.int32), 99999)
        _o = jnp.argsort(dst, stable=True)
        src = src[_o]
        dst = dst[_o]
        edge_attr_16 = 0.000196303 + 1.00016 * jax.random.normal(jax.random.fold_in(_gk, 11), (100000, 16), jnp.float32)
        edge_attr_2 = 0.000126197 + 0.999763 * jax.random.normal(jax.random.fold_in(_gk, 12), (100000, 2), jnp.float32)
        edge_type_8 = jax.random.randint(jax.random.fold_in(_gk, 14), (100000,), 0, 8, jnp.int32)
        return (x, src, dst, edge_attr_16, edge_attr_2, edge_type_8)
    x, src, dst, edge_attr_16, edge_attr_2, edge_type_8 = _rec_inputs()

    def _L0_gnn_setup():
        import jax, jax.numpy as jnp
        import numpy as np
        N = 1250
        E = 20000
        CIN = 128
        COUT = 128
        EDGE_DIM = 2
        BN_EPS = 1e-05
        key = jax.random.key(seed)
        ks = jax.random.split(key, 9)
        din = 2 * CIN + EDGE_DIM
        x = jax.random.normal(ks[0], (N, CIN), dtype=jnp.float32)
        edge_index = jax.random.randint(ks[1], (2, E), 0, N, dtype=jnp.int64)
        edge_attr = jax.random.normal(ks[2], (E, EDGE_DIM), dtype=jnp.float32)
        W1 = jax.random.normal(ks[3], (din, COUT), dtype=jnp.float32) / np.sqrt(din)
        b1 = jax.random.normal(ks[4], (COUT,), dtype=jnp.float32) * 0.01
        gamma = jnp.ones((COUT,), dtype=jnp.float32)
        beta = jnp.zeros((COUT,), dtype=jnp.float32)
        W2 = jax.random.normal(ks[5], (COUT, COUT), dtype=jnp.float32) / np.sqrt(COUT)
        b2 = jax.random.normal(ks[6], (COUT,), dtype=jnp.float32) * 0.01
        return {'x': x, 'edge_index': edge_index, 'edge_attr': edge_attr, 'W1': W1, 'b1': b1, 'gamma': gamma, 'beta': beta, 'W2': W2, 'b2': b2}
    _L0_gnn_all = _L0_gnn_setup()
    _L0_gnn_in = {k: v for k, v in _L0_gnn_all.items() if k in ('W1', 'b1', 'gamma', 'beta', 'W2', 'b2')}
    del _L0_gnn_all

    def _L1_gnn_setup():
        import jax, jax.numpy as jnp
        import numpy as np
        N_NODES = 3125
        N_EDGES = 50000
        IN_CH = 128
        OUT_CH = 128
        BN_EPS = 1e-05
        key = jax.random.key(seed)
        k1, k2, k3 = jax.random.split(key, 3)
        x = jax.random.normal(k1, (N_NODES, IN_CH), dtype=jnp.float32)
        edge_index = jax.random.randint(k2, (2, N_EDGES), 0, N_NODES, dtype=jnp.int64)
        W = jax.random.normal(k3, (OUT_CH, IN_CH), dtype=jnp.float32) * (1.0 / np.sqrt(IN_CH))
        b = jnp.zeros((OUT_CH,), dtype=jnp.float32)
        gamma = jnp.ones((OUT_CH,), dtype=jnp.float32)
        beta = jnp.zeros((OUT_CH,), dtype=jnp.float32)
        return {'x': x, 'edge_index': edge_index, 'W': W, 'b': b, 'gamma': gamma, 'beta': beta}
    _L1_gnn_all = _L1_gnn_setup()
    _L1_gnn_in = {k: v for k, v in _L1_gnn_all.items() if k in ('W', 'b', 'gamma', 'beta')}
    del _L1_gnn_all

    def _L2_gnn_setup():
        import jax, jax.numpy as jnp
        import numpy as np
        N = 3125
        E = 18750
        R = 8
        F = 128
        H = 128

        def rgcn_conv(x, src, dst, etype, W, root, bias):
            n, r = (x.shape[0], W.shape[0])
            msg = x[src]
            seg = dst * r + etype
            sums = jax.ops.segment_sum(msg, seg, num_segments=n * r)
            cnt = jax.ops.segment_sum(jnp.ones((src.shape[0],), dtype=x.dtype), seg, num_segments=n * r)
            h = (sums / jnp.maximum(cnt, 1.0)[:, None]).reshape(n, r, -1)
            return jnp.einsum('nrf,rfo->no', h, W) + x @ root + bias
        key = jax.random.key(seed)
        ks = jax.random.split(key, 12)
        s = 0.05
        x = jax.random.normal(ks[0], (N, F), dtype=jnp.float32)
        edge_index = jax.random.randint(ks[1], (2, E), 0, N, dtype=jnp.int64)
        edge_type = jnp.sort(jax.random.randint(ks[2], (E,), 0, R, dtype=jnp.int64))
        return {'x': x, 'edge_index': edge_index, 'edge_type': edge_type, 'W1': jax.random.normal(ks[3], (R, F, H), dtype=jnp.float32) * s, 'root1': jax.random.normal(ks[4], (F, H), dtype=jnp.float32) * s, 'b1': jax.random.normal(ks[5], (H,), dtype=jnp.float32) * s, 'W2': jax.random.normal(ks[6], (R, H, H), dtype=jnp.float32) * s, 'root2': jax.random.normal(ks[7], (H, H), dtype=jnp.float32) * s, 'b2': jax.random.normal(ks[8], (H,), dtype=jnp.float32) * s, 'W3': jax.random.normal(ks[9], (R, H, H), dtype=jnp.float32) * s, 'root3': jax.random.normal(ks[10], (H, H), dtype=jnp.float32) * s, 'b3': jax.random.normal(ks[11], (H,), dtype=jnp.float32) * s}
    _L2_gnn_all = _L2_gnn_setup()
    _L2_gnn_in = {k: v for k, v in _L2_gnn_all.items() if k in ('W1', 'root1', 'b1', 'W2', 'root2', 'b2', 'W3', 'root3', 'b3')}
    del _L2_gnn_all

    def _L3_gnn_setup():
        import jax, jax.numpy as jnp
        import numpy as np
        N = 50000
        IN_DIM = 128
        OUT_DIM = 128
        EA_DIM = 16
        REQ_DIM = 16
        E_TOTAL = 50000

        def _directional_msg(x, src, dst, edge_attr, req, W1, b1, W2, b2, n_nodes):
            x_j = x[src]
            req_e = jnp.broadcast_to(req, (src.shape[0], req.shape[-1]))
            m = jnp.concatenate([x_j, edge_attr, req_e], axis=-1)
            h = jax.nn.relu(m @ W1 + b1) @ W2 + b2
            return jax.ops.segment_sum(h, dst, num_segments=n_nodes)
        key = jax.random.key(seed)
        ks = jax.random.split(key, 16)
        cat_dim = IN_DIM + EA_DIM + REQ_DIM
        s = 0.02
        return {'x': jax.random.normal(ks[0], (N, IN_DIM), dtype=jnp.float32), 'edge_index': jax.random.randint(ks[1], (2, E_TOTAL), 0, N, dtype=jnp.int32), 'edge_attr': jax.random.normal(ks[2], (E_TOTAL, EA_DIM), dtype=jnp.float32), 'req_emb': jax.random.normal(ks[3], (1, REQ_DIM), dtype=jnp.float32), 'W1f': jax.random.normal(ks[4], (cat_dim, OUT_DIM), dtype=jnp.float32) * s, 'b1f': jnp.zeros((OUT_DIM,), dtype=jnp.float32), 'W2f': jax.random.normal(ks[5], (OUT_DIM, OUT_DIM), dtype=jnp.float32) * s, 'b2f': jnp.zeros((OUT_DIM,), dtype=jnp.float32), 'W1b': jax.random.normal(ks[6], (cat_dim, OUT_DIM), dtype=jnp.float32) * s, 'b1b': jnp.zeros((OUT_DIM,), dtype=jnp.float32), 'W2b': jax.random.normal(ks[7], (OUT_DIM, OUT_DIM), dtype=jnp.float32) * s, 'b2b': jnp.zeros((OUT_DIM,), dtype=jnp.float32), 'Wu': jax.random.normal(ks[8], (OUT_DIM, OUT_DIM), dtype=jnp.float32) * s, 'bu': jnp.zeros((OUT_DIM,), dtype=jnp.float32), 'eps': jnp.zeros((1,), dtype=jnp.float32)}
    _L3_gnn_all = _L3_gnn_setup()
    _L3_gnn_in = {k: v for k, v in _L3_gnn_all.items() if k in ('req_emb', 'W1f', 'b1f', 'W2f', 'b2f', 'W1b', 'b1b', 'W2b', 'b2b', 'Wu', 'bu', 'eps')}
    del _L3_gnn_all
    return {'x': x, 'src': src, 'dst': dst, 'edge_attr_16': edge_attr_16, 'edge_attr_2': edge_attr_2, 'edge_type_8': edge_type_8, 'L0_gnn_W1': _L0_gnn_in['W1'], 'L0_gnn_b1': _L0_gnn_in['b1'], 'L0_gnn_gamma': _L0_gnn_in['gamma'], 'L0_gnn_beta': _L0_gnn_in['beta'], 'L0_gnn_W2': _L0_gnn_in['W2'], 'L0_gnn_b2': _L0_gnn_in['b2'], 'L1_gnn_W': _L1_gnn_in['W'], 'L1_gnn_b': _L1_gnn_in['b'], 'L1_gnn_gamma': _L1_gnn_in['gamma'], 'L1_gnn_beta': _L1_gnn_in['beta'], 'L2_gnn_W1': _L2_gnn_in['W1'], 'L2_gnn_root1': _L2_gnn_in['root1'], 'L2_gnn_b1': _L2_gnn_in['b1'], 'L2_gnn_W2': _L2_gnn_in['W2'], 'L2_gnn_root2': _L2_gnn_in['root2'], 'L2_gnn_b2': _L2_gnn_in['b2'], 'L2_gnn_W3': _L2_gnn_in['W3'], 'L2_gnn_root3': _L2_gnn_in['root3'], 'L2_gnn_b3': _L2_gnn_in['b3'], 'L3_gnn_req_emb': _L3_gnn_in['req_emb'], 'L3_gnn_W1f': _L3_gnn_in['W1f'], 'L3_gnn_b1f': _L3_gnn_in['b1f'], 'L3_gnn_W2f': _L3_gnn_in['W2f'], 'L3_gnn_b2f': _L3_gnn_in['b2f'], 'L3_gnn_W1b': _L3_gnn_in['W1b'], 'L3_gnn_b1b': _L3_gnn_in['b1b'], 'L3_gnn_W2b': _L3_gnn_in['W2b'], 'L3_gnn_b2b': _L3_gnn_in['b2b'], 'L3_gnn_Wu': _L3_gnn_in['Wu'], 'L3_gnn_bu': _L3_gnn_in['bu'], 'L3_gnn_eps': _L3_gnn_in['eps']}

def reference(x, src, dst, edge_attr_16, edge_attr_2, edge_type_8, L0_gnn_W1, L0_gnn_b1, L0_gnn_gamma, L0_gnn_beta, L0_gnn_W2, L0_gnn_b2, L1_gnn_W, L1_gnn_b, L1_gnn_gamma, L1_gnn_beta, L2_gnn_W1, L2_gnn_root1, L2_gnn_b1, L2_gnn_W2, L2_gnn_root2, L2_gnn_b2, L2_gnn_W3, L2_gnn_root3, L2_gnn_b3, L3_gnn_req_emb, L3_gnn_W1f, L3_gnn_b1f, L3_gnn_W2f, L3_gnn_b2f, L3_gnn_W1b, L3_gnn_b1b, L3_gnn_W2b, L3_gnn_b2b, L3_gnn_Wu, L3_gnn_bu, L3_gnn_eps):
    import jax
    import jax.numpy as jnp

    def _L0_gnn_ref(x, edge_index, edge_attr, W1, b1, gamma, beta, W2, b2):
        import jax, jax.numpy as jnp
        import numpy as np
        N = 1250
        E = 20000
        CIN = 128
        COUT = 128
        EDGE_DIM = 2
        BN_EPS = 1e-05
        n_nodes = x.shape[0]
        row, col = (edge_index[0], edge_index[1])
        ef = jnp.concatenate([x[row], x[col], edge_attr], axis=-1)
        h = ef @ W1 + b1
        mu = jnp.mean(h, axis=0)
        var = jnp.mean((h - mu) ** 2, axis=0)
        h = (h - mu) * jax.lax.rsqrt(var + BN_EPS) * gamma + beta
        h = jax.nn.relu(h)
        msgs = h @ W2 + b2
        sums = jax.ops.segment_sum(msgs, row, num_segments=n_nodes)
        counts = jax.ops.segment_sum(jnp.ones((msgs.shape[0],), dtype=msgs.dtype), row, num_segments=n_nodes)
        out = sums / (counts + 1.0)[:, None]
        return out + x

    def _L1_gnn_ref(x, edge_index, W, b, gamma, beta):
        import jax, jax.numpy as jnp
        import numpy as np
        N_NODES = 3125
        N_EDGES = 50000
        IN_CH = 128
        OUT_CH = 128
        BN_EPS = 1e-05
        N = x.shape[0]
        loop = jnp.arange(N, dtype=edge_index.dtype)
        src = jnp.concatenate([edge_index[0], loop])
        dst = jnp.concatenate([edge_index[1], loop])
        deg = jax.ops.segment_sum(jnp.ones_like(dst, dtype=x.dtype), dst, num_segments=N)
        dinv = jnp.where(deg > 0, jax.lax.rsqrt(deg), 0.0)
        norm = dinv[src] * dinv[dst]
        h = x @ W.T
        msg = h[src] * norm[:, None]
        agg = jax.ops.segment_sum(msg, dst, num_segments=N) + b
        r = jax.nn.relu(agg)
        mean = jnp.mean(r, axis=0)
        var = jnp.mean((r - mean) ** 2, axis=0)
        out = (r - mean) * jax.lax.rsqrt(var + BN_EPS) * gamma + beta
        return out

    def _L2_gnn_ref(x, edge_index, edge_type, W1, root1, b1, W2, root2, b2, W3, root3, b3):
        import jax, jax.numpy as jnp
        import numpy as np
        N = 3125
        E = 18750
        R = 8
        F = 128
        H = 128

        def rgcn_conv(x, src, dst, etype, W, root, bias):
            n, r = (x.shape[0], W.shape[0])
            msg = x[src]
            seg = dst * r + etype
            sums = jax.ops.segment_sum(msg, seg, num_segments=n * r)
            cnt = jax.ops.segment_sum(jnp.ones((src.shape[0],), dtype=x.dtype), seg, num_segments=n * r)
            h = (sums / jnp.maximum(cnt, 1.0)[:, None]).reshape(n, r, -1)
            return jnp.einsum('nrf,rfo->no', h, W) + x @ root + bias
        src, dst = (edge_index[0], edge_index[1])
        u = jax.nn.relu(rgcn_conv(x, src, dst, edge_type, W1, root1, b1))
        u = jax.nn.relu(rgcn_conv(u, src, dst, edge_type, W2, root2, b2))
        return rgcn_conv(u, src, dst, edge_type, W3, root3, b3)

    def _L3_gnn_ref(x, edge_index, edge_attr, req_emb, W1f, b1f, W2f, b2f, W1b, b1b, W2b, b2b, Wu, bu, eps):
        import jax, jax.numpy as jnp
        import numpy as np
        N = 50000
        IN_DIM = 128
        OUT_DIM = 128
        EA_DIM = 16
        REQ_DIM = 16
        E_TOTAL = 50000

        def _directional_msg(x, src, dst, edge_attr, req, W1, b1, W2, b2, n_nodes):
            x_j = x[src]
            req_e = jnp.broadcast_to(req, (src.shape[0], req.shape[-1]))
            m = jnp.concatenate([x_j, edge_attr, req_e], axis=-1)
            h = jax.nn.relu(m @ W1 + b1) @ W2 + b2
            return jax.ops.segment_sum(h, dst, num_segments=n_nodes)
        n_nodes = x.shape[0]
        E = edge_index.shape[1] // 2
        req = req_emb.reshape(1, -1)
        x_self = x
        src_f, dst_f = (edge_index[0, :E], edge_index[1, :E])
        src_b, dst_b = (edge_index[0, E:], edge_index[1, E:])
        h_in = _directional_msg(x, src_f, dst_f, edge_attr[:E], req, W1f, b1f, W2f, b2f, n_nodes)
        h_out = _directional_msg(x, src_b, dst_b, edge_attr[E:], req, W1b, b1b, W2b, b2b, n_nodes)
        h = (1.0 + eps) * x_self + h_in + h_out
        return jax.nn.relu(h @ Wu + bu)
    edge_index = jnp.stack([src, dst])
    x = _layernorm(x + _L0_gnn_ref(x, edge_index, edge_attr_2, L0_gnn_W1, L0_gnn_b1, L0_gnn_gamma, L0_gnn_beta, L0_gnn_W2, L0_gnn_b2), axis=-1)
    x = _layernorm(x + _L1_gnn_ref(x, edge_index, L1_gnn_W, L1_gnn_b, L1_gnn_gamma, L1_gnn_beta), axis=-1)
    x = _layernorm(x + _L2_gnn_ref(x, edge_index, edge_type_8, L2_gnn_W1, L2_gnn_root1, L2_gnn_b1, L2_gnn_W2, L2_gnn_root2, L2_gnn_b2, L2_gnn_W3, L2_gnn_root3, L2_gnn_b3), axis=-1)
    x = _layernorm(x + _L3_gnn_ref(x, edge_index, edge_attr_16, L3_gnn_req_emb, L3_gnn_W1f, L3_gnn_b1f, L3_gnn_W2f, L3_gnn_b2f, L3_gnn_W1b, L3_gnn_b1b, L3_gnn_W2b, L3_gnn_b2b, L3_gnn_Wu, L3_gnn_bu, L3_gnn_eps), axis=-1)
    return x

_drawn_inputs = setup_inputs


def setup_inputs(seed=0):
    import zlib

    import numpy as np

    out = dict(_drawn_inputs(seed))
    spreads = {'L0_gnn_gamma': (1.0, 0.2),
     'L0_gnn_beta': (0.0, 0.1),
     'L1_gnn_b': (0.0, 0.1),
     'L1_gnn_gamma': (1.0, 0.2),
     'L1_gnn_beta': (0.0, 0.1),
     'L3_gnn_b1f': (0.0, 0.1),
     'L3_gnn_b2f': (0.0, 0.1),
     'L3_gnn_b1b': (0.0, 0.1),
     'L3_gnn_b2b': (0.0, 0.1),
     'L3_gnn_bu': (0.0, 0.1)}
    factors = {'edge_attr_16': 6.54, 'edge_attr_2': 8.0, 'L0_gnn_b1': 8.0, 'L0_gnn_b2': 4.671}
    for name, (base, spread) in spreads.items():
        noise = np.random.default_rng([zlib.crc32(name.encode()), seed]).standard_normal(out[name].shape)
        drawn = base * np.exp(spread * noise) if base else spread * noise
        out[name] = jnp.asarray(drawn.astype(out[name].dtype))
    for name, factor in factors.items():
        out[name] = (out[name] * factor).astype(out[name].dtype)
    return out
```

```python
import concourse.bass as bass
from concourse import mybir
from contextlib import ExitStack

F32, I32, BF16 = mybir.dt.float32, mybir.dt.int32, mybir.dt.bfloat16
ALU, ACT, AX = mybir.AluOpType, mybir.ActivationFunctionType, mybir.AxisListType
ds = bass.ds

N, F, E, R = 3125, 128, 100000, 8
P = 128
NW = -(-N // P)
NWP = NW + NW % 2
LAST = N - (NW - 1) * P
ACC = NW * P
B = 13
BP = 16
BODY = 2 * B
HALF = E // 2
T0 = -(-(E // P + NW) // BODY) * BODY
TH = -(-(HALF // P + NW) // BODY) * BODY
T1 = 2 * TH
PS_, LS = 125, E // 125
PD, LD = 100, E // 100
PH = PD // 2
EAD = 16
REC0, REC1 = 4, 4 + EAD
GAP = P
CHUNK = 125
EPS = 1e-5
NKEY = NW * R
G0, G1 = 7, 6
NEG = -3.0e38


SIGNALS = {
    "vector_steps": "the vector engine's own steps, one after the other",
    "pool_steps": "GpSimd's own steps",
    "x_in": "x has been loaded",
    "ids_in": "the edges' node numbers (and relations)",
    "attrs_in": "edge attributes",
    "weights_in": "a stage's weights and rows",
    "wide_in": "the widened attribute weights of layer 3",
    "zeroed": "memory that a load fills in part is zero",
    "iota_made": "the counting rows and columns",
    "ident_made": "the identity",
    "pad_made": "the records that match no node",
    "pads_out": "they are in DRAM",
    "window_counts": "edges of each window, by partition",
    "prefix_ready": "their sums over earlier partitions, and all",
    "feed_ready": "a turn of the scatter by source is laid out",
    "scatter_go": "(a place for a wait before scatters)",
    "scattered": "records scattered by source",
    "rec_made": "parts of a chunk of records",
    "rec_out": "copies of a chunk in DRAM",
    "moved": "whether an edge stands elsewhere than at its rank, by partition",
    "moved_sum": "the number of such partitions",
    "flag_made": "whether there are any",
    "given_in": "given records to scatter",
    "given_rows": "the rows they go to",
    "given_scattered": "they are scattered",
    "onehots_made": "one-hot rows for the counts",
    "counted": "columns of edges counted",
    "tables_made": "tables of tiles",
    "tables_out": "they are in DRAM",
    "tables_in": "they are back, as rows",
    "attr_summed": "sum of edge_attr_2 over the edges",
    "weight_turned": "layer 1's weight transposed",
    "mean_parts": "a mean's parts by partition",
    "mean_ready": "their sum in all partitions",
    "var_made": "a variance, for scalar's root",
    "std_parts": "layer 0's variance as a row",
    "root_made": "its root",
    "slots_in0": "even batch's records or attributes",
    "slots_in1": "odd batch's",
    "batch_ready": "a batch's row numbers (and local nodes)",
    "gather_go": "(a place for a wait before gathers)",
    "gathered0": "rows of an even batch, layer 0",
    "gathered1": "rows of an odd batch, layer 0",
    "gathered2": "rows of an even batch, layer 1",
    "gathered3": "rows of an odd batch, layer 1",
    "gathered4": "rows of an even batch, layer 2",
    "gathered5": "rows of an odd batch, layer 2",
    "gathered6": "rows of an even batch, layer 3",
    "gathered7": "rows of an odd batch, layer 3",
    "attr_turned": "transposed, in PSUM",
    "attr_back": "and in SBUF",
    "onehot_made": "one-hot matrices of a group or batch",
    "onehot_turned": "transposed, in PSUM",
    "onehot_back": "and in SBUF",
    "h_made": "products of a group's tiles in PSUM",
    "c_made": "the gathered rows added to them",
    "squared": "squares of a batch",
    "squares_added": "added to their sum",
    "c_stored0": "c of an even batch in DRAM",
    "c_stored1": "c of an odd batch",
    "c_in0": "c of an even batch loaded",
    "c_in1": "c of an odd one",
    "scaled": "c times the batch norm's scale",
    "shifted": "plus its shift",
    "messages_made": "messages of a batch or group",
    "summed": "a batch's messages added to the accumulator",
    "inv_picked": "a group's rows of relation weights, in PSUM",
    "inv_back": "and in SBUF",
    "nodes_made": "the nodes' new values",
    "table_stored": "layer 2's table is in DRAM",
    "req_made": "req_emb as a stationary operand",
    "const_ready": "req W1req",
    "const_made": "plus b1",
    "half_out": "an accumulator of half the edges has been copied out",
    "p_copied": "projection: window at its fixed place",
    "p_turned": "transposed, in PSUM",
    "p_back": "and in SBUF",
    "p_made": "product in PSUM",
    "p_taken": "product's parts copied out",
    "p_stored0": "even window's product in DRAM",
    "p_stored1": "odd window's",
    "windows_copied": "output: both sums' window at their fixed places",
    "h_psum": "their products",
    "h_summed": "h of a window",
    "h_turned": "transposed, in PSUM",
    "h_back": "and in SBUF",
    "out_psum": "h Wu",
    "out_taken": "copied out",
    "output_made": "the result",
    "output_stored": "it is in DRAM",
}


class Signal:

    def __init__(self, nc, ctx, name):
        self.sem, self.n = ctx.enter_context(nc.semaphore(name)), 0


def signals(nc, ctx):
    return {name: Signal(nc, ctx, name) for name in SIGNALS}


def passed(S, **added):
    for name, k in added.items():
        S[name].n += k


class Chain:

    def __init__(self, eng, signal):
        self.eng, self.steps, self.sem, self.n = eng, signal, signal.sem, signal.n

    def __call__(self, ins):
        ins.then_inc(self.sem, 1)
        self.n = self.n + 1
        self.eng.wait_ge(self.sem, self.n)

    def end(self):
        self.steps.n = self.n


def peeled(eng, n, body):
    body(0, True)
    with eng.Fori(1, n) as i:
        body(i, False)


def over_f(ap, w):
    return ap.unsqueeze(2).to_broadcast([P, w, F])


def over_w(ap, w):
    return ap.unsqueeze(1).to_broadcast([P, w, F])


class Memory:

    made = 0

    def __init__(self, nc):
        self.nc, self.ctx = nc, ExitStack()

    def unique(self, name):
        Memory.made += 1
        return f"{name}_{Memory.made}"

    def __enter__(self):
        self.ctx.__enter__()
        return self

    def __exit__(self, *a):
        return self.ctx.__exit__(*a)

    def sb(self, name, shape, dt=F32):
        return self.ctx.enter_context(self.nc.sbuf_tensor(self.unique(name), shape, dt))

    def ps(self, name, shape, dt=F32):
        return self.ctx.enter_context(self.nc.psum_tensor(self.unique(name), shape, dt))

    def block(self):
        return self.ctx.enter_context(self.nc.Block())


class Projection:

    def __init__(self, nc, m, S, name, cols, transposed=False, py=None, pt=None, y_cols=None):
        self.nc, self.cols, self.transposed, self.S = nc, cols, transposed, S
        self.xs = m.sb(f"{name}_window", [P, 2, F])
        self.xt = m.sb(f"{name}_windowT", [P, 2, F])
        self.y = m.sb(f"{name}_product", [P, 2, y_cols]) if y_cols else None
        self.pt = pt if transposed or pt is not None else m.ps(f"{name}_psumT", [P, 2, 512])
        self.py = m.ps(f"{name}_psum", [P, 2, -(-cols // 512) * 512]) if py is None else py

    def scalar(self, act, src, outs, l=0):
        nc, S = self.nc, self.S
        per = len(outs)

        def body(i, first):
            for k in range(2):
                n = l * NWP + 2 * i + k
                if not first:
                    used = S["p_made"] if self.transposed else S["p_turned"]
                    act.wait_ge(used.sem, used.n + n - 1)
                dst, signal = (self.xt, S["p_back"]) if self.transposed else (self.xs, S["p_copied"])
                nc.scalar.activation(dst[:, k, :].unsqueeze(1), src(2 * i + k), ACT.Copy).then_inc(signal.sem, 1)
            if not self.transposed:
                for k in range(2):
                    n = l * NWP + 2 * i + k
                    act.wait_ge(S["p_turned"].sem, S["p_turned"].n + n + 1)
                    if not first:
                        act.wait_ge(S["p_made"].sem, S["p_made"].n + n - 1)
                    nc.scalar.activation(self.xt[:, k, :], self.pt[:, k, 0:P], ACT.Copy)\
                        .then_inc(S["p_back"].sem, 1)
            for k in range(2):
                n = l * NWP + 2 * i + k
                act.wait_ge(S["p_made"].sem, S["p_made"].n + n + 1)
                stored = (S["p_stored0"], S["p_stored1"])[k]
                if self.y is not None and not first:
                    act.wait_ge(stored.sem, stored.n + 16 * (l * (NWP // 2) + i))
                for cols, dst, scale in outs:
                    to = self.y[:, k, :].unsqueeze(1) if dst is None else dst(2 * i + k)
                    nc.scalar.activation(to, self.py[:, k, cols].unsqueeze(1),
                                         ACT.Copy if scale is None else ACT.Identity,
                                         scale=1.0 if scale is None else scale(2 * i + k)).then_inc(S["p_taken"].sem, 1)
        peeled(act, NWP // 2, body)

    def tensor(self, pe, ident, weight, per, l=0, extra=None):
        nc, S = self.nc, self.S

        def body(i, first):
            if not self.transposed:
                for k in range(2):
                    n = l * NWP + 2 * i + k
                    pe.wait_ge(S["p_copied"].sem, S["p_copied"].n + n + 1)
                    if not first:
                        pe.wait_ge(S["p_back"].sem, S["p_back"].n + n - 1)
                    nc.tensor.transpose(self.pt[:, k, 0:P], self.xs[:, k, :], ident[:, :])\
                        .then_inc(S["p_turned"].sem, 1)
            for k in range(2):
                n = l * NWP + 2 * i + k
                pe.wait_ge(S["p_back"].sem, S["p_back"].n + n + 1)
                if not first:
                    pe.wait_ge(S["p_taken"].sem, S["p_taken"].n + per * (n - 1))
                for c in range(0, self.cols, 512):
                    e = min(c + 512, self.cols)
                    last = nc.tensor.matmul(self.py[:, k, c:e], self.xt[:, k, :], weight(c, e), start=True,
                                            stop=extra is None)
                    if extra is not None:
                        last = nc.tensor.matmul(self.py[:, k, c:e], extra[0], extra[1], start=False, stop=True)
                last.then_inc(S["p_made"].sem, 1)
        peeled(pe, NWP // 2, body)

    def sync(self, sp, table, per, l=0):
        S = self.S

        def body(i, first):
            for k in range(2):
                sp.wait_ge(S["p_taken"].sem, S["p_taken"].n + per * (l * NWP + 2 * i + k + 1))
                sp.dma_start(table[ds((2 * i + k) * P, P), :], self.y[:, k, :])\
                    .then_inc((S["p_stored0"], S["p_stored1"])[k].sem, 16)
        peeled(sp, NWP // 2, body)
        for s in (S["p_stored0"], S["p_stored1"]):
            sp.wait_ge(s.sem, s.n + 16 * (l + 1) * (NWP // 2))

    def passed(self, per, calls=1):
        added = {"p_back": NWP, "p_made": NWP, "p_taken": per * NWP}
        if not self.transposed:
            added |= {"p_copied": NWP, "p_turned": NWP}
        if self.y is not None:
            added |= {"p_stored0": 8 * NWP, "p_stored1": 8 * NWP}
        passed(self.S, **{k: v * calls for k, v in added.items()})


def win_of(t):
    return lambda w: t[:, ds(w, 1), :]


def count_windows(nc, v, step, win, mask, col, cnt, parts):
    n0 = step.n
    with v.Fori(0, NW) as b:
        step.n = n0 + b
        step(nc.vector.tensor_scalar(mask, win, col[0:parts, ds(b, 1)], 0.0, ALU.is_equal, ALU.add,
                                     accum_out=cnt[:, ds(b, 1)]))
    step.n = n0 + NW


def rank_edges(nc, v, step, win, ones, mask, cum, sel, col, base, pos, parts):
    n0 = step.n
    with v.Fori(0, NW) as b:
        step.n = n0 + b * 4
        step(nc.vector.tensor_scalar(mask, win, col[0:parts, ds(b, 1)], None, ALU.is_equal))
        step(nc.vector.tensor_tensor_scan(cum, ones, mask, base[:, ds(b, 1)], ALU.mult, ALU.add))
        step(nc.vector.scalar_tensor_tensor(sel, win, col[0:parts, ds(b, 1)], cum, ALU.is_equal, ALU.mult))
        step(nc.vector.tensor_tensor(pos, pos, sel, ALU.add))
    step.n = n0 + 4 * NW


def stage_setup(nc, S, top, front, d, K):
    K["rec0_sb"] = front.sb("rec0_sb", [PS_, LS, REC0])
    K["pos0"] = front.sb("pos0", [PS_, LS])
    K["win0"] = front.sb("win0", [PS_, LS])
    K["lo0"] = front.sb("lo0", [PS_, LS])
    K["QN"] = front.sb("QN", [P, NWP, F])
    K["ea2_sum"] = front.sb("ea2_sum", [PS_, 2])
    K["tot0"] = front.sb("tot0", [P, NW])
    K["W1ab"] = front.sb("W1ab", [P, 2 * F])
    K["W1c"] = front.sb("W1c", [2, F])
    K["b1"] = front.sb("b1", [P, F])
    K["W_l1"] = front.sb("W_l1", [P, F])
    with Memory(nc) as m:
        work = m.sb("rank_work", [PS_, 4, LS])
        srcI, dstI, winI = (m.sb(n, [PS_, LS], I32) for n in ("srcI", "dstI", "winI"))
        ea2 = m.sb("ea2", [PS_, LS, 2])
        cnt, base = m.sb("cnt", [PS_, NW]), m.sb("base", [PS_, NW])
        pad = m.sb("pad", [P, 2, REC1])
        pref = m.ps("prefix_psum", [P, 512])
        proj = Projection(nc, m, S, "p0", 2 * F, y_cols=F)
        outs = [(slice(0, F), win_of(K["PN"]), None), (slice(F, 2 * F), win_of(K["QN"]), None),
                (slice(F, 2 * F), None, None)]
        block = m.block()
        ones, mask, cum, sel = (work[:, i, :] for i in range(4))
        loads = [(K["W1ab"][:, 0:F], d["L0_gnn_W1"][0:F, :]), (K["W1ab"][:, F:], d["L0_gnn_W1"][F:2 * F, :]),
                 (K["W1c"][:, :], d["L0_gnn_W1"][2 * F:, :]), (K["W_l1"][:, :], d["L1_gnn_W"])]
        loads += [(K["w1c_wide"][2 * u:2 * u + 2, u, :], d["L0_gnn_W1"][2 * F:, :]) for u in range(B)]
        loads += [(K[n][:, :], d[a].rearrange("(o f) -> o f", o=1).to_broadcast([P, F]))
                  for n, a in [("b1", "L0_gnn_b1"), ("gamma0", "L0_gnn_gamma"), ("beta0", "L0_gnn_beta")]]
        x_in, w_in, ids_in, attrs_in, zeroed = S["x_in"], S["weights_in"], S["ids_in"], S["attrs_in"], S["zeroed"]

        @block.sync
        def _(sp):
            sp.dma_start(srcI[:, :], d["src"].rearrange("(p t) -> p t", p=PS_)).then_inc(ids_in.sem, 16)
            sp.dma_start(dstI[:, :], d["dst"].rearrange("(p t) -> p t", p=PS_)).then_inc(ids_in.sem, 16)
            sp.dma_start(ea2[:, :, :], d["edge_attr_2"].rearrange("(p t) c -> p t c", p=PS_))\
                .then_inc(attrs_in.sem, 16)
            sp.wait_ge(zeroed.sem, 2)
            sp.dma_start(K["X"][:, 0:NW - 1, :],
                         d["x"][0:(NW - 1) * P, :].rearrange("(w p) f -> p w f", p=P)).then_inc(x_in.sem, 16)
            sp.dma_start(K["X"][0:LAST, NW - 1, :], d["x"][(NW - 1) * P:N, :]).then_inc(x_in.sem, 16)
            for dst, src in loads:
                sp.dma_start(dst, src).then_inc(w_in.sem, 16)
            sp.wait_ge(S["pad_made"].sem, 1)
            sp.dma_start(d["rec0"][E:E + GAP, :], pad[:, 0, 0:REC0]).then_inc(S["pads_out"].sem, 16)
            sp.dma_start(d["rec1"][HALF:HALF + GAP, :], pad[:, 1, :]).then_inc(S["pads_out"].sem, 16)
            sp.dma_start(d["rec1"][E + GAP:E + 2 * GAP, :], pad[:, 1, :]).then_inc(S["pads_out"].sem, 16)
            proj.sync(sp, d["Q"], 3)
            sp.wait_ge(S["pads_out"].sem, 48)

        @block.gpsimd
        def _(pool):
            step = Chain(pool, S["pool_steps"])
            nc.gpsimd.memset(K["X"][:, :, :], 0.0).then_inc(zeroed.sem, 1)
            nc.gpsimd.memset(K["w1c_wide"][:, :, :], 0.0).then_inc(zeroed.sem, 1)
            nc.gpsimd.iota(K["col"][:, :], [[1, NKEY]], base=0, channel_multiplier=0,
                           allow_small_or_imprecise_dtypes=True).then_inc(S["iota_made"].sem, 1)
            nc.gpsimd.iota(K["row"][:, :], [[1, 1]], base=0, channel_multiplier=1,
                           allow_small_or_imprecise_dtypes=True).then_inc(S["iota_made"].sem, 1)
            nc.gpsimd.iota(K["tile_no"][:, :], [[1, BODY]], base=0, channel_multiplier=BODY,
                           allow_small_or_imprecise_dtypes=True).then_inc(S["iota_made"].sem, 1)
            step(nc.gpsimd.memset(pad[:, :, :], 0.0))
            step(nc.gpsimd.memset(pad[:, 0, 0:1], -1.0))
            nc.gpsimd.memset(pad[:, 1, 1:2], -1.0).then_inc(S["pad_made"].sem, 1)
            step.end()

        @block.vector
        def _(v):
            step = Chain(v, S["vector_steps"])
            col, row = K["col"], K["row"]
            step(nc.vector.memset(ones, 1.0))
            step(nc.vector.memset(K["ones"][:, :], 1.0))
            step(nc.vector.memset(K["zeros"][:, :], 0.0))
            step(nc.vector.memset(K["pos0"][:, :], 0.0))
            v.wait_ge(S["iota_made"].sem, 3)
            step(nc.vector.tensor_scalar(K["before"][:, :], col[:, 0:P], row[:, 0:1], None, ALU.is_gt))
            nc.vector.tensor_scalar(K["ident"][:, :], col[:, 0:P], row[:, 0:1], None, ALU.is_equal)\
                .then_inc(S["ident_made"].sem, 1)
            step(nc.vector.tensor_copy(K["col_b"][:, :], col[:, :]))
            step(nc.vector.tensor_copy(K["ident_b"][:, :], K["ident"][:, :]))
            step(nc.vector.tensor_scalar(K["half1"][:, :], row[:, 0:1], float(PH), None, ALU.is_ge))
            step(nc.vector.tensor_scalar(K["half0"][:, :], row[:, 0:1], float(PH), None, ALU.is_lt))
            step(nc.vector.tensor_scalar(K["before_half"][:, :], col[:, 0:P], float(PH), None, ALU.is_ge))
            step(nc.vector.tensor_scalar(K["before_half"][:, :], K["before_half"][:, :], K["half1"][:, 0:1], None,
                                         ALU.is_equal))
            step(nc.vector.tensor_tensor(K["before_half"][:, :], K["before_half"][:, :], K["before"][:, :], ALU.mult))
            step(nc.vector.tensor_scalar(K["in_half0"][:, :], K["ones"][:, :], K["half0"][:, 0:1], None, ALU.mult))
            step(nc.vector.tensor_scalar(K["in_half1"][:, :], K["ones"][:, :], K["half1"][:, 0:1], None, ALU.mult))
            step(nc.vector.memset(K["valid"][:, :], 1.0))
            step(nc.vector.tensor_scalar(K["valid"][:, NW - 1:NW], row[:, 0:1], float(LAST), None, ALU.is_lt))
            v.wait_ge(ids_in.sem, 32)
            win, rec = K["win0"][:, :], K["rec0_sb"]
            step(nc.vector.tensor_single_scalar(winI[:, :], srcI[:, :], 7, ALU.arith_shift_right))
            step(nc.vector.tensor_copy(win, winI[:, :]))
            count_windows(nc, v, step, win, mask, col, cnt, PS_)
            nc.vector.tensor_copy(cum[:, 0:1], cnt[:, 0:1]).then_inc(S["window_counts"].sem, 1)
            v.wait_ge(S["prefix_ready"].sem, 1)
            tot = K["tot0"]
            step(nc.vector.tensor_copy(tot[:, :], pref[:, 64:64 + NW]))
            step(nc.vector.tensor_tensor_scan(base[:, :], K["ones"][0:PS_, 0:NW], tot[0:PS_, :], -1.0,
                                              ALU.mult, ALU.add))
            step(nc.vector.tensor_tensor(base[:, :], base[:, :], tot[0:PS_, :], ALU.subtract))
            step(nc.vector.tensor_tensor(base[:, :], base[:, :], pref[0:PS_, 0:NW], ALU.add))
            rank_edges(nc, v, step, win, ones, mask, cum, sel, col, base, K["pos0"][:, :], PS_)
            v.wait_ge(attrs_in.sem, 16)
            step(nc.vector.tensor_copy(rec[:, :, 0], srcI[:, :]))
            step(nc.vector.tensor_copy(rec[:, :, 1], dstI[:, :]))
            step(nc.vector.tensor_copy(rec[:, :, 2:4], ea2[:, :, :]))
            step(nc.vector.scalar_tensor_tensor(K["lo0"][:, :], win, -float(P), rec[:, :, 0], ALU.mult, ALU.add))
            step(nc.vector.tensor_reduce(K["ea2_sum"][:, :], ea2[:, :, :].rearrange("p t c -> p c t"), AX.X, ALU.add))
            step.end()

        @block.tensor
        def _(pe):
            pe.wait_ge(w_in.sem, 16 * len(loads))
            pe.wait_ge(S["ident_made"].sem, 1)
            proj.tensor(pe, K["ident"], lambda c, e: K["W1ab"][:, c:e], 3)
            pe.wait_ge(S["window_counts"].sem, 1)
            nc.tensor.matmul(pref[0:PS_, 0:NW], K["before"][0:PS_, 0:PS_], cnt[:, :], start=True, stop=True)
            nc.tensor.matmul(pref[:, 64:64 + NW], K["ones"][0:PS_, :], cnt[:, :], start=True, stop=True)\
                .then_inc(S["prefix_ready"].sem, 1)

        @block.scalar
        def _(act):
            act.wait_ge(x_in.sem, 32)
            proj.scalar(act, win_of(K["X"]), outs)
    proj.passed(3)
    passed(S, ids_in=32, window_counts=1, prefix_ready=1, attrs_in=16, weights_in=16 * len(loads), iota_made=3, zeroed=2)


def tile_table(nc, step, K, tmp, tot, tiles, first_row, limit, tab):
    rows = tiles // BODY
    v = nc.vector
    ti, f, big, red = tmp
    tf, ct, cn, dd, diff = (f[:, i, :] for i in range(5))
    ones = K["ones"][:, 0:NW]
    step(v.tensor_scalar(ti[:, :], tot, float(P - 1), None, ALU.add))
    step(v.tensor_single_scalar(ti[:, :], ti[:, :], 7, ALU.arith_shift_right))
    step(v.tensor_copy(tf, ti[:, :]))
    step(v.tensor_tensor_scan(ct, ones, tf, 0.0, ALU.mult, ALU.add))
    step(v.tensor_tensor_scan(cn, ones, tot, float(first_row), ALU.mult, ALU.add))
    step(v.tensor_tensor(cn, cn, tot, ALU.subtract))
    step(v.tensor_tensor(dd, ct, tf, ALU.subtract))
    step(v.scalar_tensor_tensor(dd, dd, -float(P), cn, ALU.mult, ALU.add))
    step(v.tensor_tensor(diff[:, 0:NW - 1], dd[:, 1:NW], dd[:, 0:NW - 1], ALU.subtract))
    no = K["tile_no"][:, :]
    shape = [P, BODY, NW - 1]
    step(v.tensor_tensor(big[:, :, :], ct[:, 0:NW - 1].unsqueeze(1).to_broadcast(shape),
                         no.unsqueeze(2).to_broadcast(shape), ALU.is_le))
    step(v.tensor_reduce(red[:, 0, :], big[:, :, :], AX.X, ALU.add))
    step(v.tensor_tensor(big[:, :, :], big[:, :, :], diff[:, 0:NW - 1].unsqueeze(1).to_broadcast(shape), ALU.mult))
    step(v.tensor_reduce(red[:, 1, :], big[:, :, :], AX.X, ALU.add))
    step(v.scalar_tensor_tensor(red[:, 2, :], no, float(P), red[:, 1, :], ALU.mult, ALU.add))
    step(v.tensor_scalar(tab[0:rows, 0, :], red[0:rows, 2, :], dd[0:rows, 0:1], float(limit), ALU.add, ALU.min))
    step(v.tensor_scalar(tab[0:rows, 1, :], red[0:rows, 0, :], float(P), None, ALU.mult))
    step(v.tensor_scalar(tab[0:rows, 2, :], red[0:rows, 0, :], float(R), None, ALU.mult))


def stage_sort(nc, S, top, front, d, K):
    COLS = 10
    with Memory(nc) as m:
        idx_ring = m.sb("scatter_rows", [P, COLS], I32)
        rec_ring = m.sb("scatter_recs", [P, COLS * REC1])
        srcI, dstI, typI, posI = (m.sb(n, [PD, LD], I32) for n in ("by_dst_src", "by_dst_dst", "by_dst_type", "pos1_i"))
        work = m.sb("by_dst_work", [PD, 5, LD])
        pos, lo, key, place = (m.sb(n, [PD, LD]) for n in ("pos1", "lo1", "key1", "place1"))
        attr = m.sb("attr_chunk", [PD, CHUNK, EAD])
        rec = m.sb("rec_chunk", [PD, CHUNK, REC1])
        cnt, base = m.sb("cnt1", [PD, NW]), m.sb("base1", [PD, NW])
        tot = m.sb("tot1", [P, 2, NW])
        ohl = m.sb("onehot_local", [P, COLS, P], BF16)
        ohk = m.sb("onehot_key", [P, COLS, NKEY], BF16)
        tab = m.sb("tile_rows", [P, 3, 3, BODY])
        tabI = m.sb("tile_rows_i", [P, 3, 3, BODY], I32)
        tmp = (m.sb("tile_i", [P, NW], I32), m.sb("tile_f", [P, 5, NW]), m.sb("tile_m", [P, BODY, NW - 1]),
               m.sb("tile_r", [P, 3, BODY]))
        big = m.sb("mean_work", [P, NW, F])
        red = m.sb("mean_sum", [P, 2, F])
        ea_b = m.sb("attr_sum", [2, P])
        rel_f = m.sb("counts_half0", [P, NKEY])
        flag, flagI = m.sb("flag", [PD, 2]), m.sb("flag_i", [1, 1], I32)
        zeroW = m.sb("zero_bf", [P, 512], BF16)
        pref = m.ps("prefix1_psum", [P, 512])
        cps = m.ps("count_psum", [P, 2, 512])
        mps = m.ps("mean_psum", [P, 512])
        fps = m.ps("small_psum", [P, 512])
        block = m.block()
        ones, mask, cum, sel, win = (work[:, i, :] for i in range(5))

        @block.sync
        def _(sp):
            for t, name in ((dstI, "dst"), (typI, "edge_type_8"), (srcI, "src")):
                sp.dma_start(t[:, :], d[name].rearrange("(p t) -> p t", p=PD)).then_inc(S["ids_in"].sem, 16)
            attrs = d["edge_attr_16"].rearrange("(p t) c -> p t c", p=PD)
            given = d["rec1_given"].rearrange("(p t) c -> p t c", p=PD)
            halves = [d["rec1"][h * (HALF + GAP):h * (HALF + GAP) + HALF, :].rearrange("(p t) c -> p t c", p=PH)
                      for h in range(2)]

            def body(i, first):
                if not first:
                    sp.wait_ge(S["rec_out"].sem, 48 * i)
                at = ds(i * CHUNK, CHUNK)
                sp.dma_start(attr[:, :, :], attrs[:, at, :]).then_inc(S["attrs_in"].sem, 16)
                sp.wait_ge(S["rec_made"].sem, 5 * i + 5)
                sp.dma_start(given[:, at, :], rec[:, :, :]).then_inc(S["rec_out"].sem, 16)
                for h in range(2):
                    sp.dma_start(halves[h][:, at, :], rec[h * PH:(h + 1) * PH, :, :]).then_inc(S["rec_out"].sem, 16)
            peeled(sp, LD // CHUNK, body)
            sp.wait_ge(S["rec_out"].sem, 48 * (LD // CHUNK))
            sp.wait_ge(S["tables_made"].sem, 1)
            n = 0
            for g, (name, at, rows) in enumerate((("tab0", 0, T0 // BODY), ("tab1", 0, TH // BODY),
                                                  ("tab1", TH, TH // BODY))):
                for j in range(3):
                    sp.dma_start(d[name][j, at:at + rows * BODY].rearrange("(p t) -> p t", t=BODY),
                                 tabI[0:rows, g, j, :]).then_inc(S["tables_out"].sem, 16)
                sp.dma_start(d[name + "w"][0, at:at + rows * BODY].rearrange("(p t) -> p t", t=BODY),
                             tab[0:rows, g, 1, :]).then_inc(S["tables_out"].sem, 16)
                n += 4
            sp.wait_ge(S["tables_out"].sem, 16 * n)
            for g, T in ((0, T0), (1, T1)):
                sp.dma_start(K[f"tab{g}"][:, :].rearrange("r (b t) -> r b t", t=BP)[:, :, 0:B],
                             d[f"tab{g}"].rearrange("r (b t) -> r b t", t=B)).then_inc(S["tables_in"].sem, 16)
                sp.dma_start(K[f"loc{g}"][:, :], d[f"tab{g}w"].to_broadcast([P, T])).then_inc(S["tables_in"].sem, 16)
            sp.wait_ge(S["tables_in"].sem, 64)

        @block.gpsimd
        def _(pool):
            nc.gpsimd.iota(place[:, :], [[1, LD]], base=0, channel_multiplier=LD,
                           allow_small_or_imprecise_dtypes=True).then_inc(S["iota_made"].sem, 1)

            def body(i, first):
                if not first:
                    pool.wait_ge(S["scattered"].sem, 16 * COLS * i)
                nc.gpsimd.tensor_copy(idx_ring[0:PS_, :], K["pos0"][:, ds(i * COLS, COLS)]).then_inc(S["feed_ready"].sem, 1)
                nc.gpsimd.tensor_copy(rec_ring[0:PS_, 0:COLS * REC0].rearrange("p (t c) -> p t c", c=REC0),
                                      K["rec0_sb"][:, ds(i * COLS, COLS), :]).then_inc(S["feed_ready"].sem, 1)
                pool.wait_ge(S["feed_ready"].sem, 2 * i + 2)
                pool.sem_inc(S["scatter_go"].sem, 1)
                for k in range(COLS):
                    nc.gpsimd.indirect_dma_start(
                        d["rec0"][:, :], bass.IndirectOffsetOnAxis(ap=idx_ring[0:PS_, k:k + 1], axis=0),
                        rec_ring[0:PS_, k * REC0:(k + 1) * REC0], None).then_inc(S["scattered"].sem, 16)
            peeled(pool, LS // COLS, body)
            pool.wait_ge(S["scattered"].sem, 16 * LS)
            pool.wait_ge(S["flag_made"].sem, 1)
            pool.wait_ge(S["rec_out"].sem, 48 * (LD // CHUNK))
            unsorted = pool.value_load(flagI[0:1, 0:1], min_val=0, max_val=1)
            given = d["rec1_given"].rearrange("(p t) c -> p t c", p=PD)
            with pool.If(unsorted):
                def body(i, first):
                    nc.gpsimd.dma_start(rec_ring[0:PD, 0:COLS * REC1].rearrange("p (t c) -> p t c", c=REC1),
                                        given[:, ds(i * COLS, COLS), :]).then_inc(S["given_in"].sem, 16)
                    nc.gpsimd.tensor_copy(idx_ring[0:PD, :], posI[:, ds(i * COLS, COLS)]).then_inc(S["given_rows"].sem, 1)
                    pool.wait_ge(S["given_in"].sem, 16 * i + 16)
                    pool.wait_ge(S["given_rows"].sem, i + 1)
                    pool.sem_inc(S["scatter_go"].sem, 1)
                    for k in range(COLS):
                        nc.gpsimd.indirect_dma_start(
                            d["rec1"][:, :], bass.IndirectOffsetOnAxis(ap=idx_ring[0:PD, k:k + 1], axis=0),
                            rec_ring[0:PD, k * REC1:(k + 1) * REC1], None).then_inc(S["given_scattered"].sem, 16)
                    pool.wait_ge(S["given_scattered"].sem, 16 * COLS * i + 16 * COLS)
                peeled(pool, LD // COLS, body)

        @block.scalar
        def _(act):
            act.wait_ge(S["ids_in"].sem, S["ids_in"].n + 48)

            def body(i, first):
                if not first:
                    act.wait_ge(S["rec_out"].sem, 48 * i)
                at = ds(i * CHUNK, CHUNK)
                for c, ids in enumerate((srcI, dstI, typI, typI)):
                    nc.scalar.activation(rec[:, :, c], ids[:, at], ACT.Copy).then_inc(S["rec_made"].sem, 1)
                act.wait_ge(S["attrs_in"].sem, S["attrs_in"].n + 16 * i + 16)
                nc.scalar.activation(rec[:, :, REC0:REC1], attr[:, :, :], ACT.Copy).then_inc(S["rec_made"].sem, 1)
            peeled(act, LD // CHUNK, body)

        @block.vector
        def _(v):
            step = Chain(v, S["vector_steps"])
            col = K["col"]
            v.wait_ge(S["ids_in"].sem, S["ids_in"].n + 48)
            step(nc.vector.memset(zeroW[:, :], 0.0))
            step(nc.vector.memset(ones, 1.0))
            step(nc.vector.tensor_single_scalar(posI[:, :], dstI[:, :], 7, ALU.arith_shift_right))
            step(nc.vector.tensor_copy(win, posI[:, :]))
            step(nc.vector.tensor_copy(lo[:, :], dstI[:, :]))
            step(nc.vector.scalar_tensor_tensor(lo[:, :], win, -float(P), lo[:, :], ALU.mult, ALU.add))
            step(nc.vector.tensor_copy(key[:, :], typI[:, :]))
            step(nc.vector.scalar_tensor_tensor(key[:, :], win, float(R), key[:, :], ALU.mult, ALU.add))
            count_windows(nc, v, step, win, mask, col, cnt, PD)
            nc.vector.tensor_copy(cum[:, 0:1], cnt[:, 0:1]).then_inc(S["window_counts"].sem, 1)
            v.wait_ge(S["prefix_ready"].sem, S["prefix_ready"].n + 1)
            step(nc.vector.tensor_copy(tot[:, 0, :], pref[:, 64:64 + NW]))
            step(nc.vector.tensor_copy(tot[:, 1, :], pref[:, 128:128 + NW]))
            step(nc.vector.tensor_scalar(base[:, :], pref[0:PD, 0:NW], -1.0, None, ALU.add))
            for h, first_row in ((0, 0), (1, HALF + GAP)):
                start = cum[:, 0:NW]
                step(nc.vector.tensor_tensor_scan(start, K["ones"][0:PD, 0:NW], tot[0:PD, h, :], float(first_row),
                                                  ALU.mult, ALU.add))
                step(nc.vector.tensor_tensor(start, start, tot[0:PD, h, :], ALU.subtract))
                step(nc.vector.scalar_tensor_tensor(base[:, :], start, K[f"half{h}"][0:PD, 0:1], base[:, :],
                                                    ALU.mult, ALU.add))
            step(nc.vector.memset(pos[:, :], 0.0))
            rank_edges(nc, v, step, win, ones, mask, cum, sel, col, base, pos[:, :], PD)
            step(nc.vector.tensor_copy(posI[:, :], pos[:, :]))
            v.wait_ge(S["iota_made"].sem, S["iota_made"].n + 1)
            step(nc.vector.tensor_scalar(sel, ones, K["half1"][0:PD, 0:1], float(GAP), ALU.mult, ALU.mult))
            step(nc.vector.tensor_tensor(sel, sel, place[:, :], ALU.add))
            step(nc.vector.tensor_tensor(sel, sel, pos[:, :], ALU.subtract))
            step(nc.vector.tensor_tensor(sel, sel, sel, ALU.mult))
            step(nc.vector.tensor_reduce(flag[:, 0:1], sel, AX.X, ALU.max))
            nc.vector.tensor_scalar(flag[:, 1:2], flag[:, 0:1], 0.5, None, ALU.is_gt).then_inc(S["moved"].sem, 1)
            v.wait_ge(S["moved_sum"].sem, 1)
            step(nc.vector.tensor_scalar(flag[0:1, 0:1], fps[0:1, 0:1], 1.0, None, ALU.min))
            nc.vector.tensor_copy(flagI[:, :], flag[0:1, 0:1]).then_inc(S["flag_made"].sem, 1)

            def dst_body(i, first):
                for k in range(COLS):
                    t = i * COLS + k
                    if not first:
                        v.wait_ge(S["counted"].sem, t - COLS + 1)
                    tt = ds(t, 1)
                    nc.vector.tensor_scalar(ohl[0:PD, k, :], K["col_b"][0:PD, 0:P], lo[:, tt], None, ALU.is_equal)
                    nc.vector.tensor_scalar(ohk[0:PD, k, :], K["col_b"][0:PD, :], key[:, tt], None, ALU.is_equal)\
                        .then_inc(S["onehots_made"].sem, 1)
            peeled(v, LD // COLS, dst_body)

            def src_body(i, first):
                for k in range(COLS):
                    t = i * COLS + k
                    v.wait_ge(S["counted"].sem, LD + t - COLS + 1)
                    tt = ds(t, 1)
                    nc.vector.tensor_scalar(ohl[0:PS_, k, :], K["col_b"][0:PS_, 0:P], K["lo0"][:, tt], None, ALU.is_equal)
                    nc.vector.tensor_scalar(ohk[0:PS_, k, 0:NW], K["col_b"][0:PS_, 0:NW], K["win0"][:, tt], None,
                                            ALU.is_equal).then_inc(S["onehots_made"].sem, 1)
            peeled(v, LS // COLS, src_body)

            step(nc.vector.memset(tab[:, :, :, :], 0.0))
            tile_table(nc, step, K, tmp, K["tot0"][:, :], T0, 0, E, tab[:, 0, :, :])
            for h in range(2):
                first_row = h * (HALF + GAP)
                tile_table(nc, step, K, tmp, tot[:, h, :], TH, first_row, first_row + HALF, tab[:, 1 + h, :, :])
            nc.vector.tensor_copy(tabI[:, :, :, :], tab[:, :, :, :]).then_inc(S["tables_made"].sem, 1)

            v.wait_ge(S["counted"].sem, LD + LS)
            inv = K["inv_count"]
            step(nc.vector.tensor_copy(inv[:, :], cps[:, 0, 0:NKEY]))
            step(nc.vector.tensor_reduce(K["deg"][:, :], inv[:, :].rearrange("p (w r) -> p w r", r=R), AX.X, ALU.add))
            step(nc.vector.tensor_scalar(inv[:, :], inv[:, :], 1.0, None, ALU.max))
            step(nc.vector.reciprocal(inv[:, :], inv[:, :]))
            step(nc.vector.tensor_copy(rel_f[:, :], cps[:, 0, 256:256 + NKEY]))
            step(nc.vector.tensor_reduce(K["deg_f"][:, :], rel_f[:, :].rearrange("p (w r) -> p w r", r=R), AX.X, ALU.add))
            step(nc.vector.tensor_copy(K["out_deg"][:, :], cps[:, 1, 0:NW]))
            for i, (t, n) in enumerate((("PN", "out_deg"), ("QN", "deg"))):
                step(nc.vector.tensor_tensor(big[:, :, :], K[t][:, 0:NW, :], over_f(K[n][:, :], NW), ALU.mult))
                step(nc.vector.tensor_reduce(red[:, i, :], big[:, :, :].rearrange("p w f -> p f w"), AX.X, ALU.add))
            v.wait_ge(S["attr_summed"].sem, 1)
            step(nc.vector.tensor_copy(ea_b[:, :], fps[0:2, P:2 * P]))
            nc.vector.tensor_tensor(red[:, 0, :], red[:, 0, :], red[:, 1, :], ALU.add).then_inc(S["mean_parts"].sem, 1)
            v.wait_ge(S["mean_ready"].sem, 1)
            mean = red[:, 1, :]
            step(nc.vector.scalar_tensor_tensor(mean, mps[:, 0:F], 1.0 / E, K["b1"][:, :], ALU.mult, ALU.add))
            step(nc.vector.tensor_tensor(mean, K["b1"][:, :], mean, ALU.subtract))
            step(nc.vector.tensor_tensor(K["PN"][:, 0:NW, :], K["PN"][:, 0:NW, :], over_w(mean, NW), ALU.add))
            v.wait_ge(S["weight_turned"].sem, 1)
            step(nc.vector.tensor_copy(K["W_l1T"][:, :], fps[:, 2 * P:3 * P]))
            step.end()

        @block.tensor
        def _(pe):
            pe.wait_ge(S["window_counts"].sem, S["window_counts"].n + 1)
            nc.tensor.matmul(pref[0:PD, 0:NW], K["before_half"][0:PD, 0:PD], cnt[:, :], start=True, stop=True)
            nc.tensor.matmul(pref[:, 64:64 + NW], K["in_half0"][0:PD, :], cnt[:, :], start=True, stop=True)
            nc.tensor.matmul(pref[:, 128:128 + NW], K["in_half1"][0:PD, :], cnt[:, :], start=True, stop=True)                .then_inc(S["prefix_ready"].sem, 1)
            nc.tensor.transpose(fps[:, 2 * P:3 * P], K["W_l1"][:, :], K["ident"][:, :]).then_inc(S["weight_turned"].sem, 1)
            nc.tensor.matmul(fps[0:2, P:2 * P], K["ea2_sum"][:, :], K["ones"][0:PS_, :], start=True, stop=True)                .then_inc(S["attr_summed"].sem, 1)
            pe.wait_ge(S["moved"].sem, 1)
            nc.tensor.matmul(fps[0:1, 0:1], flag[:, 1:2], K["ones"][0:PD, 0:1], start=True, stop=True)                .then_inc(S["moved_sum"].sem, 1)
            for j in range(2):
                nc.tensor.matmul(cps[:, j, :], zeroW[:, 0:P], zeroW[:, :], start=True, stop=True)

            def dst_body(i, first):
                for k in range(COLS):
                    pe.wait_ge(S["onehots_made"].sem, i * COLS + k + 1)
                    nc.tensor.matmul(cps[:, 0, 0:NKEY], ohl[0:PD, k, :], ohk[0:PD, k, :], start=False, stop=True,
                                     skip_group_check=True)
                    nc.tensor.matmul(cps[:, 0, 256:256 + NKEY], ohl[0:PH, k, :], ohk[0:PH, k, :], start=False, stop=True,
                                     skip_group_check=True).then_inc(S["counted"].sem, 1)
            peeled(pe, LD // COLS, dst_body)

            def src_body(i, first):
                for k in range(COLS):
                    pe.wait_ge(S["onehots_made"].sem, LD + i * COLS + k + 1)
                    nc.tensor.matmul(cps[:, 1, 0:NW], ohl[0:PS_, k, :], ohk[0:PS_, k, 0:NW], start=False, stop=True,
                                     skip_group_check=True).then_inc(S["counted"].sem, 1)
            peeled(pe, LS // COLS, src_body)
            pe.wait_ge(S["mean_parts"].sem, 1)
            nc.tensor.matmul(mps[:, 0:F], K["ones"][:, :], red[:, 0, :], start=True, stop=False)
            nc.tensor.matmul(mps[:, 0:F], ea_b[:, :], K["W1c"][:, :], start=False, stop=True)                .then_inc(S["mean_ready"].sem, 1)
    passed(S, ids_in=48, window_counts=1, prefix_ready=1, attrs_in=16 * (LD // CHUNK), iota_made=1, mean_parts=1,
             mean_ready=1)


GROUPS = [(0, 4), (4, 7), (7, 10), (10, 13)]
NG = len(GROUPS)
PARTS = ((0, G0), (G0, B))
GATHERED = 16 * B
BANK7 = 7 * 512


def need(eng, signal, count, base=0):
    if isinstance(count, int) and count <= 0 and not (isinstance(base, int) and base + count > 0):
        return
    eng.wait_ge(signal.sem, signal.n + base + count)


def batches(eng, n_bodies, batch):
    def body(i, first):
        for h in range(2):
            batch(2 * i + h, h, i)
    peeled(eng, n_bodies, body)


def offsets(eng, tab, row, b, top):
    Memory.made += 1
    regs = [eng.alloc_register(name=f"tile_{Memory.made}_{u}") for u in range(B)]
    eng.load(regs, tab[row:row + 1, ds(b * BP, B)])
    return [eng.snap(r, donate=True, min_val=0, max_val=top) for r in regs]


def clear_acc(nc, K, psum):
    for c in range(0, ACC, 512):
        last = nc.tensor.matmul(psum[:, c:c + 512], K["zeros"][:, 0:P], K["zeros"][:, :], start=True, stop=True)
    return last


def layer_norm(nc, v, step, S, V, big, st, n):
    mean, var = st[:, 0, :], st[:, 1, :]
    step(nc.vector.tensor_reduce(mean, V, AX.X, ALU.add))
    step(nc.vector.tensor_scalar(mean, mean, 1.0 / F, None, ALU.mult))
    step(nc.vector.tensor_tensor(V, V, over_f(mean, NW), ALU.subtract))
    step(nc.vector.tensor_tensor(big, V, V, ALU.mult))
    step(nc.vector.tensor_reduce(var, big, AX.X, ALU.add))
    nc.vector.tensor_scalar(var, var, 1.0 / F, EPS, ALU.mult, ALU.add).then_inc(S["var_made"].sem, 1)
    v.wait_ge(S["root_made"].sem, S["root_made"].n + n + 1)
    step(nc.vector.reciprocal(var, var))
    step(nc.vector.tensor_tensor(V, V, over_f(var, NW), ALU.mult))


def root(nc, act, S, x, n):
    act.wait_ge(S["var_made"].sem, S["var_made"].n + n + 1)
    nc.scalar.activation(x, x, ACT.Sqrt).then_inc(S["root_made"].sem, 1)


def stage_edge_mlp(nc, S, top, d, K):
    with Memory(nc) as m:
        slots = m.sb("slots", [P, 2, B, REC0])
        idx = m.sb("rows", [P, 2, B], I32)
        valid, row = m.sb("in_window", [P, B]), m.sb("row", [P, B])
        oh = m.sb("onehot", [P, 2, B, P], BF16)
        ohT = m.sb("onehotT", [P, 2, 512])
        ea, eaT = m.sb("attr", [P, 2, 2 * B]), m.sb("attrT", [2 * B, 2, P])
        q = m.sb("Q_rows", [P, 2, B, F])
        c = m.sb("c", [P, 2, B * F])
        sq = m.sb("c_squared", [P, 2, B * F])
        total = m.sb("squares_sum", [P, B * F])
        ps_t, ps_h = m.ps("psum_onehotT", [P, 2, 1024], BF16), m.ps("psum_h", [P, 2, 512])
        ps_e, ps_s = m.ps("psum_attrT", [P, 512]), m.ps("psum_squares", [P, 512])
        block = m.block()
        slots_in, gathered, stored = (S["slots_in0"], S["slots_in1"]), (S["gathered0"], S["gathered1"]), (S["c_stored0"], S["c_stored1"])
        bodies = T0 // BODY
        loc, tab = K["loc0"], K["tab0"]

        @block.sync
        def _(sp):
            def batch(b, h, i):
                off = offsets(sp, tab, 0, b, E)
                need(sp, S["batch_ready"], b - 1)
                for u in range(B):
                    sp.dma_start(slots[:, h, u, :], d["rec0"][ds(off[u], P), :]).then_inc(slots_in[h].sem, 16)
            batches(sp, bodies, batch)

        @block.gpsimd
        def _(pool):
            def batch(b, h, i):
                need(pool, S["c_made"], NG * (b - 1))
                need(pool, S["batch_ready"], b + 1)
                pool.sem_inc(S["gather_go"].sem, 1)
                for u in range(B):
                    nc.gpsimd.indirect_dma_start(q[:, h, u, :], None, d["Q"][:, :],
                                                 bass.IndirectOffsetOnAxis(ap=idx[:, h, u:u + 1], axis=0))\
                        .then_inc(gathered[h].sem, 16)
            batches(pool, bodies, batch)

        @block.vector
        def _(v):
            step = Chain(v, S["vector_steps"])
            n0 = step.n

            def add(b, h, i):
                need(v, gathered[h], GATHERED * (i + 1))
                need(v, stored[h], 16 * i)
                for g, (s, e) in enumerate(GROUPS):
                    need(v, S["h_made"], NG * b + g + 1)
                    nc.vector.tensor_tensor(c[:, h, s * F:e * F], ps_h[:, g % 2, 0:(e - s) * F],
                                            q[:, h, s:e, :].rearrange("p t f -> p (t f)"), ALU.add)\
                        .then_inc(S["c_made"].sem, 1)

            def add_squares(b, h):
                need(v, S["squared"], b + 1)
                need(v, S["squares_added"], b)
                nc.vector.tensor_tensor(total[:, :], total[:, :], sq[:, h, :], ALU.add)\
                    .then_inc(S["squares_added"].sem, 1)

            def batch(b, h, i):
                step.n = n0 + b * 4
                at = ds(b * B, B)
                need(v, slots_in[h], GATHERED * (i + 1))
                need(v, gathered[h], GATHERED * i)
                need(v, S["attr_turned"], b - 1)
                step(nc.vector.tensor_tensor(loc[:, at], slots[:, h, :, 0], loc[:, at], ALU.subtract))
                step(nc.vector.tensor_scalar(valid[:, :], loc[:, at], 0.0, None, ALU.is_ge))
                step(nc.vector.scalar_tensor_tensor(valid[:, :], loc[:, at], float(P), valid[:, :], ALU.is_lt, ALU.mult))
                step(nc.vector.scalar_tensor_tensor(row[:, :], slots[:, h, :, 1], 1.0 - NWP * P, valid[:, :],
                                                    ALU.add, ALU.mult))
                nc.vector.tensor_scalar(idx[:, h, :], row[:, :], NWP * P - 1.0, None, ALU.add)
                nc.vector.tensor_tensor(ea[:, h, :].rearrange("p (t c) -> p t c", c=2), slots[:, h, :, 2:4],
                                        valid[:, :].unsqueeze(2).to_broadcast([P, B, 2]), ALU.mult)\
                    .then_inc(S["batch_ready"].sem, 1)
                for g, (s, e) in enumerate(GROUPS):
                    need(v, S["onehot_turned"], NG * (b - 2) + g + 1)
                    for u in range(s, e):
                        last = nc.vector.tensor_scalar(oh[:, h, u, :], K["col"][:, 0:P], loc[:, ds(b * B + u, 1)], None,
                                                       ALU.is_equal)
                    last.then_inc(S["onehot_made"].sem, 1)
                if h:
                    add(b - 1, 0, i)
                elif not isinstance(i, int):
                    add(b - 1, 1, i - 1)
                if not isinstance(i, int):
                    add_squares(b - 2, h)
            step(nc.vector.memset(total[:, :], 0.0))
            n0 = step.n
            batches(v, bodies, batch)
            last = 2 * bodies - 1
            add(last, 1, bodies - 1)
            add_squares(last - 1, 0)
            add_squares(last, 1)
            step.n = n0 + 4 * 2 * bodies
            v.wait_ge(S["squares_added"].sem, 2 * bodies)
            step(nc.vector.tensor_reduce(sq[:, 0, 0:F], total[:, :].rearrange("p (t f) -> p f t", f=F), AX.X, ALU.add))
            v.sem_inc(S["mean_parts"].sem, 1)
            v.wait_ge(S["mean_ready"].sem, S["mean_ready"].n + 1)
            var, scale = K["stat"][:, 0, :], K["scale"]
            step(nc.vector.tensor_scalar(K["one"][:, :], ps_s[:, 0:1], 1.0 / E, EPS, ALU.mult, ALU.add))
            nc.vector.tensor_scalar(var, K["ident"][:, :], K["one"][:, 0:1], None, ALU.mult)\
                .then_inc(S["var_made"].sem, 1)
            v.wait_ge(S["root_made"].sem, 1)
            step(nc.vector.reciprocal(scale[:, :], var))
            step(nc.vector.tensor_tensor(scale[:, :], scale[:, :], K["gamma0"][:, :], ALU.mult))
            step.end()

        @block.scalar
        def _(act):
            def batch(b, h, i):
                need(act, S["attr_turned"], b + 1)
                need(act, S["h_made"], NG * (b - 1))
                nc.scalar.activation(eaT[:, h, :], ps_e[0:2 * B, 0:P], ACT.Copy).then_inc(S["attr_back"].sem, 1)
                for g, (s, e) in enumerate(GROUPS):
                    need(act, S["onehot_turned"], NG * b + g + 1)
                    need(act, S["h_made"], NG * b + g - 1)
                    nc.scalar.activation(ohT[:, g % 2, 0:(e - s) * P], ps_t[:, g % 2, 0:(e - s) * P], ACT.Copy)\
                        .then_inc(S["onehot_back"].sem, 1)
                need(act, S["c_made"], NG * (b + 1))
                need(act, S["squares_added"], b - 1)
                nc.scalar.activation(sq[:, h, :], c[:, h, :], ACT.Square).then_inc(S["squared"].sem, 1)
                act.dma_start(d["c"][ds(b, 1), :, :].rearrange("o p f -> (o p) f"), c[:, h, :])\
                    .then_inc(stored[h].sem, 16)
            batches(act, bodies, batch)
            for s in stored:
                act.wait_ge(s.sem, 16 * bodies)
            act.wait_ge(S["var_made"].sem, 1)
            act.wait_ge(S["std_parts"].sem, 1)
            nc.scalar.activation(K["stat"][:, 0, :], ps_e[:, 0:P], ACT.Sqrt).then_inc(S["root_made"].sem, 1)

        @block.tensor
        def _(pe):
            def turn(b, h, g):
                s, e = GROUPS[g]
                need(pe, S["onehot_made"], NG * b + g + 1)
                need(pe, S["onehot_back"], NG * b + g - 1)
                for u in range(s, e):
                    last = nc.tensor.transpose(ps_t[:, g % 2, (u - s) * P:(u - s + 1) * P], oh[:, h, u, :], K["ident_b"][:, :])
                last.then_inc(S["onehot_turned"].sem, 1)

            def batch(b, h, i):
                win = offsets(pe, tab, 1, b, (NW - 1) * P)
                turn(b, h, 0)
                need(pe, S["batch_ready"], b + 1)
                need(pe, S["attr_back"], b)
                nc.tensor.transpose(ps_e[0:2 * B, 0:P], ea[:, h, :], K["ident"][:, :]).then_inc(S["attr_turned"].sem, 1)
                for g, (s, e) in enumerate(GROUPS):
                    if g + 1 < NG:
                        turn(b, h, g + 1)
                    need(pe, S["attr_back"], b + 1)
                    need(pe, S["onehot_back"], NG * b + g + 1)
                    need(pe, S["c_made"], NG * b + g - 1)
                    for u in range(s, e):
                        o = ps_h[:, g % 2, (u - s) * F:(u - s + 1) * F]
                        nc.tensor.matmul(o, ohT[:, g % 2, (u - s) * P:(u - s + 1) * P], K["PNf"][:, ds(win[u], F)],
                                         start=True, stop=False)
                        last = nc.tensor.matmul(o, eaT[:, h, :], K["w1c_wide"][:, u, :], start=False, stop=True)
                    last.then_inc(S["h_made"].sem, 1)
            batches(pe, bodies, batch)
            pe.wait_ge(S["mean_parts"].sem, S["mean_parts"].n + 1)
            nc.tensor.matmul(ps_s[:, 0:1], sq[:, 0, 0:F], K["ones"][:, 0:1], start=True, stop=True)\
                .then_inc(S["mean_ready"].sem, 1)
            pe.wait_ge(S["var_made"].sem, 1)
            pe.wait_ge(S["attr_back"].sem, 2 * bodies)
            nc.tensor.matmul(ps_e[:, 0:P], K["ones"][:, :], K["stat"][:, 0, :], start=True, stop=True)\
                .then_inc(S["std_parts"].sem, 1)
    n = 2 * bodies
    passed(S, batch_ready=n, mean_parts=1, mean_ready=1, slots_in0=GATHERED * bodies, slots_in1=GATHERED * bodies,
             gathered0=GATHERED * bodies, gathered1=GATHERED * bodies, c_made=NG * n, onehot_made=NG * n,
             onehot_turned=NG * n, onehot_back=NG * n, h_made=NG * n, attr_turned=n, attr_back=n, var_made=1, root_made=1)


def stage_edge_sum(nc, S, top, d, K):
    with Memory(nc) as m:
        c = m.sb("c_in", [P, 2, B, F])
        t = m.sb("normed", [P, 2, B, F])
        msg = m.sb("messages", [P, 2, B, F])
        oh = m.sb("onehot", [P, 2, B, P])
        acc = m.ps("acc", [P, 4096])
        block = m.block()
        c_in = (S["c_in0"], S["c_in1"])
        bodies = T0 // BODY

        @block.sync
        def _(sp):
            def batch(b, h, i):
                need(sp, S["scaled"], b - 1)
                sp.dma_start(c[:, h, :, :].rearrange("p t f -> p (t f)"),
                             d["c"][ds(b, 1), :, :].rearrange("o p f -> (o p) f")).then_inc(c_in[h].sem, 16)
            batches(sp, bodies, batch)

        @block.gpsimd
        def _(pool):
            def batch(b, h, i):
                need(pool, S["scaled"], b + 1)
                nc.gpsimd.tensor_tensor(t[:, h, :, :], t[:, h, :, :], over_w(K["beta0"][:, :], B), ALU.add)\
                    .then_inc(S["shifted"].sem, 1)
            batches(pool, bodies, batch)

        @block.vector
        def _(v):
            def batch(b, h, i):
                need(v, c_in[h], 16 * (i + 1))
                need(v, S["messages_made"], b - 1)
                nc.vector.tensor_tensor(t[:, h, :, :], c[:, h, :, :], over_w(K["scale"][:, :], B), ALU.mult)\
                    .then_inc(S["scaled"].sem, 1)
                need(v, S["summed"], b - 1)
                nc.vector.tensor_tensor(oh[:, h, :, :], K["col"][:, 0:P].unsqueeze(1).to_broadcast([P, B, P]),
                                        K["loc0"][:, ds(b * B, B)].unsqueeze(2).to_broadcast([P, B, P]),
                                        ALU.is_equal).then_inc(S["onehot_made"].sem, 1)
            batches(v, bodies, batch)
            nc.vector.memset(K["ST"][:, ACC:], 0.0)
            v.wait_ge(S["summed"].sem, S["summed"].n + 2 * bodies)
            nc.vector.tensor_copy(K["ST"][:, 0:ACC // 2], acc[:, 0:ACC // 2])
            nc.vector.tensor_copy(K["ST"][:, ACC // 2:ACC], acc[:, ACC // 2:ACC])

        @block.scalar
        def _(act):
            def batch(b, h, i):
                need(act, S["shifted"], b + 1)
                need(act, S["summed"], b - 1)
                nc.scalar.activation(msg[:, h, :, :], t[:, h, :, :], ACT.Relu).then_inc(S["messages_made"].sem, 1)
            batches(act, bodies, batch)

        @block.tensor
        def _(pe):
            clear_acc(nc, K, acc)

            def batch(b, h, i):
                win = offsets(pe, K["tab0"], 1, b, (NW - 1) * P)
                need(pe, S["onehot_made"], b + 1)
                need(pe, S["messages_made"], b + 1)
                for u in range(B):
                    last = nc.tensor.matmul(acc[:, ds(win[u], P)], msg[:, h, u, :], oh[:, h, u, :], start=False,
                                            stop=True, skip_group_check=True)
                last.then_inc(S["summed"].sem, 1)
            batches(pe, bodies, batch)
    n = 2 * bodies
    passed(S, messages_made=n, summed=n, onehot_made=n)


def stage_nodes0(nc, S, top, d, K):
    with Memory(nc) as m:
        big, st = m.sb("node_work", [P, NW, F]), m.sb("node_stats", [P, 2, NW])
        W2, b2 = m.sb("W2", [P, F]), m.sb("b2", [P, F])
        rdeg = m.sb("rdeg", [P, NW])
        Y = m.sb("Y0", [P, NWP, F])
        p_sum = Projection(nc, m, S, "p1", F, transposed=True)
        p_tab = Projection(nc, m, S, "p2", F, y_cols=F, py=p_sum.py)
        block = m.block()
        X = K["X"][:, 0:NW, :]
        outs = [(slice(0, F), win_of(Y), None)]
        scale = lambda w: K["dinv"][:, ds(w, 1)]
        outs_tab = [(slice(0, F), win_of(K["H"]), scale), (slice(0, F), None, scale)]

        @block.sync
        def _(sp):
            sp.dma_start(W2[:, :], d["L0_gnn_W2"]).then_inc(S["weights_in"].sem, 16)
            sp.dma_start(b2[:, :], d["L0_gnn_b2"].rearrange("(o f) -> o f", o=1).to_broadcast([P, F]))\
                .then_inc(S["weights_in"].sem, 16)
            passed(S, p_back=NWP, p_made=NWP, p_taken=NWP)
            p_tab.sync(sp, d["H"], 2)
            passed(S, p_back=-NWP, p_made=-NWP, p_taken=-NWP)

        @block.scalar
        def _(act):
            p_sum.scalar(act, lambda w: K["STf"][:, ds(w * P, P)].unsqueeze(1), outs)
            root(nc, act, S, K["dinv"][:, 0:NW], 0)
            root(nc, act, S, st[:, 1, :], 1)
            act.wait_ge(S["nodes_made"].sem, S["nodes_made"].n + 1)
            passed(S, p_back=NWP, p_made=NWP, p_taken=NWP)
            p_tab.scalar(act, win_of(K["X"]), outs_tab)
            passed(S, p_back=-NWP, p_made=-NWP, p_taken=-NWP)

        @block.tensor
        def _(pe):
            pe.wait_ge(S["weights_in"].sem, S["weights_in"].n + 32)
            p_sum.tensor(pe, None, lambda c, e: W2[:, :], 1)
            passed(S, p_back=NWP, p_made=NWP, p_taken=NWP)
            p_tab.tensor(pe, K["ident"], lambda c, e: K["W_l1T"][:, :], 2)
            passed(S, p_back=-NWP, p_made=-NWP, p_taken=-NWP)

        @block.vector
        def _(v):
            step = Chain(v, S["vector_steps"])
            v.wait_ge(S["weights_in"].sem, S["weights_in"].n + 32)
            step(nc.vector.memset(K["dinv"][:, :], 1.0))
            nc.vector.tensor_scalar(K["dinv"][:, 0:NW], K["deg"][:, :], 1.0, None, ALU.add).then_inc(S["var_made"].sem, 1)
            v.wait_ge(S["root_made"].sem, S["root_made"].n + 1)
            step(nc.vector.reciprocal(K["dinv"][:, 0:NW], K["dinv"][:, 0:NW]))
            step(nc.vector.tensor_scalar(rdeg[:, :], K["out_deg"][:, :], 1.0, None, ALU.add))
            step(nc.vector.reciprocal(rdeg[:, :], rdeg[:, :]))
            step(nc.vector.tensor_tensor(big[:, :, :], over_f(K["out_deg"][:, :], NW), over_w(b2[:, :], NW), ALU.mult))
            v.wait_ge(S["p_taken"].sem, S["p_taken"].n + NWP)
            step(nc.vector.tensor_tensor(big[:, :, :], big[:, :, :], Y[:, 0:NW, :], ALU.add))
            step(nc.vector.tensor_tensor(big[:, :, :], big[:, :, :], over_f(rdeg[:, :], NW), ALU.mult))
            step(nc.vector.scalar_tensor_tensor(X, X, 2.0, big[:, :, :], ALU.mult, ALU.add))
            layer_norm(nc, v, step, S, X, big[:, :, :], st, 1)
            v.sem_inc(S["nodes_made"].sem, 1)
            step.end()
    p_sum.passed(1)
    p_tab.passed(2)
    passed(S, weights_in=32, var_made=2, root_made=2, nodes_made=1)


def stage_gcn(nc, S, top, d, K):
    with Memory(nc) as m:
        idx = m.sb("rows", [P, 2, B], I32)
        oh = m.sb("onehot", [P, 2, B, P])
        ohb = m.sb("onehot_bf", [P, 2, B, P], BF16)
        ohT = m.sb("onehotT", [P, G0 * P])
        rows = m.sb("H_rows", [P, 2, B, F])
        inv = m.sb("inv_rows", [P, 2, B, R])
        rel = m.sb("onehot_relation", [P, B, R])
        acc = m.ps("acc", [P, 4096])
        ps_t, ps_r = acc[:, BANK7:BANK7 + G0 * P // 2].bitcast(BF16), acc[:, BANK7 + G0 * P // 2:BANK7 + G0 * (P // 2 + R)]
        block = m.block()
        slots_in, gathered = (S["slots_in0"], S["slots_in1"]), (S["gathered2"], S["gathered3"])
        bodies, n = T1 // BODY, 2 * (T1 // BODY)
        slots, loc, tab = K["slots1"], K["loc1"], K["tab1"]

        @block.sync
        def _(sp):
            def batch(b, h, i):
                off = offsets(sp, tab, 0, b, E + GAP)
                need(sp, slots_in[h], GATHERED * i)
                for u in range(B):
                    sp.dma_start(slots[:, ds(b * B + u, 1), :].rearrange("p o c -> p (o c)"),
                                 d["rec1"][ds(off[u], P), 0:REC0]).then_inc(slots_in[h].sem, 16)
            batches(sp, bodies, batch)

        @block.gpsimd
        def _(pool):
            def batch(b, h, i):
                need(pool, S["summed"], b - 1)
                need(pool, S["batch_ready"], b + 1)
                pool.sem_inc(S["gather_go"].sem, 1)
                for u in range(B):
                    nc.gpsimd.indirect_dma_start(rows[:, h, u, :], None, d["H"][:, :],
                                                 bass.IndirectOffsetOnAxis(ap=idx[:, h, u:u + 1], axis=0))\
                        .then_inc(gathered[h].sem, 16)
            batches(pool, bodies, batch)

        @block.vector
        def _(v):
            step = Chain(v, S["vector_steps"])
            n0 = step.n

            def weights(b, h):
                need(v, S["inv_back"], 2 * (b + 1))
                at = ds(b * B, B)
                step(nc.vector.tensor_tensor(rel[:, :, :], K["col"][:, 0:R].unsqueeze(1).to_broadcast([P, B, R]),
                                             slots[:, at, 2:3].to_broadcast([P, B, R]), ALU.is_equal))
                step(nc.vector.tensor_tensor(rel[:, :, :], rel[:, :, :], inv[:, h, :, :], ALU.mult))
                step(nc.vector.tensor_reduce(K["weight"][:, at], rel[:, :, :], AX.X, ALU.add))

            def batch(b, h, i):
                step.n = n0 + 4 * b - (0 if isinstance(b, int) and b == 0 else 3)
                at = ds(b * B, B)
                need(v, slots_in[h], GATHERED * (i + 1))
                need(v, gathered[h], GATHERED * i)
                nc.vector.tensor_copy(idx[:, h, :], slots[:, at, 0])
                step(nc.vector.tensor_tensor(loc[:, at], slots[:, at, 1], loc[:, at], ALU.subtract))
                v.sem_inc(S["batch_ready"].sem, 1)
                need(v, S["summed"], b - 1)
                for u in range(B):
                    nc.vector.tensor_scalar(ohb[:, h, u, :], K["col_b"][:, 0:P], loc[:, ds(b * B + u, 1)], None,
                                            ALU.is_equal)
                for u in range(B):
                    last = nc.vector.tensor_scalar(oh[:, h, u, :], K["col"][:, 0:P], loc[:, ds(b * B + u, 1)], None,
                                                   ALU.is_equal)
                last.then_inc(S["onehot_made"].sem, 1)
                if not (isinstance(b, int) and b == 0):
                    weights(b - 1, 1 - h)
            batches(v, bodies, batch)
            step.n = n0 + 4 * n - 3
            weights(n - 1, 1)
            v.wait_ge(S["summed"].sem, S["summed"].n + n)
            step(nc.vector.tensor_copy(K["ACC"][:, 0:ACC], acc[:, 0:ACC]))
            step.end()

        @block.scalar
        def _(act):
            def batch(b, h, i):
                for g, (s, e) in enumerate(PARTS):
                    need(act, S["onehot_turned"], 2 * b + g + 1)
                    nc.scalar.activation(ohT[:, 0:(e - s) * P], ps_t[:, 0:(e - s) * P], ACT.Copy)\
                        .then_inc(S["onehot_back"].sem, 1)
                    need(act, S["inv_picked"], 2 * b + g + 1)
                    nc.scalar.activation(inv[:, h, s:e, :].rearrange("p t r -> p (t r)"), ps_r[:, 0:(e - s) * R],
                                         ACT.Copy).then_inc(S["inv_back"].sem, 1)
            batches(act, bodies, batch)

        @block.tensor
        def _(pe):
            clear_acc(nc, K, acc)

            def batch(b, h, i):
                win = offsets(pe, tab, 1, b, (NW - 1) * P)
                win_r = offsets(pe, tab, 2, b, (NW - 1) * R)

                def add(u):
                    return nc.tensor.matmul(acc[:, ds(win[u], F)], oh[:, h, u, :], rows[:, h, u, :], start=False,
                                            stop=True, skip_group_check=True)
                need(pe, S["onehot_made"], b + 1)
                need(pe, gathered[h], GATHERED * (i + 1))
                for g, (s, e) in enumerate(PARTS):
                    need(pe, S["inv_back"], 2 * b + g)
                    for u in range(s, e):
                        last = nc.tensor.transpose(ps_t[:, (u - s) * P:(u - s + 1) * P], ohb[:, h, u, :],
                                                   K["ident_b"][:, :])
                    last.then_inc(S["onehot_turned"].sem, 1)
                    for u in range(s, e - 3):
                        add(u)
                    need(pe, S["onehot_back"], 2 * b + g + 1)
                    for u in range(s, e):
                        last = nc.tensor.matmul(ps_r[:, (u - s) * R:(u - s + 1) * R], ohT[:, (u - s) * P:(u - s + 1) * P],
                                                K["inv_count"][:, ds(win_r[u], R)], start=True, stop=True)
                    last.then_inc(S["inv_picked"].sem, 1)
                    for u in range(e - 3, e):
                        last = add(u)
                last.then_inc(S["summed"].sem, 1)
            batches(pe, bodies, batch)
    passed(S, slots_in0=GATHERED * bodies, slots_in1=GATHERED * bodies, batch_ready=n, onehot_made=n, summed=n,
             onehot_turned=2 * n, onehot_back=2 * n)


def stage_nodes1(nc, S, top, d, K):
    with Memory(nc) as m:
        big, st = m.sb("node_work", [P, NW, F]), m.sb("node_stats", [P, 2, NW])
        rows = m.sb("rows_l1", [P, 3, F])
        part = m.sb("part_sums", [P, 2, F])
        ps = m.ps("node_psum", [P, 2, 512])
        block = m.block()
        X, V = K["X"][:, 0:NW, :], K["ACC"].rearrange("p (w f) -> p w f", f=F)
        b, gamma, beta = (rows[:, i, :] for i in range(3))
        dinv = over_f(K["dinv"][:, 0:NW], NW)

        @block.sync
        def _(sp):
            for i, n in enumerate(("L1_gnn_b", "L1_gnn_gamma", "L1_gnn_beta")):
                sp.dma_start(rows[:, i, :], d[n].rearrange("(o f) -> o f", o=1).to_broadcast([P, F]))\
                    .then_inc(S["weights_in"].sem, 16)

        @block.vector
        def _(v):
            step = Chain(v, S["vector_steps"])
            step(nc.vector.tensor_tensor(V, V, K["H"][:, 0:NW, :], ALU.add))
            step(nc.vector.tensor_tensor(V, V, dinv, ALU.mult))
            v.wait_ge(S["weights_in"].sem, S["weights_in"].n + 48)
            step(nc.vector.tensor_tensor(V, V, over_w(b, NW), ALU.add))
            step(nc.vector.tensor_scalar(K["ACC"][:, :], K["ACC"][:, :], 0.0, None, ALU.max))
            step(nc.vector.tensor_tensor(V, V, over_f(K["valid"][:, :], NW), ALU.mult))
            nc.vector.tensor_reduce(part[:, 0, :], V.rearrange("p w f -> p f w"), AX.X, ALU.add)\
                .then_inc(S["mean_parts"].sem, 1)
            v.wait_ge(S["mean_ready"].sem, S["mean_ready"].n + 1)
            step(nc.vector.tensor_scalar(part[:, 0, :], ps[:, 0, 0:F], 1.0 / N, None, ALU.mult))
            step(nc.vector.tensor_tensor(V, V, over_w(part[:, 0, :], NW), ALU.subtract))
            step(nc.vector.tensor_tensor(big[:, :, :], V, over_f(K["valid"][:, :], NW), ALU.mult))
            step(nc.vector.tensor_tensor(big[:, :, :], big[:, :, :], big[:, :, :], ALU.mult))
            nc.vector.tensor_reduce(part[:, 1, :], big[:, :, :].rearrange("p w f -> p f w"), AX.X, ALU.add)\
                .then_inc(S["mean_parts"].sem, 1)
            v.wait_ge(S["mean_ready"].sem, S["mean_ready"].n + 2)
            nc.vector.tensor_scalar(part[:, 1, :], ps[:, 1, 0:F], 1.0 / N, EPS, ALU.mult, ALU.add)\
                .then_inc(S["var_made"].sem, 1)
            v.wait_ge(S["root_made"].sem, S["root_made"].n + 1)
            step(nc.vector.reciprocal(part[:, 1, :], part[:, 1, :]))
            step(nc.vector.tensor_tensor(part[:, 1, :], part[:, 1, :], gamma, ALU.mult))
            step(nc.vector.tensor_tensor(V, V, over_w(part[:, 1, :], NW), ALU.mult))
            step(nc.vector.tensor_tensor(V, V, over_w(beta, NW), ALU.add))
            step(nc.vector.tensor_tensor(X, X, V, ALU.add))
            layer_norm(nc, v, step, S, X, big[:, :, :], st, 1)
            step.end()

        @block.tensor
        def _(pe):
            for i in range(2):
                pe.wait_ge(S["mean_parts"].sem, S["mean_parts"].n + i + 1)
                nc.tensor.matmul(ps[:, i, 0:F], K["ones"][:, :], part[:, i, :], start=True, stop=True)\
                    .then_inc(S["mean_ready"].sem, 1)

        @block.scalar
        def _(act):
            root(nc, act, S, part[:, 1, :], 0)
            root(nc, act, S, st[:, 1, :], 1)
    passed(S, weights_in=48, mean_parts=2, mean_ready=2, var_made=2, root_made=2)


def stage_rgcn(nc, S, top, d, K):
    L, C = 3, R * F + F
    with Memory(nc) as m:
        W = m.sb("W_relations", [P, L, C])
        bias = m.sb("bias_l2", [P, L, F])
        floor = m.sb("floor", [P, L])
        U, ROOT = m.sb("U", [P, NWP, F]), m.sb("ROOT", [P, NWP, F])
        idx = m.sb("rows", [P, 2, B], I32)
        oh = m.sb("onehot", [P, 2, B, P])
        rows = m.sb("Y_rows", [P, 2, B, F])
        st = m.sb("node_stats", [P, 2, NW])
        ps = m.ps("acc", [P, 4096])
        proj = Projection(nc, m, S, "p3", C, y_cols=R * F, py="later", pt="later")
        proj.py = ps[:, 0:3072].rearrange("p (k c) -> p k c", k=2)
        proj.pt = ps[:, 3072:4096].rearrange("p (k c) -> p k c", k=2)
        block = m.block()
        gathered = (S["gathered4"], S["gathered5"])
        bodies, n = T1 // BODY, 2 * (T1 // BODY)
        slots, loc, tab = K["slots1"], K["loc1"], K["tab1"]
        outs = [(slice(0, R * F), None, None), (slice(R * F, C), win_of(ROOT), None)]
        table = d["Y"].rearrange("n (r f) -> (n r) f", r=R)
        U25, ROOT25 = U[:, 0:NW, :], ROOT[:, 0:NW, :]

        @block.sync
        def _(sp):
            for l in range(L):
                w, r, b = (d[f"L2_gnn_{x}{l + 1}"] for x in ("W", "root", "b"))
                sp.dma_start(W[:, l, 0:R * F].rearrange("f (r h) -> f r h", r=R), w.rearrange("r f h -> f r h"))\
                    .then_inc(S["weights_in"].sem, 16)
                sp.dma_start(W[:, l, R * F:C], r).then_inc(S["weights_in"].sem, 16)
                sp.dma_start(bias[:, l, :], b.rearrange("(o f) -> o f", o=1).to_broadcast([P, F]))\
                    .then_inc(S["weights_in"].sem, 16)
            with sp.Fori(0, L) as l:
                proj.sync(sp, d["Y"], 2, l)
                sp.sem_inc(S["table_stored"].sem, 1)

        @block.scalar
        def _(act):
            with act.Fori(0, L) as l:
                act.wait_ge(S["nodes_made"].sem, S["nodes_made"].n + l + 1)
                proj.scalar(act, win_of(U), outs, l)
            root(nc, act, S, st[:, 1, :], 0)

        @block.gpsimd
        def _(pool):
            with pool.Fori(0, L) as l:
                pool.wait_ge(S["table_stored"].sem, l + 1)

                def batch(b, h, i):
                    need(pool, S["summed"], b - 1, l * n)
                    need(pool, S["batch_ready"], b + 1, l * n)
                    pool.sem_inc(S["gather_go"].sem, 1)
                    for u in range(B):
                        nc.gpsimd.indirect_dma_start(rows[:, h, u, :], None, table,
                                                     bass.IndirectOffsetOnAxis(ap=idx[:, h, u:u + 1], axis=0))\
                            .then_inc(gathered[h].sem, 16)
                batches(pool, bodies, batch)

        @block.vector
        def _(v):
            step = Chain(v, S["vector_steps"])
            step(nc.vector.memset(floor[:, :], 0.0))
            step(nc.vector.memset(floor[:, L - 1:L], NEG))
            step(nc.vector.tensor_copy(U[:, :, :], K["X"][:, :, :]))
            v.sem_inc(S["nodes_made"].sem, 1)
            v.wait_ge(S["weights_in"].sem, S["weights_in"].n + 48 * L)
            n0, per_layer = step.n, 3
            with v.Fori(0, L) as l:
                def batch(b, h, i):
                    at = ds(b * B, B)
                    need(v, gathered[h], GATHERED * i, l * (GATHERED * bodies))
                    nc.vector.scalar_tensor_tensor(idx[:, h, :], slots[:, at, 0], float(R), slots[:, at, 2],
                                                   ALU.mult, ALU.add).then_inc(S["batch_ready"].sem, 1)
                    need(v, S["summed"], b - 1, l * n)
                    for u in range(B):
                        t = ds(b * B + u, 1)
                        last = nc.vector.tensor_scalar(oh[:, h, u, :], K["col"][:, 0:P], loc[:, t], K["weight"][:, t],
                                                       ALU.is_equal, ALU.mult)
                    last.then_inc(S["onehot_made"].sem, 1)
                batches(v, bodies, batch)
                step.n = n0 + l * per_layer
                v.wait_ge(S["summed"].sem, S["summed"].n + l * n + n)
                accs = ps[:, 0:ACC].rearrange("p (w f) -> p w f", f=F)
                step(nc.vector.tensor_tensor(ROOT25, ROOT25, accs, ALU.add))
                step(nc.vector.tensor_tensor(ROOT25, ROOT25, bias[:, ds(l, 1), :].to_broadcast([P, NW, F]), ALU.add))
                step(nc.vector.tensor_scalar(U25, ROOT25, floor[:, ds(l, 1)], None, ALU.max))
                v.sem_inc(S["nodes_made"].sem, 1)
            step.n = n0 + L * per_layer
            X = K["X"][:, 0:NW, :]
            step(nc.vector.tensor_tensor(X, X, U25, ALU.add))
            layer_norm(nc, v, step, S, X, ROOT25, st, 0)
            step.end()

        @block.tensor
        def _(pe):
            pe.wait_ge(S["weights_in"].sem, S["weights_in"].n + 48 * L)
            with pe.Fori(0, L) as l:
                proj.tensor(pe, K["ident"], lambda c, e: W[:, ds(l, 1), c:e].rearrange("p o c -> p (o c)"), 2, l)
                pe.wait_ge(S["p_taken"].sem, S["p_taken"].n + (l + 1) * (2 * NWP))
                clear_acc(nc, K, ps)

                def batch(b, h, i):
                    win = offsets(pe, tab, 1, b, (NW - 1) * P)
                    need(pe, S["onehot_made"], b + 1, l * n)
                    need(pe, gathered[h], GATHERED * (i + 1), l * (GATHERED * bodies))
                    for u in range(B):
                        last = nc.tensor.matmul(ps[:, ds(win[u], F)], oh[:, h, u, :], rows[:, h, u, :], start=False,
                                                stop=True, skip_group_check=True)
                    last.then_inc(S["summed"].sem, 1)
                batches(pe, bodies, batch)
    proj.passed(2, L)
    passed(S, weights_in=48 * L, batch_ready=L * n, onehot_made=L * n, summed=L * n, nodes_made=L + 1, var_made=1,
             root_made=1)


def stage_table3(nc, S, top, d, K):
    with Memory(nc) as m:
        W, Wr = m.sb("W1fb", [P, 2 * F]), m.sb("W1req", [EAD, 2 * F])
        b1, req = m.sb("b1fb", [P, 2 * F]), m.sb("req", [EAD, P])
        const = m.sb("const_fb", [P, 2 * F])
        pc = m.ps("const_psum", [P, 512])
        proj = Projection(nc, m, S, "p4", 2 * F, y_cols=2 * F)
        block = m.block()
        loads = [(W[:, i * F:(i + 1) * F], d[f"L3_gnn_W1{x}"][0:F, :]) for i, x in enumerate("fb")]
        loads += [(Wr[:, i * F:(i + 1) * F], d[f"L3_gnn_W1{x}"][F + EAD:, :]) for i, x in enumerate("fb")]
        loads += [(b1[:, i * F:(i + 1) * F], d[f"L3_gnn_b1{x}"].rearrange("(o f) -> o f", o=1).to_broadcast([P, F]))
                  for i, x in enumerate("fb")]
        loads += [(K["one"][0:EAD, 0:1], d["L3_gnn_req_emb"].rearrange("o c -> c o"))]
        wide = K["w1e_wide"]
        wide_loads = [(wide[EAD * j:EAD * (j + 1), i, j, :], d[f"L3_gnn_W1{x}"][F:F + EAD, :])
                      for i, x in enumerate("fb") for j in range(G0)]

        @block.sync
        def _(sp):
            for dst, src in loads:
                sp.dma_start(dst, src).then_inc(S["weights_in"].sem, 16)
            sp.wait_ge(S["zeroed"].sem, S["zeroed"].n + 1)
            for dst, src in wide_loads:
                sp.dma_start(dst, src).then_inc(S["wide_in"].sem, 16)
            proj.sync(sp, d["T3"], 1)
            sp.wait_ge(S["wide_in"].sem, 16 * len(wide_loads))

        @block.gpsimd
        def _(pool):
            nc.gpsimd.memset(wide[:, :, :, :], 0.0).then_inc(S["zeroed"].sem, 1)

        @block.vector
        def _(v):
            step = Chain(v, S["vector_steps"])
            v.wait_ge(S["weights_in"].sem, S["weights_in"].n + 16 * len(loads))
            nc.vector.tensor_scalar(req[:, :], K["ones"][0:EAD, :], K["one"][0:EAD, 0:1], None, ALU.mult)\
                .then_inc(S["req_made"].sem, 1)
            v.wait_ge(S["const_ready"].sem, 1)
            nc.vector.tensor_tensor(const[:, :], pc[:, 0:2 * F], b1[:, :], ALU.add).then_inc(S["const_made"].sem, 1)
            step.end()
        @block.tensor
        def _(pe):
            pe.wait_ge(S["req_made"].sem, 1)
            nc.tensor.matmul(pc[:, 0:2 * F], req[:, :], Wr[:, :], start=True, stop=True).then_inc(S["const_ready"].sem, 1)
            pe.wait_ge(S["const_made"].sem, 1)
            proj.tensor(pe, K["ident"], lambda c, e: W[:, :], 1, extra=(K["ones"][0:1, :], const[0:1, :]))

        @block.scalar
        def _(act):
            proj.scalar(act, win_of(K["X"]), [(slice(0, 2 * F), None, None)])
    proj.passed(1)
    passed(S, weights_in=16 * len(loads), zeroed=1)


def stage_directional(nc, S, top, d, K):
    with Memory(nc) as m:
        attr = m.sb("attr", [P, 2, B, EAD])
        attrT = m.sb("attrT", [P, 2, 2, P])
        idx = m.sb("rows", [P, 2, B], I32)
        oh = m.sb("onehot", [P, 2, B, P])
        rows = m.sb("T3_rows", [P, 2, B, F])
        msg = m.sb("messages", [P, 2, B, F])
        acc = m.ps("acc", [P, 4096])
        block = m.block()
        attr_in, gathered = (S["slots_in0"], S["slots_in1"]), (S["gathered6"], S["gathered7"])
        bodies, n = TH // BODY, 2 * (TH // BODY)
        slots, loc, tab = K["slots1"], K["loc1"], K["tab1"]
        bank = acc[:, BANK7:BANK7 + 512]
        table = d["T3"].rearrange("n (k f) -> (n k) f", k=2)

        @block.sync
        def _(sp):
            for half in range(2):
                def batch(b, h, i):
                    off = offsets(sp, tab, 0, half * (TH // B) + b, E + GAP)
                    need(sp, S["attr_turned"], b - 1, half * n)
                    for u in range(B):
                        sp.dma_start(attr[:, h, u, :], d["rec1"][ds(off[u], P), REC0:REC1]).then_inc(attr_in[h].sem, 16)
                batches(sp, bodies, batch)

        @block.gpsimd
        def _(pool):
            for half in range(2):
                def batch(b, h, i):
                    need(pool, S["c_made"], NG * (b - 1), half * NG * n)
                    need(pool, S["batch_ready"], b + 1, half * n)
                    pool.sem_inc(S["gather_go"].sem, 1)
                    for u in range(B):
                        nc.gpsimd.indirect_dma_start(rows[:, h, u, :], None, table,
                                                     bass.IndirectOffsetOnAxis(ap=idx[:, h, u:u + 1], axis=0))\
                            .then_inc(gathered[h].sem, 16)
                batches(pool, bodies, batch)

        @block.vector
        def _(v):
            for half in range(2):
                nc.vector.memset(K["STf" if half == 0 else "STb"][:, ACC:], 0.0)

                def add(b, h, i):
                    need(v, gathered[h], GATHERED * (i + 1), half * GATHERED * bodies)
                    need(v, S["summed"], b - 1, half * n)
                    for g, (s, e) in enumerate(GROUPS):
                        need(v, S["h_made"], NG * b + g + 1, half * NG * n)
                        nc.vector.tensor_tensor(msg[:, h, s:e, :].rearrange("p t f -> p (t f)"),
                                                bank[:, 0:(e - s) * F],
                                                rows[:, h, s:e, :].rearrange("p t f -> p (t f)"), ALU.add)\
                            .then_inc(S["c_made"].sem, 1)

                def batch(b, h, i):
                    at = ds(half * TH + b * B, B)
                    need(v, gathered[h], GATHERED * i, half * GATHERED * bodies)
                    nc.vector.tensor_scalar(idx[:, h, :], slots[:, at, 0], 2.0, float(half), ALU.mult, ALU.add)\
                        .then_inc(S["batch_ready"].sem, 1)
                    if h:
                        add(b - 1, 0, i)
                    elif not isinstance(i, int):
                        add(b - 1, 1, i - 1)
                    need(v, S["summed"], b - 1, half * n)
                    for u in range(B):
                        last = nc.vector.tensor_scalar(oh[:, h, u, :], K["col"][:, 0:P],
                                                       loc[:, ds(half * TH + b * B + u, 1)], None, ALU.is_equal)
                    last.then_inc(S["onehot_made"].sem, 1)
                batches(v, bodies, batch)
                add(n - 1, 1, bodies - 1)
                v.wait_ge(S["summed"].sem, S["summed"].n + (half + 1) * n)
                nc.vector.tensor_copy(K["STf" if half == 0 else "STb"][:, 0:ACC], acc[:, 0:ACC])\
                    .then_inc(S["half_out"].sem, 1)

        @block.scalar
        def _(act):
            for half in range(2):
                def batch(b, h, i):
                    need(act, S["attr_turned"], b + 1, half * n)
                    for k, (s, e) in enumerate(PARTS):
                        w = (e - s) * EAD
                        last = nc.scalar.activation(attrT[0:w, h, k, :], bank[0:w, k * P:(k + 1) * P], ACT.Copy)
                    last.then_inc(S["attr_back"].sem, 1)
                    for g, (s, e) in enumerate(GROUPS):
                        need(act, S["c_made"], NG * b + g + 1, half * NG * n)
                        nc.scalar.activation(msg[:, h, s:e, :], msg[:, h, s:e, :], ACT.Relu).then_inc(S["messages_made"].sem, 1)
                batches(act, bodies, batch)

        @block.tensor
        def _(pe):
            for half in range(2):
                if half:
                    pe.wait_ge(S["half_out"].sem, 1)
                clear_acc(nc, K, acc)

                def batch(b, h, i):
                    win = offsets(pe, tab, 1, half * (TH // B) + b, (NW - 1) * P)

                    def add(g):
                        s, e = GROUPS[g]
                        need(pe, S["messages_made"], NG * b + g + 1, half * NG * n)
                        for u in range(s, e):
                            last = nc.tensor.matmul(acc[:, ds(win[u], P)], msg[:, h, u, :], oh[:, h, u, :], start=False,
                                                    stop=True, skip_group_check=True)
                        return last
                    need(pe, attr_in[h], GATHERED * (i + 1), half * GATHERED * bodies)
                    need(pe, S["c_made"], NG * b, half * NG * n)
                    for k, (s, e) in enumerate(PARTS):
                        w = (e - s) * EAD
                        last = nc.tensor.transpose(bank[0:w, k * P:(k + 1) * P],
                                                   attr[:, h, s:e, :].rearrange("p t c -> p (t c)"), K["ident"][:, :])
                    last.then_inc(S["attr_turned"].sem, 1)
                    need(pe, S["attr_back"], b + 1, half * n)
                    for g, (s, e) in enumerate(GROUPS):
                        need(pe, S["c_made"], NG * b + g, half * NG * n)
                        for u in range(s, e):
                            k = u >= G0
                            w = (PARTS[k][1] - PARTS[k][0]) * EAD
                            last = nc.tensor.matmul(bank[:, (u - s) * F:(u - s + 1) * F], attrT[0:w, h, int(k), :],
                                                    K["w1e_wide"][0:w, half, u - PARTS[k][0], :], start=True, stop=True)
                        last.then_inc(S["h_made"].sem, 1)
                        if g == 1:
                            need(pe, S["onehot_made"], b + 1, half * n)
                        if g:
                            add(g - 1)
                    add(NG - 1).then_inc(S["summed"].sem, 1)
                batches(pe, bodies, batch)
    passed(S, summed=2 * n, c_made=2 * NG * n, messages_made=2 * NG * n)


def stage_output(nc, S, top, d, K, out):
    with Memory(nc) as m:
        Wf, Wb, Wu = (m.sb(n, [P, F]) for n in ("W2f", "W2b", "Wu"))
        rows = m.sb("rows_l3", [P, 3, F])
        eps = m.sb("eps", [P, 1])
        hb, Y = m.sb("h_base", [P, NWP, F]), m.sb("Y3", [P, NWP, F])
        degb = m.sb("deg_b", [P, NW])
        st = m.sb("node_stats", [P, 2, NW])
        sf, sb_, hT = (m.sb(n, [P, 2, F]) for n in ("windowf", "windowb", "hT"))
        h = m.sb("h", [P, 2, F])
        ps_h, ps_t, ps_o = (m.ps(n, [P, 2, 512]) for n in ("psum_h", "psum_hT", "psum_out"))
        block = m.block()
        X, Y25, hb25 = K["X"][:, 0:NW, :], Y[:, 0:NW, :], hb[:, 0:NW, :]
        loads = [(Wf[:, :], d["L3_gnn_W2f"]), (Wb[:, :], d["L3_gnn_W2b"]), (Wu[:, :], d["L3_gnn_Wu"]),
                 (eps[:, :], d["L3_gnn_eps"].rearrange("(o f) -> o f", o=1).to_broadcast([P, 1]))]
        loads += [(rows[:, i, :], d[f"L3_gnn_{n}"].rearrange("(o f) -> o f", o=1).to_broadcast([P, F]))
                  for i, n in enumerate(("b2f", "b2b", "bu"))]

        @block.sync
        def _(sp):
            for dst, src in loads:
                sp.dma_start(dst, src).then_inc(S["weights_in"].sem, 16)
            sp.wait_ge(S["output_made"].sem, 1)
            sp.dma_start(out[0:(NW - 1) * P, :].rearrange("(w p) f -> p w f", p=P), Y[:, 0:NW - 1, :])\
                .then_inc(S["output_stored"].sem, 16)
            sp.dma_start(out[(NW - 1) * P:N, :], Y[0:LAST, NW - 1, :]).then_inc(S["output_stored"].sem, 16)
            sp.wait_ge(S["output_stored"].sem, 32)

        @block.scalar
        def _(act):
            def body(i, first):
                for k in range(2):
                    n = 2 * i + k
                    w = ds(n * P, P)
                    if not first:
                        act.wait_ge(S["h_psum"].sem, n - 1)
                    nc.scalar.activation(sf[:, k, :], K["STf"][:, w], ACT.Copy)
                    nc.scalar.activation(sb_[:, k, :], K["STb"][:, w], ACT.Copy).then_inc(S["windows_copied"].sem, 1)
                for k in range(2):
                    n = 2 * i + k
                    act.wait_ge(S["h_turned"].sem, n + 1)
                    if not first:
                        act.wait_ge(S["out_psum"].sem, n - 1)
                    nc.scalar.activation(hT[:, k, :], ps_t[:, k, 0:F], ACT.Copy).then_inc(S["h_back"].sem, 1)
                for k in range(2):
                    n = 2 * i + k
                    act.wait_ge(S["out_psum"].sem, n + 1)
                    nc.scalar.activation(Y[:, ds(n, 1), :], ps_o[:, k, 0:F].unsqueeze(1), ACT.Copy)\
                        .then_inc(S["out_taken"].sem, 1)
            peeled(act, NWP // 2, body)
            root(nc, act, S, st[:, 1, :], 0)

        @block.tensor
        def _(pe):
            pe.wait_ge(S["weights_in"].sem, S["weights_in"].n + 16 * len(loads))

            def body(i, first):
                for k in range(2):
                    n = 2 * i + k
                    pe.wait_ge(S["windows_copied"].sem, n + 1)
                    if not first:
                        pe.wait_ge(S["h_summed"].sem, n - 1)
                    nc.tensor.matmul(ps_h[:, k, 0:F], sf[:, k, :], Wf[:, :], start=True, stop=False)
                    nc.tensor.matmul(ps_h[:, k, 0:F], sb_[:, k, :], Wb[:, :], start=False, stop=True)\
                        .then_inc(S["h_psum"].sem, 1)
                for k in range(2):
                    n = 2 * i + k
                    pe.wait_ge(S["h_summed"].sem, n + 1)
                    if not first:
                        pe.wait_ge(S["h_back"].sem, n - 1)
                    nc.tensor.transpose(ps_t[:, k, 0:F], h[:, k, :], K["ident"][:, :]).then_inc(S["h_turned"].sem, 1)
                for k in range(2):
                    n = 2 * i + k
                    pe.wait_ge(S["h_back"].sem, n + 1)
                    if not first:
                        pe.wait_ge(S["out_taken"].sem, n - 1)
                    nc.tensor.matmul(ps_o[:, k, 0:F], hT[:, k, :], Wu[:, :], start=True, stop=True)\
                        .then_inc(S["out_psum"].sem, 1)
            peeled(pe, NWP // 2, body)

        @block.vector
        def _(v):
            step = Chain(v, S["vector_steps"])
            v.wait_ge(S["weights_in"].sem, S["weights_in"].n + 16 * len(loads))
            step(nc.vector.memset(hb[:, NW:NWP, :], 0.0))
            step(nc.vector.tensor_scalar(eps[:, :], eps[:, :], 1.0, None, ALU.add))
            step(nc.vector.tensor_tensor(degb[:, :], K["deg"][:, :], K["deg_f"][:, :], ALU.subtract))
            step(nc.vector.tensor_tensor(hb25, over_f(K["deg_f"][:, :], NW), over_w(rows[:, 0, :], NW), ALU.mult))
            step(nc.vector.tensor_tensor(Y25, over_f(degb[:, :], NW), over_w(rows[:, 1, :], NW), ALU.mult))
            step(nc.vector.tensor_tensor(hb25, hb25, Y25, ALU.add))
            step(nc.vector.scalar_tensor_tensor(hb25, X, eps[:, 0:1], hb25, ALU.mult, ALU.add))

            def body(i, first):
                for k in range(2):
                    n = 2 * i + k
                    v.wait_ge(S["h_psum"].sem, n + 1)
                    if not first:
                        v.wait_ge(S["h_turned"].sem, n - 1)
                    nc.vector.tensor_tensor(h[:, k, :].unsqueeze(1), ps_h[:, k, 0:F].unsqueeze(1), hb[:, ds(n, 1), :], ALU.add)\
                        .then_inc(S["h_summed"].sem, 1)
            peeled(v, NWP // 2, body)
            v.wait_ge(S["out_taken"].sem, NWP)
            step(nc.vector.tensor_tensor(Y25, Y25, over_w(rows[:, 2, :], NW), ALU.add))
            step(nc.vector.scalar_tensor_tensor(Y25, Y25, 0.0, X, ALU.max, ALU.add))
            layer_norm(nc, v, step, S, Y25, hb25, st, 0)
            v.sem_inc(S["output_made"].sem, 1)
            step.end()


def build(nc, d, out):
    scratch = {
        "Q": [NWP * P, F],
        "rec0": [E + GAP, REC0], "rec1": [E + 2 * GAP, REC1], "rec1_given": [E, REC1],
        "tab0w": [1, T0], "tab1w": [1, T1],
        "c": [T0 // B, P, B * F],
        "H": [NWP * P, F], "Y": [NWP * P, R * F], "T3": [NWP * P, 2 * F],
    }
    for name, shape in scratch.items():
        d[name] = nc.dram_tensor(f"scratch_{name}", shape, F32).ap()
    for g, T in ((0, T0), (1, T1)):
        d[f"tab{g}"] = nc.dram_tensor(f"scratch_tab{g}", [3, T], I32).ap()
    with Memory(nc) as top:
        S = signals(nc, top.ctx)
        K = {name: top.sb(name, shape, dt) for name, shape, dt in [
            ("X", [P, NWP, F], F32),
            ("col", [P, NKEY], F32), ("row", [P, 1], F32), ("tile_no", [P, BODY], F32),
            ("col_b", [P, NKEY], BF16), ("ident_b", [P, P], BF16), ("ones", [P, P], F32), ("zeros", [P, 512], BF16), ("ident", [P, P], F32), ("before", [P, P], F32),
            ("before_half", [P, P], F32), ("half0", [P, 1], F32), ("half1", [P, 1], F32),
            ("in_half0", [P, P], F32), ("in_half1", [P, P], F32), ("valid", [P, NW], F32),
            ("W_l1T", [P, F], F32), ("gamma0", [P, F], F32), ("beta0", [P, F], F32), ("scale", [P, F], F32),
            ("stat", [P, 1, F], F32), ("one", [P, 1], F32), ("dinv", [P, NWP], F32),
            ("tab0", [3, T0 // B * BP], I32), ("tab1", [3, T1 // B * BP], I32), ("loc0", [P, T0], F32), ("loc1", [P, T1], F32),
            ("inv_count", [P, NKEY], F32), ("deg", [P, NW], F32), ("deg_f", [P, NW], F32), ("out_deg", [P, NW], F32),
        ]}
        with Memory(nc) as layer0:
            K["PN"] = layer0.sb("PN", [P, NWP, F])
            K["w1c_wide"] = layer0.sb("w1c_wide", [2 * B, B, F])
            with Memory(nc) as front:
                stage_setup(nc, S, top, front, d, K)
                stage_sort(nc, S, top, front, d, K)
            K["PNf"] = K["PN"][:, :, :].rearrange("p w f -> p (w f)")
            stage_edge_mlp(nc, S, top, d, K)
        K["slots1"], K["weight"] = top.sb("slots1", [P, T1, REC0]), top.sb("edge_weight", [P, T1])
        with Memory(nc) as gcn:
            K["H"] = gcn.sb("H", [P, NWP, F])
            with Memory(nc) as sums:
                K["STf"] = K["ST"] = sums.sb("ST", [P, NWP * P])
                stage_edge_sum(nc, S, top, d, K)
                stage_nodes0(nc, S, top, d, K)
            K["ACC"] = gcn.sb("ACC", [P, ACC])
            stage_gcn(nc, S, top, d, K)
            K["ACC"] = K["ACC"][:, :]
            stage_nodes1(nc, S, top, d, K)
        stage_rgcn(nc, S, top, d, K)
        K["STf"], K["STb"] = top.sb("STf", [P, NWP * P]), top.sb("STb", [P, NWP * P])
        with Memory(nc) as directional:
            K["w1e_wide"] = directional.sb("w1e_wide", [G0 * EAD, 2, G0, F])
            stage_table3(nc, S, top, d, K)
            stage_directional(nc, S, top, d, K)
        stage_output(nc, S, top, d, K, out)


_OUT = (N, F)


def kernel(**inputs):
    import numpy as _np
    import concourse.bacc as _bacc
    from concourse.bass_utils import run_bass_kernel_spmd as _run

    nc = _bacc.Bacc("TRN2", target_bir_lowering=False, num_devices=1)
    arrays, d = {}, {}
    for name, value in inputs.items():
        a = _np.ascontiguousarray(value)
        arrays[f"in_{name}"] = a
        d[name] = nc.dram_tensor(f"in_{name}", a.shape, mybir.dt.from_np(a.dtype), kind="ExternalInput").ap()
    out = nc.dram_tensor("out_nodes", _OUT, F32, kind="ExternalOutput").ap()
    build(nc, d, out)
    r = _run(nc, [arrays], core_ids=[0])
    return r.results[0]["out_nodes"]
```

```python
import concourse.bass as bass
from concourse import mybir
from contextlib import ExitStack

F32, I32, BF16 = mybir.dt.float32, mybir.dt.int32, mybir.dt.bfloat16
ALU, ACT, AX = mybir.AluOpType, mybir.ActivationFunctionType, mybir.AxisListType
ds = bass.ds

N, F, E, R = 3125, 128, 100000, 8
P = 128
NW = -(-N // P)
NWP = NW + NW % 2
LAST = N - (NW - 1) * P
ACC = NW * P
B = 13
BP = 16
BODY = 2 * B
HALF = E // 2
T0 = -(-(E // P + NW) // BODY) * BODY
TH = -(-(HALF // P + NW) // BODY) * BODY
T1 = 2 * TH
PS_, LS = 125, E // 125
PD, LD = 100, E // 100
PH = PD // 2
EAD = 16
REC0, REC1 = 4, 4 + EAD
GAP = P
CHUNK = 125
EPS = 1e-5
NKEY = NW * R
WU = 5
assert NW % WU == 0
TERMS = (("high", "high"), ("high", "middle"), ("high", "low"), ("middle", "high"), ("middle", "middle"), ("low", "high"))
NT = len(TERMS)
G0, G1 = 7, 6
KA = NT * 2 * G0
NEG = -3.0e38


SIGNALS = {
    "vector_steps": "the vector engine's own steps, one after the other",
    "pool_steps": "GpSimd's own steps",
    "x_in": "x has been loaded",
    "ids_in": "the edges' node numbers (and relations)",
    "attrs_in": "edge attributes",
    "weights_in": "a stage's weights and rows",
    "wide0_in": "the widened attribute weights of layer 0",
    "wide_in": "the widened attribute weights of layer 3",
    "zeroed": "memory that a load fills in part is zero",
    "iota_made": "the counting rows and columns",
    "ident_made": "the identity",
    "pad_made": "the records that match no node",
    "pads_out": "they are in DRAM",
    "window_counts": "edges of each window, by partition",
    "prefix_ready": "their sums over earlier partitions, and all",
    "feed_ready": "a turn of the scatter by source is laid out",
    "scatter_go": "(a place for a wait before scatters)",
    "scattered0": "records of even turns scattered by source",
    "scattered1": "those of odd turns",
    "rec_made": "parts of a chunk of records",
    "rec_out": "copies of a chunk in DRAM",
    "moved": "whether an edge stands elsewhere than at its rank, by partition",
    "moved_sum": "the number of such partitions",
    "flag_made": "whether there are any",
    "given_in": "given records to scatter",
    "given_rows": "the rows they go to",
    "given_scattered": "they are scattered",
    "onehots_made": "one-hot rows for the counts",
    "counted": "turns of columns of edges counted",
    "tables_made": "tables of tiles",
    "tables_out": "they are in DRAM",
    "tables_in": "they are back, as rows",
    "attr_summed": "sum of edge_attr_2 over the edges",
    "weight_turned": "layer 1's weight transposed",
    "mean_parts": "a mean's parts by partition",
    "mean_ready": "their sum in all partitions",
    "var_made": "a variance, for scalar's root",
    "std_parts": "layer 0's variance as a row",
    "root_made": "its root",
    "slots_in0": "even batch's records or attributes",
    "slots_in1": "odd batch's",
    "batch_ready": "a batch's row numbers (and local nodes)",
    "gather_go": "(a place for a wait before gathers)",
    "gathered0": "rows of an even batch, layer 0",
    "gathered1": "rows of an odd batch, layer 0",
    "gathered2": "rows of an even batch, layer 1",
    "gathered3": "rows of an odd batch, layer 1",
    "gathered4": "rows of an even batch, layer 2",
    "gathered5": "rows of an odd batch, layer 2",
    "gathered6": "rows of an even batch, layer 3",
    "gathered7": "rows of an odd batch, layer 3",
    "attr_made": "a batch's attributes, masked and split",
    "attr_turned": "a batch's attributes transposed, in PSUM",
    "attr_back": "and in SBUF",
    "onehot_made": "one-hot matrices of a group or batch",
    "onehot_turned": "transposed, in PSUM",
    "onehot_back": "and in SBUF",
    "h_made": "products of a group's tiles in PSUM",
    "c_made": "the gathered rows added to them",
    "squared": "squares of a batch",
    "squares_added": "added to their sum",
    "c_stored0": "c of an even batch in DRAM",
    "c_stored1": "c of an odd batch",
    "c_in0": "c of an even batch loaded",
    "c_in1": "c of an odd one",
    "scaled": "c times the batch norm's scale",
    "shifted": "plus its shift",
    "messages_made": "messages of a batch or group",
    "summed": "messages of a batch (layer 1: of a part of it) added to the accumulator",
    "inv_picked": "a group's rows of relation weights, in PSUM",
    "inv_back": "and in SBUF",
    "nodes_made": "the nodes' new values",
    "table_stored": "layer 2's table is in DRAM",
    "req_made": "req_emb as a stationary operand",
    "const_ready": "req W1req",
    "const_made": "plus b1",
    "half_out": "an accumulator of half the edges has been copied out",
    "p_copied": "projection: window at its fixed place",
    "p_turned": "transposed, in PSUM",
    "p_back": "and in SBUF",
    "p_made": "product in PSUM",
    "p_taken": "product's parts copied out",
    "p_stored0": "even window's product in DRAM",
    "p_stored1": "odd window's",
    "windows_copied": "output: both sums' window at their fixed places",
    "h_psum": "their products",
    "h_summed": "h of a window",
    "h_turned": "transposed, in PSUM",
    "h_back": "and in SBUF",
    "out_psum": "h Wu",
    "out_taken": "copied out",
    "output_made": "the result",
    "output_stored": "it is in DRAM",
}


class Signal:

    def __init__(self, nc, ctx, name):
        self.sem, self.n = ctx.enter_context(nc.semaphore(name)), 0


def signals(nc, ctx):
    return {name: Signal(nc, ctx, name) for name in SIGNALS}


def passed(S, **added):
    for name, k in added.items():
        S[name].n += k


class Chain:

    def __init__(self, eng, signal):
        self.eng, self.steps, self.sem, self.n = eng, signal, signal.sem, signal.n

    def __call__(self, ins):
        ins.then_inc(self.sem, 1)
        self.n = self.n + 1
        self.eng.wait_ge(self.sem, self.n)

    def end(self):
        self.steps.n = self.n


def peeled(eng, n, body):
    body(0, True)
    with eng.Fori(1, n) as i:
        body(i, False)


def over_f(ap, w):
    return ap.unsqueeze(2).to_broadcast([P, w, F])


def over_w(ap, w):
    return ap.unsqueeze(1).to_broadcast([P, w, F])


class Memory:

    made = 0

    def __init__(self, nc):
        self.nc, self.ctx = nc, ExitStack()

    def unique(self, name):
        Memory.made += 1
        return f"{name}_{Memory.made}"

    def __enter__(self):
        self.ctx.__enter__()
        return self

    def __exit__(self, *a):
        return self.ctx.__exit__(*a)

    def sb(self, name, shape, dt=F32):
        return self.ctx.enter_context(self.nc.sbuf_tensor(self.unique(name), shape, dt))

    def ps(self, name, shape, dt=F32):
        return self.ctx.enter_context(self.nc.psum_tensor(self.unique(name), shape, dt))

    def block(self):
        return self.ctx.enter_context(self.nc.Block())


class Projection:

    def __init__(self, nc, m, S, name, cols, transposed=False, py=None, pt=None, y_cols=None, keep=None):
        self.nc, self.cols, self.transposed, self.S, self.keep = nc, cols, transposed, S, keep
        self.xs = m.sb(f"{name}_window", [P, 2, F])
        self.xt = m.sb(f"{name}_windowT", [P, 2, F])
        self.y = m.sb(f"{name}_product", [P, 2, y_cols]) if y_cols else None
        self.pt = pt if transposed or pt is not None else m.ps(f"{name}_psumT", [P, 2, 512])
        self.py = m.ps(f"{name}_psum", [P, 2, -(-cols // 512) * 512]) if py is None else py

    def steps(self, eng, step):
        for n in range(4):
            step(n, n % 2)
        with eng.Fori(2, NWP // 2 - 1) as i:
            for k in range(2):
                step(2 * i + k, k)
        for k in range(2):
            step(NWP - 2 + k, k)

    def scalar(self, act, src, outs, l=0):
        nc, S, base = self.nc, self.S, l * NWP

        def out(n, k):
            need(act, S["p_made"], n + 1, base)
            if self.y is not None:
                need(act, (S["p_stored0"], S["p_stored1"])[k], 8 * (n - k), l * (8 * NWP))
            for cols, dst, scale in outs:
                to = self.y[:, k, :].unsqueeze(1) if dst is None else dst(n)
                nc.scalar.activation(to, self.py[:, k, cols].unsqueeze(1),
                                     ACT.Copy if scale is None else ACT.Identity,
                                     scale=1.0 if scale is None else scale(n)).then_inc(S["p_taken"].sem, 1)

        def copy(n, k):
            need(act, S["p_turned"], n - 1, base)
            nc.scalar.activation(self.xs[:, k, :].unsqueeze(1), src(n), ACT.Copy).then_inc(S["p_copied"].sem, 1)

        def step(n, k):
            if self.transposed:
                need(act, S["p_made"], n - 1, base)
                nc.scalar.activation(self.xt[:, k, :].unsqueeze(1), src(n), ACT.Copy).then_inc(S["p_back"].sem, 1)
            else:
                if not (isinstance(n, int) and n == NWP - 1):
                    copy(n + 1, 1 - k)
                need(act, S["p_turned"], n + 1, base)
                need(act, S["p_made"], n - 1, base)
                if self.keep is not None:
                    nc.scalar.activation(self.keep[:, ds(n, 1), :], self.pt[:, k, 0:P].unsqueeze(1), ACT.Copy)
                nc.scalar.activation(self.xt[:, k, :], self.pt[:, k, 0:P], ACT.Copy).then_inc(S["p_back"].sem, 1)
            if not (isinstance(n, int) and n == 0):
                out(n - 1, 1 - k)
        if not self.transposed:
            copy(0, 0)
        self.steps(act, step)
        out(NWP - 1, 1)

    def tensor(self, pe, ident, weight, per, l=0, extra=None):
        nc, S, base = self.nc, self.S, l * NWP

        def product(n, k):
            need(pe, S["p_back"], n + 1, base)
            need(pe, S["p_taken"], per * (n - 1), l * (per * NWP))
            for c in range(0, self.cols, 512):
                e = min(c + 512, self.cols)
                last = nc.tensor.matmul(self.py[:, k, c:e], self.xt[:, k, :], weight(c, e), start=True,
                                        stop=extra is None)
                if extra is not None:
                    last = nc.tensor.matmul(self.py[:, k, c:e], extra[0], extra[1], start=False, stop=True)
            last.then_inc(S["p_made"].sem, 1)

        def step(n, k):
            if not self.transposed:
                need(pe, S["p_copied"], n + 1, base)
                need(pe, S["p_back"], n - 1, base)
                nc.tensor.transpose(self.pt[:, k, 0:P], self.xs[:, k, :], ident[:, :]).then_inc(S["p_turned"].sem, 1)
            if not (isinstance(n, int) and n == 0):
                product(n - 1, 1 - k)
        self.steps(pe, step)
        product(NWP - 1, 1)

    def sync(self, sp, table, per, l=0):
        S = self.S

        def body(i, first):
            for k in range(2):
                sp.wait_ge(S["p_taken"].sem, S["p_taken"].n + per * (l * NWP + 2 * i + k + 1))
                sp.dma_start(table[ds((2 * i + k) * P, P), :], self.y[:, k, :])\
                    .then_inc((S["p_stored0"], S["p_stored1"])[k].sem, 16)
        peeled(sp, NWP // 2, body)
        for s in (S["p_stored0"], S["p_stored1"]):
            sp.wait_ge(s.sem, s.n + 16 * (l + 1) * (NWP // 2))

    def passed(self, per, calls=1):
        added = {"p_back": NWP, "p_made": NWP, "p_taken": per * NWP}
        if not self.transposed:
            added |= {"p_copied": NWP, "p_turned": NWP}
        if self.y is not None:
            added |= {"p_stored0": 8 * NWP, "p_stored1": 8 * NWP}
        passed(self.S, **{k: v * calls for k, v in added.items()})


def win_of(t):
    return lambda w: t[:, ds(w, 1), :]


def count_windows(nc, v, step, win, mask, col, cnt, parts):
    n0 = step.n
    with v.Fori(0, NW // WU) as i:
        step.n = n0 + i * WU
        for k in range(WU):
            b = ds(i * WU + k, 1)
            step(nc.vector.tensor_scalar(mask, win, col[0:parts, b], 0.0, ALU.is_equal, ALU.add,
                                         accum_out=cnt[:, b]))
    step.n = n0 + NW


def rank_edges(nc, v, step, win, ones, mask, cum, sel, col, base, pos, parts):
    n0 = step.n
    with v.Fori(0, NW // WU) as i:
        step.n = n0 + i * (4 * WU)
        for k in range(WU):
            b = ds(i * WU + k, 1)
            step(nc.vector.tensor_scalar(mask, win, col[0:parts, b], None, ALU.is_equal))
            step(nc.vector.tensor_tensor_scan(cum, ones, mask, base[:, b], ALU.mult, ALU.add))
            step(nc.vector.scalar_tensor_tensor(sel, win, col[0:parts, b], cum, ALU.is_equal, ALU.mult))
            step(nc.vector.tensor_tensor(pos, pos, sel, ALU.add))
    step.n = n0 + 4 * NW


def stage_setup(nc, S, top, front, d, K):
    K["w1c_wide32"] = front.sb("w1c_wide32", [KA, G0, F])
    K["rec0_sb"] = front.sb("rec0_sb", [PS_, LS, REC0])
    K["pos0"] = front.sb("pos0", [PS_, LS])
    K["win0"] = front.sb("win0", [PS_, LS])
    K["lo0"] = front.sb("lo0", [PS_, LS])
    K["QN"] = front.sb("QN", [P, NWP, F])
    K["ea2_sum"] = front.sb("ea2_sum", [PS_, 2])
    K["tot0"] = front.sb("tot0", [P, NW])
    K["W1ab"] = front.sb("W1ab", [P, 2 * F])
    K["W1c"] = front.sb("W1c", [2, F])
    K["b1"] = front.sb("b1", [P, F])
    K["W_l1"] = front.sb("W_l1", [P, F])
    with Memory(nc) as m:
        work = m.sb("rank_work", [PS_, 4, LS])
        srcI, dstI, winI = (m.sb(n, [PS_, LS], I32) for n in ("srcI", "dstI", "winI"))
        ea2 = m.sb("ea2", [PS_, LS, 2])
        cnt, base = m.sb("cnt", [PS_, NW]), m.sb("base", [PS_, NW])
        pad = m.sb("pad", [P, 2, REC1])
        pref = m.ps("prefix_psum", [P, 512])
        proj = Projection(nc, m, S, "p0", 2 * F, y_cols=F)
        outs = [(slice(0, F), win_of(K["PN"]), None), (slice(F, 2 * F), win_of(K["QN"]), None),
                (slice(F, 2 * F), None, None)]
        block = m.block()
        ones, mask, cum, sel = (work[:, i, :] for i in range(4))
        loads = [(K["W1ab"][:, 0:F], d["L0_gnn_W1"][0:F, :]), (K["W1ab"][:, F:], d["L0_gnn_W1"][F:2 * F, :]),
                 (K["W1c"][:, :], d["L0_gnn_W1"][2 * F:, :]), (K["W_l1"][:, :], d["L1_gnn_W"])]
        wide_loads = [(K["w1c_wide32"][(j * G0 + u) * 2:(j * G0 + u) * 2 + 2, u, :], d["L0_gnn_W1"][2 * F:, :])
                      for j in range(NT) for u in range(G0)]
        loads += [(K[n][:, :], d[a].rearrange("(o f) -> o f", o=1).to_broadcast([P, F]))
                  for n, a in [("b1", "L0_gnn_b1"), ("gamma0", "L0_gnn_gamma"), ("beta0", "L0_gnn_beta")]]
        x_in, w_in, ids_in, attrs_in, zeroed = S["x_in"], S["weights_in"], S["ids_in"], S["attrs_in"], S["zeroed"]

        @block.sync
        def _(sp):
            sp.dma_start(srcI[:, :], d["src"].rearrange("(p t) -> p t", p=PS_)).then_inc(ids_in.sem, 16)
            sp.dma_start(dstI[:, :], d["dst"].rearrange("(p t) -> p t", p=PS_)).then_inc(ids_in.sem, 16)
            sp.dma_start(ea2[:, :, :], d["edge_attr_2"].rearrange("(p t) c -> p t c", p=PS_))\
                .then_inc(attrs_in.sem, 16)
            sp.wait_ge(zeroed.sem, 2)
            sp.dma_start(K["X"][:, 0:NW - 1, :],
                         d["x"][0:(NW - 1) * P, :].rearrange("(w p) f -> p w f", p=P)).then_inc(x_in.sem, 16)
            sp.dma_start(K["X"][0:LAST, NW - 1, :], d["x"][(NW - 1) * P:N, :]).then_inc(x_in.sem, 16)
            for dst, src in loads:
                sp.dma_start(dst, src).then_inc(w_in.sem, 16)
            for dst, src in wide_loads:
                sp.dma_start(dst, src).then_inc(S["wide0_in"].sem, 16)
            sp.wait_ge(S["pad_made"].sem, 1)
            sp.dma_start(d["rec0"][E:E + GAP, :], pad[:, 0, 0:REC0]).then_inc(S["pads_out"].sem, 16)
            sp.dma_start(d["rec1"][HALF:HALF + GAP, :], pad[:, 1, :]).then_inc(S["pads_out"].sem, 16)
            sp.dma_start(d["rec1"][E + GAP:E + 2 * GAP, :], pad[:, 1, :]).then_inc(S["pads_out"].sem, 16)
            proj.sync(sp, d["Q"], 3)
            sp.wait_ge(S["pads_out"].sem, 48)
            sp.wait_ge(S["wide0_in"].sem, 16 * len(wide_loads))

        @block.gpsimd
        def _(pool):
            step = Chain(pool, S["pool_steps"])
            nc.gpsimd.memset(K["X"][:, :, :], 0.0).then_inc(zeroed.sem, 1)
            nc.gpsimd.memset(K["w1c_wide32"][:, :, :], 0.0).then_inc(zeroed.sem, 1)
            nc.gpsimd.iota(K["col"][:, :], [[1, NKEY]], base=0, channel_multiplier=0,
                           allow_small_or_imprecise_dtypes=True).then_inc(S["iota_made"].sem, 1)
            nc.gpsimd.iota(K["row"][:, :], [[1, 1]], base=0, channel_multiplier=1,
                           allow_small_or_imprecise_dtypes=True).then_inc(S["iota_made"].sem, 1)
            nc.gpsimd.iota(K["tile_no"][:, :], [[1, BODY]], base=0, channel_multiplier=BODY,
                           allow_small_or_imprecise_dtypes=True).then_inc(S["iota_made"].sem, 1)
            step(nc.gpsimd.memset(pad[:, :, :], 0.0))
            step(nc.gpsimd.memset(pad[:, 0, 0:1], -1.0))
            nc.gpsimd.memset(pad[:, 1, 1:2], -1.0).then_inc(S["pad_made"].sem, 1)
            step.end()

        @block.vector
        def _(v):
            step = Chain(v, S["vector_steps"])
            col, row = K["col"], K["row"]
            step(nc.vector.memset(ones, 1.0))
            step(nc.vector.memset(K["ones"][:, :], 1.0))
            step(nc.vector.memset(K["zeros"][:, :], 0.0))
            step(nc.vector.memset(K["pos0"][:, :], 0.0))
            v.wait_ge(S["iota_made"].sem, 3)
            step(nc.vector.tensor_scalar(K["before"][:, :], col[:, 0:P], row[:, 0:1], None, ALU.is_gt))
            nc.vector.tensor_scalar(K["ident"][:, :], col[:, 0:P], row[:, 0:1], None, ALU.is_equal)\
                .then_inc(S["ident_made"].sem, 1)
            step(nc.vector.tensor_copy(K["col_b"][:, :], col[:, :]))
            step(nc.vector.tensor_copy(K["ident_b"][:, :], K["ident"][:, :]))
            step(nc.vector.tensor_scalar(K["half1"][:, :], row[:, 0:1], float(PH), None, ALU.is_ge))
            step(nc.vector.tensor_scalar(K["half0"][:, :], row[:, 0:1], float(PH), None, ALU.is_lt))
            step(nc.vector.tensor_scalar(K["before_half"][:, :], col[:, 0:P], float(PH), None, ALU.is_ge))
            step(nc.vector.tensor_scalar(K["before_half"][:, :], K["before_half"][:, :], K["half1"][:, 0:1], None,
                                         ALU.is_equal))
            step(nc.vector.tensor_tensor(K["before_half"][:, :], K["before_half"][:, :], K["before"][:, :], ALU.mult))
            step(nc.vector.tensor_scalar(K["in_half0"][:, :], K["ones"][:, :], K["half0"][:, 0:1], None, ALU.mult))
            step(nc.vector.tensor_scalar(K["in_half1"][:, :], K["ones"][:, :], K["half1"][:, 0:1], None, ALU.mult))
            step(nc.vector.memset(K["valid"][:, :], 1.0))
            step(nc.vector.tensor_scalar(K["valid"][:, NW - 1:NW], row[:, 0:1], float(LAST), None, ALU.is_lt))
            v.wait_ge(ids_in.sem, 32)
            win, rec = K["win0"][:, :], K["rec0_sb"]
            step(nc.vector.tensor_single_scalar(winI[:, :], srcI[:, :], 7, ALU.arith_shift_right))
            step(nc.vector.tensor_copy(win, winI[:, :]))
            count_windows(nc, v, step, win, mask, col, cnt, PS_)
            nc.vector.tensor_copy(cum[:, 0:1], cnt[:, 0:1]).then_inc(S["window_counts"].sem, 1)
            v.wait_ge(S["prefix_ready"].sem, 1)
            tot = K["tot0"]
            step(nc.vector.tensor_copy(tot[:, :], pref[:, 64:64 + NW]))
            step(nc.vector.tensor_tensor_scan(base[:, :], K["ones"][0:PS_, 0:NW], tot[0:PS_, :], -1.0,
                                              ALU.mult, ALU.add))
            step(nc.vector.tensor_tensor(base[:, :], base[:, :], tot[0:PS_, :], ALU.subtract))
            step(nc.vector.tensor_tensor(base[:, :], base[:, :], pref[0:PS_, 0:NW], ALU.add))
            rank_edges(nc, v, step, win, ones, mask, cum, sel, col, base, K["pos0"][:, :], PS_)
            v.wait_ge(attrs_in.sem, 16)
            step(nc.vector.tensor_copy(rec[:, :, 0], srcI[:, :]))
            step(nc.vector.tensor_copy(rec[:, :, 1], dstI[:, :]))
            step(nc.vector.tensor_copy(rec[:, :, 2:4], ea2[:, :, :]))
            step(nc.vector.scalar_tensor_tensor(K["lo0"][:, :], win, -float(P), rec[:, :, 0], ALU.mult, ALU.add))
            step(nc.vector.tensor_reduce(K["ea2_sum"][:, :], ea2[:, :, :].rearrange("p t c -> p c t"), AX.X, ALU.add))
            step.end()

        @block.tensor
        def _(pe):
            pe.wait_ge(S["window_counts"].sem, 1)
            nc.tensor.matmul(pref[0:PS_, 0:NW], K["before"][0:PS_, 0:PS_], cnt[:, :], start=True, stop=True)
            nc.tensor.matmul(pref[:, 64:64 + NW], K["ones"][0:PS_, :], cnt[:, :], start=True, stop=True)\
                .then_inc(S["prefix_ready"].sem, 1)
            pe.wait_ge(w_in.sem, 16 * len(loads))
            pe.wait_ge(S["ident_made"].sem, 1)
            proj.tensor(pe, K["ident"], lambda c, e: K["W1ab"][:, c:e], 3)

        @block.scalar
        def _(act):
            act.wait_ge(x_in.sem, 32)
            proj.scalar(act, win_of(K["X"]), outs)
    proj.passed(3)
    passed(S, ids_in=32, window_counts=1, prefix_ready=1, attrs_in=16, weights_in=16 * len(loads), iota_made=3, zeroed=2)


def tile_table(nc, step, K, tmp, tot, tiles, first_row, limit, tab):
    rows = tiles // BODY
    v = nc.vector
    ti, f, big, red = tmp
    tf, ct, cn, dd, diff = (f[:, i, :] for i in range(5))
    ones = K["ones"][:, 0:NW]
    step(v.tensor_scalar(ti[:, :], tot, float(P - 1), None, ALU.add))
    step(v.tensor_single_scalar(ti[:, :], ti[:, :], 7, ALU.arith_shift_right))
    step(v.tensor_copy(tf, ti[:, :]))
    step(v.tensor_tensor_scan(ct, ones, tf, 0.0, ALU.mult, ALU.add))
    step(v.tensor_tensor_scan(cn, ones, tot, float(first_row), ALU.mult, ALU.add))
    step(v.tensor_tensor(cn, cn, tot, ALU.subtract))
    step(v.tensor_tensor(dd, ct, tf, ALU.subtract))
    step(v.scalar_tensor_tensor(dd, dd, -float(P), cn, ALU.mult, ALU.add))
    step(v.tensor_tensor(diff[:, 0:NW - 1], dd[:, 1:NW], dd[:, 0:NW - 1], ALU.subtract))
    no = K["tile_no"][:, :]
    shape = [P, BODY, NW - 1]
    step(v.tensor_tensor(big[:, :, :], ct[:, 0:NW - 1].unsqueeze(1).to_broadcast(shape),
                         no.unsqueeze(2).to_broadcast(shape), ALU.is_le))
    step(v.tensor_reduce(red[:, 0, :], big[:, :, :], AX.X, ALU.add))
    step(v.tensor_tensor(big[:, :, :], big[:, :, :], diff[:, 0:NW - 1].unsqueeze(1).to_broadcast(shape), ALU.mult))
    step(v.tensor_reduce(red[:, 1, :], big[:, :, :], AX.X, ALU.add))
    step(v.scalar_tensor_tensor(red[:, 2, :], no, float(P), red[:, 1, :], ALU.mult, ALU.add))
    step(v.tensor_scalar(tab[0:rows, 0, :], red[0:rows, 2, :], dd[0:rows, 0:1], float(limit), ALU.add, ALU.min))
    step(v.tensor_scalar(tab[0:rows, 1, :], red[0:rows, 0, :], float(P), None, ALU.mult))
    step(v.tensor_scalar(tab[0:rows, 2, :], red[0:rows, 0, :], float(R), None, ALU.mult))


def stage_sort(nc, S, top, front, d, K):
    COLS = 10
    with Memory(nc) as m:
        idx_ring = m.sb("scatter_rows", [P, 2, COLS], I32)
        rec_ring = m.sb("scatter_recs", [P, 2, COLS * REC1])
        srcI, dstI, typI, posI = (m.sb(n, [PD, LD], I32) for n in ("by_dst_src", "by_dst_dst", "by_dst_type", "pos1_i"))
        work = m.sb("by_dst_work", [PD, 5, LD])
        pos, lo, key, place = (m.sb(n, [PD, LD]) for n in ("pos1", "lo1", "key1", "place1"))
        attr = m.sb("attr_chunk", [PD, CHUNK, EAD])
        rec = m.sb("rec_chunk", [PD, CHUNK, REC1])
        cnt, base = m.sb("cnt1", [PD, NW]), m.sb("base1", [PD, NW])
        tot = m.sb("tot1", [P, 2, NW])
        ohl = m.sb("onehot_local", [P, 2, COLS, P], BF16)
        ohk = m.sb("onehot_key", [P, 2, COLS, NKEY], BF16)
        tab = m.sb("tile_rows", [P, 3, 3, BODY])
        tabI = m.sb("tile_rows_i", [P, 3, 3, BODY], I32)
        tmp = (m.sb("tile_i", [P, NW], I32), m.sb("tile_f", [P, 5, NW]), m.sb("tile_m", [P, BODY, NW - 1]),
               m.sb("tile_r", [P, 3, BODY]))
        wide_rest, wide_parts = m.sb("w1c_rest", [KA, G0, F]), m.sb("w1c_parts", [KA, 3, G0, F], BF16)
        term, is_term, takes = m.sb("term", [KA, 1]), m.sb("is_term", [KA, NT]), m.sb("takes_part", [KA, 3])
        big = m.sb("mean_work", [P, NW, F])
        red = m.sb("mean_sum", [P, 2, F])
        ea_b = m.sb("attr_sum", [2, P])
        rel_f = m.sb("counts_half0", [P, NKEY])
        flag, flagI = m.sb("flag", [PD, 2]), m.sb("flag_i", [1, 1], I32)
        zeroW = m.sb("zero_bf", [P, 512], BF16)
        pref = m.ps("prefix1_psum", [P, 512])
        cps = m.ps("count_psum", [P, 2, 512])
        mps = m.ps("mean_psum", [P, 512])
        fps = m.ps("small_psum", [P, 512])
        block = m.block()
        ones, mask, cum, sel, win = (work[:, i, :] for i in range(5))

        @block.sync
        def _(sp):
            for t, name in ((dstI, "dst"), (typI, "edge_type_8"), (srcI, "src")):
                sp.dma_start(t[:, :], d[name].rearrange("(p t) -> p t", p=PD)).then_inc(S["ids_in"].sem, 16)
            attrs = d["edge_attr_16"].rearrange("(p t) c -> p t c", p=PD)
            given = d["rec1_given"].rearrange("(p t) c -> p t c", p=PD)
            halves = [d["rec1"][h * (HALF + GAP):h * (HALF + GAP) + HALF, :].rearrange("(p t) c -> p t c", p=PH)
                      for h in range(2)]

            def body(i, first):
                if not first:
                    sp.wait_ge(S["rec_out"].sem, 48 * i)
                at = ds(i * CHUNK, CHUNK)
                sp.dma_start(attr[:, :, :], attrs[:, at, :]).then_inc(S["attrs_in"].sem, 16)
                sp.wait_ge(S["rec_made"].sem, 5 * i + 5)
                sp.dma_start(given[:, at, :], rec[:, :, :]).then_inc(S["rec_out"].sem, 16)
                for h in range(2):
                    sp.dma_start(halves[h][:, at, :], rec[h * PH:(h + 1) * PH, :, :]).then_inc(S["rec_out"].sem, 16)
            peeled(sp, LD // CHUNK, body)
            sp.wait_ge(S["rec_out"].sem, 48 * (LD // CHUNK))
            sp.wait_ge(S["tables_made"].sem, 1)
            n = 0
            for g, (name, at, rows) in enumerate((("tab0", 0, T0 // BODY), ("tab1", 0, TH // BODY),
                                                  ("tab1", TH, TH // BODY))):
                for j in range(3):
                    sp.dma_start(d[name][j, at:at + rows * BODY].rearrange("(p t) -> p t", t=BODY),
                                 tabI[0:rows, g, j, :]).then_inc(S["tables_out"].sem, 16)
                sp.dma_start(d[name + "w"][0, at:at + rows * BODY].rearrange("(p t) -> p t", t=BODY),
                             tab[0:rows, g, 1, :]).then_inc(S["tables_out"].sem, 16)
                n += 4
            sp.wait_ge(S["tables_out"].sem, 16 * n)
            for g, T in ((0, T0), (1, T1)):
                sp.dma_start(K[f"tab{g}"][:, :].rearrange("r (b t) -> r b t", t=BP)[:, :, 0:B],
                             d[f"tab{g}"].rearrange("r (b t) -> r b t", t=B)).then_inc(S["tables_in"].sem, 16)
                sp.dma_start(K[f"loc{g}"][:, :], d[f"tab{g}w"].to_broadcast([P, T])).then_inc(S["tables_in"].sem, 16)
            sp.wait_ge(S["tables_in"].sem, 64)

        @block.gpsimd
        def _(pool):
            nc.gpsimd.iota(place[:, :], [[1, LD]], base=0, channel_multiplier=LD,
                           allow_small_or_imprecise_dtypes=True).then_inc(S["iota_made"].sem, 1)

            def body(i, first):
                for h in range(2):
                    turn = 2 * i + h
                    if not first:
                        pool.wait_ge(S[f"scattered{h}"].sem, 16 * COLS * i)
                    nc.gpsimd.tensor_copy(idx_ring[0:PS_, h, :], K["pos0"][:, ds(turn * COLS, COLS)])\
                        .then_inc(S["feed_ready"].sem, 1)
                    nc.gpsimd.tensor_copy(rec_ring[0:PS_, h, 0:COLS * REC0].rearrange("p (t c) -> p t c", c=REC0),
                                          K["rec0_sb"][:, ds(turn * COLS, COLS), :]).then_inc(S["feed_ready"].sem, 1)
                    pool.wait_ge(S["feed_ready"].sem, 2 * turn + 2)
                    pool.sem_inc(S["scatter_go"].sem, 1)
                    for k in range(COLS):
                        nc.gpsimd.indirect_dma_start(
                            d["rec0"][:, :], bass.IndirectOffsetOnAxis(ap=idx_ring[0:PS_, h, k:k + 1], axis=0),
                            rec_ring[0:PS_, h, k * REC0:(k + 1) * REC0], None).then_inc(S[f"scattered{h}"].sem, 16)
            peeled(pool, LS // COLS // 2, body)
            for h in range(2):
                pool.wait_ge(S[f"scattered{h}"].sem, 8 * LS)
            pool.wait_ge(S["flag_made"].sem, 1)
            pool.wait_ge(S["rec_out"].sem, 48 * (LD // CHUNK))
            unsorted = pool.value_load(flagI[0:1, 0:1], min_val=0, max_val=1)
            given = d["rec1_given"].rearrange("(p t) c -> p t c", p=PD)
            with pool.If(unsorted):
                def body(i, first):
                    nc.gpsimd.dma_start(rec_ring[0:PD, 0, 0:COLS * REC1].rearrange("p (t c) -> p t c", c=REC1),
                                        given[:, ds(i * COLS, COLS), :]).then_inc(S["given_in"].sem, 16)
                    nc.gpsimd.tensor_copy(idx_ring[0:PD, 0, :], posI[:, ds(i * COLS, COLS)]).then_inc(S["given_rows"].sem, 1)
                    pool.wait_ge(S["given_in"].sem, 16 * i + 16)
                    pool.wait_ge(S["given_rows"].sem, i + 1)
                    pool.sem_inc(S["scatter_go"].sem, 1)
                    for k in range(COLS):
                        nc.gpsimd.indirect_dma_start(
                            d["rec1"][:, :], bass.IndirectOffsetOnAxis(ap=idx_ring[0:PD, 0, k:k + 1], axis=0),
                            rec_ring[0:PD, 0, k * REC1:(k + 1) * REC1], None).then_inc(S["given_scattered"].sem, 16)
                    pool.wait_ge(S["given_scattered"].sem, 16 * COLS * i + 16 * COLS)
                peeled(pool, LD // COLS, body)

        @block.scalar
        def _(act):
            act.wait_ge(S["ids_in"].sem, S["ids_in"].n + 48)

            def body(i, first):
                if not first:
                    act.wait_ge(S["rec_out"].sem, 48 * i)
                at = ds(i * CHUNK, CHUNK)
                for c, ids in enumerate((srcI, dstI, typI, typI)):
                    nc.scalar.activation(rec[:, :, c], ids[:, at], ACT.Copy).then_inc(S["rec_made"].sem, 1)
                act.wait_ge(S["attrs_in"].sem, S["attrs_in"].n + 16 * i + 16)
                nc.scalar.activation(rec[:, :, REC0:REC1], attr[:, :, :], ACT.Copy).then_inc(S["rec_made"].sem, 1)
            peeled(act, LD // CHUNK, body)

        @block.vector
        def _(v):
            step = Chain(v, S["vector_steps"])
            col = K["col"]
            v.wait_ge(S["ids_in"].sem, S["ids_in"].n + 48)
            step(nc.vector.memset(zeroW[:, :], 0.0))
            step(nc.vector.memset(ones, 1.0))
            step(nc.vector.tensor_single_scalar(posI[:, :], dstI[:, :], 7, ALU.arith_shift_right))
            step(nc.vector.tensor_copy(win, posI[:, :]))
            step(nc.vector.tensor_copy(lo[:, :], dstI[:, :]))
            step(nc.vector.scalar_tensor_tensor(lo[:, :], win, -float(P), lo[:, :], ALU.mult, ALU.add))
            step(nc.vector.tensor_copy(key[:, :], typI[:, :]))
            step(nc.vector.scalar_tensor_tensor(key[:, :], win, float(R), key[:, :], ALU.mult, ALU.add))
            count_windows(nc, v, step, win, mask, col, cnt, PD)
            nc.vector.tensor_copy(cum[:, 0:1], cnt[:, 0:1]).then_inc(S["window_counts"].sem, 1)
            v.wait_ge(S["prefix_ready"].sem, S["prefix_ready"].n + 1)
            step(nc.vector.tensor_copy(tot[:, 0, :], pref[:, 64:64 + NW]))
            step(nc.vector.tensor_copy(tot[:, 1, :], pref[:, 128:128 + NW]))
            step(nc.vector.tensor_scalar(base[:, :], pref[0:PD, 0:NW], -1.0, None, ALU.add))
            for h, first_row in ((0, 0), (1, HALF + GAP)):
                start = cum[:, 0:NW]
                step(nc.vector.tensor_tensor_scan(start, K["ones"][0:PD, 0:NW], tot[0:PD, h, :], float(first_row),
                                                  ALU.mult, ALU.add))
                step(nc.vector.tensor_tensor(start, start, tot[0:PD, h, :], ALU.subtract))
                step(nc.vector.scalar_tensor_tensor(base[:, :], start, K[f"half{h}"][0:PD, 0:1], base[:, :],
                                                    ALU.mult, ALU.add))
            step(nc.vector.memset(pos[:, :], 0.0))
            rank_edges(nc, v, step, win, ones, mask, cum, sel, col, base, pos[:, :], PD)
            step(nc.vector.tensor_copy(posI[:, :], pos[:, :]))
            v.wait_ge(S["iota_made"].sem, S["iota_made"].n + 1)
            step(nc.vector.tensor_scalar(sel, ones, K["half1"][0:PD, 0:1], float(GAP), ALU.mult, ALU.mult))
            step(nc.vector.tensor_tensor(sel, sel, place[:, :], ALU.add))
            step(nc.vector.tensor_tensor(sel, sel, pos[:, :], ALU.subtract))
            step(nc.vector.tensor_tensor(sel, sel, sel, ALU.mult))
            step(nc.vector.tensor_reduce(flag[:, 0:1], sel, AX.X, ALU.max))
            nc.vector.tensor_scalar(flag[:, 1:2], flag[:, 0:1], 0.5, None, ALU.is_gt).then_inc(S["moved"].sem, 1)
            v.wait_ge(S["moved_sum"].sem, 1)
            step(nc.vector.tensor_scalar(flag[0:1, 0:1], fps[0:1, 0:1], 1.0, None, ALU.min))
            nc.vector.tensor_copy(flagI[:, :], flag[0:1, 0:1]).then_inc(S["flag_made"].sem, 1)

            def onehot(to, parts, keys, value, t):
                shape = [parts, COLS, keys]
                return nc.vector.tensor_tensor(to, K["col_b"][0:parts, 0:keys].unsqueeze(1).to_broadcast(shape),
                                               value[:, ds(t, COLS)].unsqueeze(2).to_broadcast(shape), ALU.is_equal)

            def dst_body(i, first):
                for h in range(2):
                    turn = 2 * i + h
                    if not first:
                        v.wait_ge(S["counted"].sem, turn - 1)
                    onehot(ohl[0:PD, h, :, :], PD, P, lo, turn * COLS)
                    onehot(ohk[0:PD, h, :, :], PD, NKEY, key, turn * COLS).then_inc(S["onehots_made"].sem, 1)
            peeled(v, LD // COLS // 2, dst_body)

            def src_body(i, first):
                for h in range(2):
                    turn = 2 * i + h
                    v.wait_ge(S["counted"].sem, LD // COLS + turn - 1)
                    onehot(ohl[0:PS_, h, :, :], PS_, P, K["lo0"], turn * COLS)
                    onehot(ohk[0:PS_, h, :, 0:NW], PS_, NW, K["win0"], turn * COLS).then_inc(S["onehots_made"].sem, 1)
            peeled(v, LS // COLS // 2, src_body)

            step(nc.vector.memset(tab[:, :, :, :], 0.0))
            tile_table(nc, step, K, tmp, K["tot0"][:, :], T0, 0, E, tab[:, 0, :, :])
            for h in range(2):
                first_row = h * (HALF + GAP)
                tile_table(nc, step, K, tmp, tot[:, h, :], TH, first_row, first_row + HALF, tab[:, 1 + h, :, :])
            nc.vector.tensor_copy(tabI[:, :, :, :], tab[:, :, :, :]).then_inc(S["tables_made"].sem, 1)

            wide, rest = K["w1c_wide32"][:, :, :], wide_rest[:, :, :]
            parts = [wide_parts[:, i, :, :] for i in range(3)]
            step(nc.vector.tensor_copy(parts[0], wide))
            step(nc.vector.tensor_tensor(rest, wide, parts[0], ALU.subtract))
            step(nc.vector.tensor_copy(parts[1], rest))
            step(nc.vector.tensor_tensor(parts[2], rest, parts[1], ALU.subtract))
            step(nc.vector.tensor_scalar(is_term[:, 0:NT - 1], col[0:KA, 1:NT], float(2 * G0), None, ALU.mult))
            step(nc.vector.tensor_scalar(is_term[:, 0:NT - 1], is_term[:, 0:NT - 1], K["row"][0:KA, 0:1], None, ALU.is_le))
            step(nc.vector.tensor_reduce(term[:, :], is_term[:, 0:NT - 1], AX.X, ALU.add))
            step(nc.vector.tensor_scalar(is_term[:, :], col[0:KA, 0:NT], term[:, 0:1], None, ALU.is_equal))
            step(nc.vector.memset(takes[:, :], 0.0))
            for j, (_, part) in enumerate(TERMS):
                i = ("high", "middle", "low").index(part)
                step(nc.vector.tensor_tensor(takes[:, i:i + 1], takes[:, i:i + 1], is_term[:, j:j + 1], ALU.add))
            wide = K["w1c_wide"][:, :, :]
            step(nc.vector.tensor_scalar(wide, parts[0], takes[:, 0:1], None, ALU.mult))
            for i in (1, 2):
                step(nc.vector.scalar_tensor_tensor(wide, parts[i], takes[:, i:i + 1], wide, ALU.mult, ALU.add))

            v.wait_ge(S["counted"].sem, (LD + LS) // COLS)
            inv = K["inv_count"]
            step(nc.vector.tensor_copy(inv[:, :], cps[:, 0, 0:NKEY]))
            step(nc.vector.tensor_reduce(K["deg"][:, :], inv[:, :].rearrange("p (w r) -> p w r", r=R), AX.X, ALU.add))
            step(nc.vector.tensor_scalar(inv[:, :], inv[:, :], 1.0, None, ALU.max))
            step(nc.vector.reciprocal(inv[:, :], inv[:, :]))
            step(nc.vector.tensor_copy(rel_f[:, :], cps[:, 0, 256:256 + NKEY]))
            step(nc.vector.tensor_reduce(K["deg_f"][:, :], rel_f[:, :].rearrange("p (w r) -> p w r", r=R), AX.X, ALU.add))
            step(nc.vector.tensor_copy(K["out_deg"][:, :], cps[:, 1, 0:NW]))
            for i, (t, n) in enumerate((("PN", "out_deg"), ("QN", "deg"))):
                step(nc.vector.tensor_tensor(big[:, :, :], K[t][:, 0:NW, :], over_f(K[n][:, :], NW), ALU.mult))
                step(nc.vector.tensor_reduce(red[:, i, :], big[:, :, :].rearrange("p w f -> p f w"), AX.X, ALU.add))
            v.wait_ge(S["attr_summed"].sem, 1)
            step(nc.vector.tensor_copy(ea_b[:, :], fps[0:2, P:2 * P]))
            nc.vector.tensor_tensor(red[:, 0, :], red[:, 0, :], red[:, 1, :], ALU.add).then_inc(S["mean_parts"].sem, 1)
            v.wait_ge(S["mean_ready"].sem, 1)
            mean = red[:, 1, :]
            step(nc.vector.scalar_tensor_tensor(mean, mps[:, 0:F], 1.0 / E, K["b1"][:, :], ALU.mult, ALU.add))
            step(nc.vector.tensor_tensor(mean, K["b1"][:, :], mean, ALU.subtract))
            step(nc.vector.tensor_tensor(K["PN"][:, 0:NW, :], K["PN"][:, 0:NW, :], over_w(mean, NW), ALU.add))
            v.wait_ge(S["weight_turned"].sem, 1)
            step(nc.vector.tensor_copy(K["W_l1T"][:, :], fps[:, 2 * P:3 * P]))
            step.end()

        @block.tensor
        def _(pe):
            pe.wait_ge(S["window_counts"].sem, S["window_counts"].n + 1)
            nc.tensor.matmul(pref[0:PD, 0:NW], K["before_half"][0:PD, 0:PD], cnt[:, :], start=True, stop=True)
            nc.tensor.matmul(pref[:, 64:64 + NW], K["in_half0"][0:PD, :], cnt[:, :], start=True, stop=True)
            nc.tensor.matmul(pref[:, 128:128 + NW], K["in_half1"][0:PD, :], cnt[:, :], start=True, stop=True)                .then_inc(S["prefix_ready"].sem, 1)
            nc.tensor.transpose(fps[:, 2 * P:3 * P], K["W_l1"][:, :], K["ident"][:, :]).then_inc(S["weight_turned"].sem, 1)
            nc.tensor.matmul(fps[0:2, P:2 * P], K["ea2_sum"][:, :], K["ones"][0:PS_, :], start=True, stop=True)                .then_inc(S["attr_summed"].sem, 1)
            pe.wait_ge(S["moved"].sem, 1)
            nc.tensor.matmul(fps[0:1, 0:1], flag[:, 1:2], K["ones"][0:PD, 0:1], start=True, stop=True)                .then_inc(S["moved_sum"].sem, 1)
            for j in range(2):
                nc.tensor.matmul(cps[:, j, :], zeroW[:, 0:P], zeroW[:, :], start=True, stop=True)

            def dst_body(i, first):
                for h in range(2):
                    pe.wait_ge(S["onehots_made"].sem, 2 * i + h + 1)
                    for k in range(COLS):
                        nc.tensor.matmul(cps[:, 0, 0:NKEY], ohl[0:PD, h, k, :], ohk[0:PD, h, k, :], start=False,
                                         stop=True, skip_group_check=True)
                        last = nc.tensor.matmul(cps[:, 0, 256:256 + NKEY], ohl[0:PH, h, k, :], ohk[0:PH, h, k, :],
                                                start=False, stop=True, skip_group_check=True)
                    last.then_inc(S["counted"].sem, 1)
            peeled(pe, LD // COLS // 2, dst_body)

            def src_body(i, first):
                for h in range(2):
                    pe.wait_ge(S["onehots_made"].sem, LD // COLS + 2 * i + h + 1)
                    for k in range(COLS):
                        last = nc.tensor.matmul(cps[:, 1, 0:NW], ohl[0:PS_, h, k, :], ohk[0:PS_, h, k, 0:NW],
                                                start=False, stop=True, skip_group_check=True)
                    last.then_inc(S["counted"].sem, 1)
            peeled(pe, LS // COLS // 2, src_body)
            pe.wait_ge(S["mean_parts"].sem, 1)
            nc.tensor.matmul(mps[:, 0:F], K["ones"][:, :], red[:, 0, :], start=True, stop=False)
            nc.tensor.matmul(mps[:, 0:F], ea_b[:, :], K["W1c"][:, :], start=False, stop=True)                .then_inc(S["mean_ready"].sem, 1)
    passed(S, ids_in=48, window_counts=1, prefix_ready=1, attrs_in=16 * (LD // CHUNK), iota_made=1, mean_parts=1,
             mean_ready=1)


GROUPS = [(0, 4), (4, 7), (7, 10), (10, 13)]
NG = len(GROUPS)
PARTS = ((0, G0), (G0, B))
GATHERED = 16 * B
BANK7 = 7 * 512


def need(eng, signal, count, base=0):
    if isinstance(count, int) and count <= 0 and not (isinstance(base, int) and base + count > 0):
        return
    eng.wait_ge(signal.sem, signal.n + base + count)


def batches(eng, n_bodies, batch):
    def body(i, first):
        for h in range(2):
            batch(2 * i + h, h, i)
    peeled(eng, n_bodies, body)


def offsets(eng, tab, row, b, top):
    Memory.made += 1
    regs = [eng.alloc_register(name=f"tile_{Memory.made}_{u}") for u in range(B)]
    eng.load(regs, tab[row:row + 1, ds(b * BP, B)])
    return [eng.snap(r, donate=True, min_val=0, max_val=top) for r in regs]


def clear_acc(nc, K, psum):
    for c in range(0, ACC, 512):
        last = nc.tensor.matmul(psum[:, c:c + 512], K["zeros"][:, 0:P], K["zeros"][:, :], start=True, stop=True)
    return last


def layer_norm(nc, v, step, S, V, big, st, n):
    mean, var = st[:, 0, :], st[:, 1, :]
    step(nc.vector.tensor_reduce(mean, V, AX.X, ALU.add))
    step(nc.vector.tensor_scalar(mean, mean, 1.0 / F, None, ALU.mult))
    step(nc.vector.tensor_tensor(V, V, over_f(mean, NW), ALU.subtract))
    step(nc.vector.tensor_tensor(big, V, V, ALU.mult))
    step(nc.vector.tensor_reduce(var, big, AX.X, ALU.add))
    nc.vector.tensor_scalar(var, var, 1.0 / F, EPS, ALU.mult, ALU.add).then_inc(S["var_made"].sem, 1)
    v.wait_ge(S["root_made"].sem, S["root_made"].n + n + 1)
    step(nc.vector.reciprocal(var, var))
    step(nc.vector.tensor_tensor(V, V, over_f(var, NW), ALU.mult))


def root(nc, act, S, x, n):
    act.wait_ge(S["var_made"].sem, S["var_made"].n + n + 1)
    nc.scalar.activation(x, x, ACT.Sqrt).then_inc(S["root_made"].sem, 1)


def stage_edge_mlp(nc, S, top, d, K):
    with Memory(nc) as m:
        slots = m.sb("slots", [P, 2, 2 * G0, REC0])
        idx = m.sb("rows", [P, 2, B], I32)
        valid, row = m.sb("in_window", [P, 2 * G0]), m.sb("row", [P, B])
        oh = m.sb("onehot", [P, 2, B, P], BF16)
        ohT = m.sb("onehotT", [P, 2, 512])
        attr, rest = m.sb("attr", [P, 4 * G0]), m.sb("attr_rest", [P, 4 * G0])
        high, middle = m.sb("attr_high", [P, 4 * G0], BF16), m.sb("attr_middle", [P, 4 * G0], BF16)
        ea, eaT = m.sb("attr_terms", [P, 2, 2, NT, 2 * G0], BF16), m.sb("attr_termsT", [KA, 2, 2, P], BF16)
        q = m.sb("Q_rows", [P, 2, B, F])
        c = m.sb("c", [P, 2, B * F])
        sq = m.sb("c_squared", [P, 2, B * F])
        total = m.sb("squares_sum", [P, B * F])
        ps_t, ps_h = m.ps("psum_onehotT", [P, 2, 1024], BF16), m.ps("psum_h", [P, 2, 512])
        ps_e, ps_s = m.ps("psum_attrT", [P, 1024], BF16), m.ps("psum_squares", [P, 512])
        block = m.block()
        slots_in, gathered, stored = (S["slots_in0"], S["slots_in1"]), (S["gathered0"], S["gathered1"]), (S["c_stored0"], S["c_stored1"])
        bodies = T0 // BODY
        loc, tab = K["loc0"], K["tab0"]

        @block.sync
        def _(sp):
            def batch(b, h, i):
                off = offsets(sp, tab, 0, b, E)
                need(sp, S["attr_made"], b - 1)
                for u in range(B):
                    sp.dma_start(slots[:, h, u, :], d["rec0"][ds(off[u], P), :]).then_inc(slots_in[h].sem, 16)
            batches(sp, bodies, batch)

        @block.gpsimd
        def _(pool):
            def batch(b, h, i):
                need(pool, S["c_made"], NG * (b - 1))
                need(pool, S["batch_ready"], b + 1)
                pool.sem_inc(S["gather_go"].sem, 1)
                for u in range(B):
                    nc.gpsimd.indirect_dma_start(q[:, h, u, :], None, d["Q"][:, :],
                                                 bass.IndirectOffsetOnAxis(ap=idx[:, h, u:u + 1], axis=0))\
                        .then_inc(gathered[h].sem, 16)
            batches(pool, bodies, batch)

        @block.vector
        def _(v):
            step = Chain(v, S["vector_steps"])
            n0 = step.n

            def add(b, h, i):
                need(v, gathered[h], GATHERED * (i + 1))
                need(v, stored[h], 16 * i)
                for g, (s, e) in enumerate(GROUPS):
                    need(v, S["h_made"], NG * b + g + 1)
                    nc.vector.tensor_tensor(c[:, h, s * F:e * F], ps_h[:, g % 2, 0:(e - s) * F],
                                            q[:, h, s:e, :].rearrange("p t f -> p (t f)"), ALU.add)\
                        .then_inc(S["c_made"].sem, 1)

            def add_squares(b, h):
                need(v, S["squared"], b + 1)
                need(v, S["squares_added"], b)
                nc.vector.tensor_tensor(total[:, :], total[:, :], sq[:, h, :], ALU.add)\
                    .then_inc(S["squares_added"].sem, 1)

            def batch(b, h, i):
                step.n = n0 + b * 8
                at = ds(b * B, B)
                need(v, slots_in[h], GATHERED * (i + 1))
                need(v, gathered[h], GATHERED * i)
                need(v, S["attr_turned"], b - 1)
                step(nc.vector.tensor_tensor(loc[:, at], slots[:, h, 0:B, 0], loc[:, at], ALU.subtract))
                ok = valid[:, 0:B]
                step(nc.vector.tensor_scalar(ok, loc[:, at], 0.0, None, ALU.is_ge))
                step(nc.vector.scalar_tensor_tensor(ok, loc[:, at], float(P), ok, ALU.is_lt, ALU.mult))
                step(nc.vector.scalar_tensor_tensor(row[:, :], slots[:, h, 0:B, 1], 1.0 - NWP * P, ok,
                                                    ALU.add, ALU.mult))
                nc.vector.tensor_scalar(idx[:, h, :], row[:, :], NWP * P - 1.0, None, ALU.add)\
                    .then_inc(S["batch_ready"].sem, 1)
                step(nc.vector.tensor_tensor(attr[:, :].rearrange("p (t c) -> p t c", c=2), slots[:, h, :, 2:4],
                                             valid[:, :].unsqueeze(2).to_broadcast([P, 2 * G0, 2]), ALU.mult))
                step(nc.vector.tensor_copy(high[:, :], attr[:, :]))
                step(nc.vector.tensor_tensor(rest[:, :], attr[:, :], high[:, :], ALU.subtract))
                step(nc.vector.tensor_copy(middle[:, :], rest[:, :]))
                by_part = lambda x: x[:, :].rearrange("p (k c) -> p k c", k=2)
                nc.vector.tensor_tensor(ea[:, h, :, 5, :], by_part(rest), by_part(middle), ALU.subtract)
                for j in range(3):
                    nc.vector.tensor_copy(ea[:, h, :, j, :], by_part(high))
                nc.vector.tensor_copy(ea[:, h, :, 3, :], by_part(middle))
                nc.vector.tensor_copy(ea[:, h, :, 4, :], by_part(middle)).then_inc(S["attr_made"].sem, 1)
                for g, (s, e) in enumerate(GROUPS):
                    need(v, S["onehot_turned"], NG * (b - 2) + g + 1)
                    for u in range(s, e):
                        last = nc.vector.tensor_scalar(oh[:, h, u, :], K["col"][:, 0:P], loc[:, ds(b * B + u, 1)], None,
                                                       ALU.is_equal)
                    last.then_inc(S["onehot_made"].sem, 1)
                if h:
                    add(b - 1, 0, i)
                elif not isinstance(i, int):
                    add(b - 1, 1, i - 1)
                if not isinstance(i, int):
                    add_squares(b - 2, h)
            step(nc.vector.memset(total[:, :], 0.0))
            step(nc.vector.memset(valid[:, :], 0.0))
            step(nc.vector.memset(slots[:, :, B, :], 0.0))
            n0 = step.n
            batches(v, bodies, batch)
            last = 2 * bodies - 1
            add(last, 1, bodies - 1)
            add_squares(last - 1, 0)
            add_squares(last, 1)
            step.n = n0 + 8 * 2 * bodies
            v.wait_ge(S["squares_added"].sem, 2 * bodies)
            step(nc.vector.tensor_reduce(sq[:, 0, 0:F], total[:, :].rearrange("p (t f) -> p f t", f=F), AX.X, ALU.add))
            v.sem_inc(S["mean_parts"].sem, 1)
            v.wait_ge(S["mean_ready"].sem, S["mean_ready"].n + 1)
            var, scale = K["stat"][:, 0, :], K["scale"]
            step(nc.vector.tensor_scalar(K["one"][:, :], ps_s[:, 0:1], 1.0 / E, EPS, ALU.mult, ALU.add))
            nc.vector.tensor_scalar(var, K["ident"][:, :], K["one"][:, 0:1], None, ALU.mult)\
                .then_inc(S["var_made"].sem, 1)
            v.wait_ge(S["root_made"].sem, 1)
            step(nc.vector.reciprocal(scale[:, :], var))
            step(nc.vector.tensor_tensor(scale[:, :], scale[:, :], K["gamma0"][:, :], ALU.mult))
            step.end()

        @block.scalar
        def _(act):
            def batch(b, h, i):
                need(act, S["attr_turned"], b + 1)
                need(act, S["h_made"], NG * (b - 1))
                nc.scalar.activation(eaT[:, h, :, :], ps_e[0:KA, 0:2 * P].rearrange("k (g e) -> k g e", g=2), ACT.Copy).then_inc(S["attr_back"].sem, 1)
                for g, (s, e) in enumerate(GROUPS):
                    need(act, S["onehot_turned"], NG * b + g + 1)
                    need(act, S["h_made"], NG * b + g - 1)
                    nc.scalar.activation(ohT[:, g % 2, 0:(e - s) * P], ps_t[:, g % 2, 0:(e - s) * P], ACT.Copy)\
                        .then_inc(S["onehot_back"].sem, 1)
                need(act, S["c_made"], NG * (b + 1))
                need(act, S["squares_added"], b - 1)
                nc.scalar.activation(sq[:, h, :], c[:, h, :], ACT.Square).then_inc(S["squared"].sem, 1)
                act.dma_start(d["c"][ds(b, 1), :, :].rearrange("o p f -> (o p) f"), c[:, h, :])\
                    .then_inc(stored[h].sem, 16)
            batches(act, bodies, batch)
            for s in stored:
                act.wait_ge(s.sem, 16 * bodies)
            act.wait_ge(S["var_made"].sem, 1)
            act.wait_ge(S["std_parts"].sem, 1)
            nc.scalar.activation(K["stat"][:, 0, :], ps_s[:, P:2 * P], ACT.Sqrt).then_inc(S["root_made"].sem, 1)

        @block.tensor
        def _(pe):
            def turn(b, h, g):
                s, e = GROUPS[g]
                need(pe, S["onehot_made"], NG * b + g + 1)
                need(pe, S["onehot_back"], NG * b + g - 1)
                for u in range(s, e):
                    last = nc.tensor.transpose(ps_t[:, g % 2, (u - s) * P:(u - s + 1) * P], oh[:, h, u, :], K["ident_b"][:, :])
                last.then_inc(S["onehot_turned"].sem, 1)

            def batch(b, h, i):
                win = offsets(pe, tab, 1, b, (NW - 1) * P)
                turn(b, h, 0)
                need(pe, S["attr_made"], b + 1)
                need(pe, S["attr_back"], b)
                for k in range(2):
                    last = nc.tensor.transpose(ps_e[0:KA, k * P:(k + 1) * P], ea[:, h, k, :, :].rearrange("p j c -> p (j c)"),
                                               K["ident_b"][:, :])
                last.then_inc(S["attr_turned"].sem, 1)
                for g, (s, e) in enumerate(GROUPS):
                    if g + 1 < NG:
                        turn(b, h, g + 1)
                    need(pe, S["attr_back"], b + 1)
                    need(pe, S["onehot_back"], NG * b + g + 1)
                    need(pe, S["c_made"], NG * b + g - 1)
                    for u in range(s, e):
                        o = ps_h[:, g % 2, (u - s) * F:(u - s + 1) * F]
                        nc.tensor.matmul(o, ohT[:, g % 2, (u - s) * P:(u - s + 1) * P], K["PNf"][:, ds(win[u], F)],
                                         start=True, stop=False)
                        k = int(u >= G0)
                        last = nc.tensor.matmul(o, eaT[:, h, k, :], K["w1c_wide"][:, u - k * G0, :], start=False, stop=True)
                    last.then_inc(S["h_made"].sem, 1)
            batches(pe, bodies, batch)
            pe.wait_ge(S["mean_parts"].sem, S["mean_parts"].n + 1)
            nc.tensor.matmul(ps_s[:, 0:1], sq[:, 0, 0:F], K["ones"][:, 0:1], start=True, stop=True)\
                .then_inc(S["mean_ready"].sem, 1)
            pe.wait_ge(S["var_made"].sem, 1)
            pe.wait_ge(S["attr_back"].sem, 2 * bodies)
            nc.tensor.matmul(ps_s[:, P:2 * P], K["ones"][:, :], K["stat"][:, 0, :], start=True, stop=True)\
                .then_inc(S["std_parts"].sem, 1)
    n = 2 * bodies
    passed(S, batch_ready=n, attr_made=n, mean_parts=1, mean_ready=1, slots_in0=GATHERED * bodies, slots_in1=GATHERED * bodies,
             gathered0=GATHERED * bodies, gathered1=GATHERED * bodies, c_made=NG * n, onehot_made=NG * n,
             onehot_turned=NG * n, onehot_back=NG * n, h_made=NG * n, attr_turned=n, attr_back=n, var_made=1, root_made=1)


def stage_edge_sum(nc, S, top, d, K):
    with Memory(nc) as m:
        c = m.sb("c_in", [P, 2, B, F])
        t = m.sb("normed", [P, 2, B, F])
        msg = m.sb("messages", [P, 2, B, F])
        oh = m.sb("onehot", [P, 2, B, P])
        acc = m.ps("acc", [P, 4096])
        block = m.block()
        c_in = (S["c_in0"], S["c_in1"])
        bodies = T0 // BODY

        @block.sync
        def _(sp):
            def batch(b, h, i):
                need(sp, S["scaled"], b - 1)
                sp.dma_start(c[:, h, :, :].rearrange("p t f -> p (t f)"),
                             d["c"][ds(b, 1), :, :].rearrange("o p f -> (o p) f")).then_inc(c_in[h].sem, 16)
            batches(sp, bodies, batch)

        @block.gpsimd
        def _(pool):
            def batch(b, h, i):
                need(pool, S["scaled"], b + 1)
                nc.gpsimd.tensor_tensor(t[:, h, :, :], t[:, h, :, :], over_w(K["beta0"][:, :], B), ALU.add)\
                    .then_inc(S["shifted"].sem, 1)
            batches(pool, bodies, batch)

        @block.vector
        def _(v):
            def onehot(b, h):
                need(v, S["summed"], b - 1)
                nc.vector.tensor_tensor(oh[:, h, :, :], K["col"][:, 0:P].unsqueeze(1).to_broadcast([P, B, P]),
                                        K["loc0"][:, ds(b * B, B)].unsqueeze(2).to_broadcast([P, B, P]),
                                        ALU.is_equal).then_inc(S["onehot_made"].sem, 1)

            def batch(b, h, i):
                need(v, c_in[h], 16 * (i + 1))
                need(v, S["messages_made"], b - 1)
                nc.vector.tensor_tensor(t[:, h, :, :], c[:, h, :, :], over_w(K["scale"][:, :], B), ALU.mult)\
                    .then_inc(S["scaled"].sem, 1)
                if h or not isinstance(i, int):
                    onehot(b - 1, 1 - h)
            batches(v, bodies, batch)
            onehot(2 * bodies - 1, 1)
            nc.vector.memset(K["ST"][:, ACC:], 0.0)
            v.wait_ge(S["summed"].sem, S["summed"].n + 2 * bodies)
            nc.vector.tensor_copy(K["ST"][:, 0:ACC // 2], acc[:, 0:ACC // 2])
            nc.vector.tensor_copy(K["ST"][:, ACC // 2:ACC], acc[:, ACC // 2:ACC])

        @block.scalar
        def _(act):
            def batch(b, h, i):
                need(act, S["shifted"], b + 1)
                need(act, S["summed"], b - 1)
                nc.scalar.activation(msg[:, h, :, :], t[:, h, :, :], ACT.Relu).then_inc(S["messages_made"].sem, 1)
            batches(act, bodies, batch)

        @block.tensor
        def _(pe):
            clear_acc(nc, K, acc)

            def batch(b, h, i):
                win = offsets(pe, K["tab0"], 1, b, (NW - 1) * P)
                need(pe, S["onehot_made"], b + 1)
                need(pe, S["messages_made"], b + 1)
                for u in range(B):
                    last = nc.tensor.matmul(acc[:, ds(win[u], P)], msg[:, h, u, :], oh[:, h, u, :], start=False,
                                            stop=True, skip_group_check=True)
                last.then_inc(S["summed"].sem, 1)
            batches(pe, bodies, batch)
    n = 2 * bodies
    passed(S, messages_made=n, summed=n, onehot_made=n)


def stage_nodes0(nc, S, top, d, K):
    with Memory(nc) as m:
        big, st = m.sb("node_work", [P, NW, F]), m.sb("node_stats", [P, 2, NW])
        W2, b2 = m.sb("W2", [P, F]), m.sb("b2", [P, F])
        rdeg = m.sb("rdeg", [P, NW])
        Y = m.sb("Y0", [P, NWP, F])
        p_sum = Projection(nc, m, S, "p1", F, transposed=True)
        p_tab = Projection(nc, m, S, "p2", F, y_cols=F, py=p_sum.py)
        block = m.block()
        X = K["X"][:, 0:NW, :]
        outs = [(slice(0, F), win_of(Y), None)]
        scale = lambda w: K["dinv"][:, ds(w, 1)]
        outs_tab = [(slice(0, F), win_of(K["H"]), scale), (slice(0, F), None, scale)]

        @block.sync
        def _(sp):
            sp.dma_start(W2[:, :], d["L0_gnn_W2"]).then_inc(S["weights_in"].sem, 16)
            sp.dma_start(b2[:, :], d["L0_gnn_b2"].rearrange("(o f) -> o f", o=1).to_broadcast([P, F]))\
                .then_inc(S["weights_in"].sem, 16)
            passed(S, p_back=NWP, p_made=NWP, p_taken=NWP)
            p_tab.sync(sp, d["H"], 2)
            passed(S, p_back=-NWP, p_made=-NWP, p_taken=-NWP)

        @block.scalar
        def _(act):
            root(nc, act, S, K["dinv"][:, 0:NW], 0)
            p_sum.scalar(act, lambda w: K["STf"][:, ds(w * P, P)].unsqueeze(1), outs)
            root(nc, act, S, st[:, 1, :], 1)
            act.wait_ge(S["nodes_made"].sem, S["nodes_made"].n + 1)
            passed(S, p_back=NWP, p_made=NWP, p_taken=NWP)
            p_tab.scalar(act, win_of(K["X"]), outs_tab)
            passed(S, p_back=-NWP, p_made=-NWP, p_taken=-NWP)

        @block.tensor
        def _(pe):
            pe.wait_ge(S["weights_in"].sem, S["weights_in"].n + 32)
            p_sum.tensor(pe, None, lambda c, e: W2[:, :], 1)
            passed(S, p_back=NWP, p_made=NWP, p_taken=NWP)
            p_tab.tensor(pe, K["ident"], lambda c, e: K["W_l1T"][:, :], 2)
            passed(S, p_back=-NWP, p_made=-NWP, p_taken=-NWP)

        @block.vector
        def _(v):
            step = Chain(v, S["vector_steps"])
            v.wait_ge(S["weights_in"].sem, S["weights_in"].n + 32)
            step(nc.vector.memset(K["dinv"][:, :], 1.0))
            nc.vector.tensor_scalar(K["dinv"][:, 0:NW], K["deg"][:, :], 1.0, None, ALU.add).then_inc(S["var_made"].sem, 1)
            v.wait_ge(S["root_made"].sem, S["root_made"].n + 1)
            step(nc.vector.reciprocal(K["dinv"][:, 0:NW], K["dinv"][:, 0:NW]))
            step(nc.vector.tensor_scalar(rdeg[:, :], K["out_deg"][:, :], 1.0, None, ALU.add))
            step(nc.vector.reciprocal(rdeg[:, :], rdeg[:, :]))
            step(nc.vector.tensor_tensor(big[:, :, :], over_f(K["out_deg"][:, :], NW), over_w(b2[:, :], NW), ALU.mult))
            v.wait_ge(S["p_taken"].sem, S["p_taken"].n + NWP)
            step(nc.vector.tensor_tensor(big[:, :, :], big[:, :, :], Y[:, 0:NW, :], ALU.add))
            step(nc.vector.tensor_tensor(big[:, :, :], big[:, :, :], over_f(rdeg[:, :], NW), ALU.mult))
            step(nc.vector.scalar_tensor_tensor(X, X, 2.0, big[:, :, :], ALU.mult, ALU.add))
            layer_norm(nc, v, step, S, X, big[:, :, :], st, 1)
            v.sem_inc(S["nodes_made"].sem, 1)
            step.end()
    p_sum.passed(1)
    p_tab.passed(2)
    passed(S, weights_in=32, var_made=2, root_made=2, nodes_made=1)


def stage_gcn(nc, S, top, d, K):
    with Memory(nc) as m:
        idx = m.sb("rows", [P, 2, B], I32)
        oh = m.sb("onehot", [P, 2, B, P])
        ohb = m.sb("onehot_bf", [P, 2, B, P], BF16)
        ohT = m.sb("onehotT", [P, G0 * P])
        rows = m.sb("H_rows", [P, 2, B, F])
        inv = m.sb("inv_rows", [P, 2, B, R])
        rel = m.sb("onehot_relation", [P, B, R])
        acc = m.ps("acc", [P, 4096])
        ps_t, ps_r = acc[:, BANK7:BANK7 + G0 * P // 2].bitcast(BF16), acc[:, BANK7 + G0 * P // 2:BANK7 + G0 * (P // 2 + R)]
        block = m.block()
        slots_in, gathered = (S["slots_in0"], S["slots_in1"]), (S["gathered2"], S["gathered3"])
        bodies, n = T1 // BODY, 2 * (T1 // BODY)
        slots, loc, tab = K["slots1"], K["loc1"], K["tab1"]

        @block.sync
        def _(sp):
            def batch(b, h, i):
                off = offsets(sp, tab, 0, b, E + GAP)
                need(sp, slots_in[h], GATHERED * i)
                for u in range(B):
                    sp.dma_start(slots[:, ds(b * B + u, 1), :].rearrange("p o c -> p (o c)"),
                                 d["rec1"][ds(off[u], P), 0:REC0]).then_inc(slots_in[h].sem, 16)
            batches(sp, bodies, batch)

        @block.gpsimd
        def _(pool):
            def batch(b, h, i):
                need(pool, S["batch_ready"], b + 1)
                for g, (s, e) in enumerate(PARTS):
                    need(pool, S["summed"], 2 * b - 3 + g)
                    pool.sem_inc(S["gather_go"].sem, 1)
                    for u in range(s, e):
                        nc.gpsimd.indirect_dma_start(rows[:, h, u, :], None, d["H"][:, :],
                                                     bass.IndirectOffsetOnAxis(ap=idx[:, h, u:u + 1], axis=0))\
                            .then_inc(gathered[h].sem, 16)
            batches(pool, bodies, batch)

        @block.vector
        def _(v):
            step = Chain(v, S["vector_steps"])
            n0 = step.n

            def weights(b, h):
                need(v, S["inv_back"], 2 * (b + 1))
                at = ds(b * B, B)
                step(nc.vector.tensor_tensor(rel[:, :, :], K["col"][:, 0:R].unsqueeze(1).to_broadcast([P, B, R]),
                                             slots[:, at, 2:3].to_broadcast([P, B, R]), ALU.is_equal))
                step(nc.vector.tensor_tensor(rel[:, :, :], rel[:, :, :], inv[:, h, :, :], ALU.mult))
                step(nc.vector.tensor_reduce(K["weight"][:, at], rel[:, :, :], AX.X, ALU.add))

            def batch(b, h, i):
                first = isinstance(i, int)
                step.n = n0 + b if first else n0 + 2 + 4 * (b - 2)
                at = ds(b * B, B)
                need(v, slots_in[h], GATHERED * (i + 1))
                need(v, gathered[h], GATHERED * i)
                nc.vector.tensor_copy(idx[:, h, :], slots[:, at, 0])
                step(nc.vector.tensor_tensor(loc[:, at], slots[:, at, 1], loc[:, at], ALU.subtract))
                v.sem_inc(S["batch_ready"].sem, 1)
                if not first:
                    weights(b - 2, h)
                need(v, S["summed"], 2 * (b - 1))
                for u in range(B):
                    nc.vector.tensor_scalar(ohb[:, h, u, :], K["col_b"][:, 0:P], loc[:, ds(b * B + u, 1)], None,
                                            ALU.is_equal)
                for u in range(B):
                    last = nc.vector.tensor_scalar(oh[:, h, u, :], K["col"][:, 0:P], loc[:, ds(b * B + u, 1)], None,
                                                   ALU.is_equal)
                last.then_inc(S["onehot_made"].sem, 1)
            batches(v, bodies, batch)
            step.n = n0 + 2 + 4 * (n - 2)
            weights(n - 2, 0)
            weights(n - 1, 1)
            v.wait_ge(S["summed"].sem, S["summed"].n + 2 * n)
            step(nc.vector.tensor_copy(K["ACC"][:, 0:ACC], acc[:, 0:ACC]))
            step.end()

        @block.scalar
        def _(act):
            def batch(b, h, i):
                for g, (s, e) in enumerate(PARTS):
                    need(act, S["onehot_turned"], 2 * b + g + 1)
                    nc.scalar.activation(ohT[:, 0:(e - s) * P], ps_t[:, 0:(e - s) * P], ACT.Copy)\
                        .then_inc(S["onehot_back"].sem, 1)
                    need(act, S["inv_picked"], 2 * b + g + 1)
                    nc.scalar.activation(inv[:, h, s:e, :].rearrange("p t r -> p (t r)"), ps_r[:, 0:(e - s) * R],
                                         ACT.Copy).then_inc(S["inv_back"].sem, 1)
            batches(act, bodies, batch)

        @block.tensor
        def _(pe):
            clear_acc(nc, K, acc)

            def batch(b, h, i):
                win = offsets(pe, tab, 1, b, (NW - 1) * P)
                win_r = offsets(pe, tab, 2, b, (NW - 1) * R)

                def add(u):
                    return nc.tensor.matmul(acc[:, ds(win[u], F)], oh[:, h, u, :], rows[:, h, u, :], start=False,
                                            stop=True, skip_group_check=True)
                need(pe, S["onehot_made"], b + 1)
                need(pe, gathered[h], GATHERED * (i + 1))
                for g, (s, e) in enumerate(PARTS):
                    need(pe, S["inv_back"], 2 * b + g)
                    for u in range(s, e):
                        last = nc.tensor.transpose(ps_t[:, (u - s) * P:(u - s + 1) * P], ohb[:, h, u, :],
                                                   K["ident_b"][:, :])
                    last.then_inc(S["onehot_turned"].sem, 1)
                    for u in range(s, e - 3):
                        add(u)
                    need(pe, S["onehot_back"], 2 * b + g + 1)
                    for u in range(s, e):
                        last = nc.tensor.matmul(ps_r[:, (u - s) * R:(u - s + 1) * R], ohT[:, (u - s) * P:(u - s + 1) * P],
                                                K["inv_count"][:, ds(win_r[u], R)], start=True, stop=True)
                    last.then_inc(S["inv_picked"].sem, 1)
                    for u in range(e - 3, e):
                        last = add(u)
                    last.then_inc(S["summed"].sem, 1)
            batches(pe, bodies, batch)
    passed(S, slots_in0=GATHERED * bodies, slots_in1=GATHERED * bodies, batch_ready=n, onehot_made=n, summed=2 * n,
             onehot_turned=2 * n, onehot_back=2 * n)


def stage_nodes1(nc, S, top, d, K):
    with Memory(nc) as m:
        big, st = m.sb("node_work", [P, NW, F]), m.sb("node_stats", [P, 2, NW])
        rows = m.sb("rows_l1", [P, 3, F])
        part = m.sb("part_sums", [P, 2, F])
        ps = m.ps("node_psum", [P, 2, 512])
        block = m.block()
        X, V = K["X"][:, 0:NW, :], K["ACC"].rearrange("p (w f) -> p w f", f=F)
        b, gamma, beta = (rows[:, i, :] for i in range(3))
        dinv = over_f(K["dinv"][:, 0:NW], NW)

        @block.sync
        def _(sp):
            for i, n in enumerate(("L1_gnn_b", "L1_gnn_gamma", "L1_gnn_beta")):
                sp.dma_start(rows[:, i, :], d[n].rearrange("(o f) -> o f", o=1).to_broadcast([P, F]))\
                    .then_inc(S["weights_in"].sem, 16)

        @block.vector
        def _(v):
            step = Chain(v, S["vector_steps"])
            step(nc.vector.tensor_tensor(V, V, K["H"][:, 0:NW, :], ALU.add))
            step(nc.vector.tensor_tensor(V, V, dinv, ALU.mult))
            v.wait_ge(S["weights_in"].sem, S["weights_in"].n + 48)
            step(nc.vector.tensor_tensor(V, V, over_w(b, NW), ALU.add))
            step(nc.vector.tensor_scalar(K["ACC"][:, :], K["ACC"][:, :], 0.0, None, ALU.max))
            step(nc.vector.tensor_tensor(V, V, over_f(K["valid"][:, :], NW), ALU.mult))
            nc.vector.tensor_reduce(part[:, 0, :], V.rearrange("p w f -> p f w"), AX.X, ALU.add)\
                .then_inc(S["mean_parts"].sem, 1)
            v.wait_ge(S["mean_ready"].sem, S["mean_ready"].n + 1)
            step(nc.vector.tensor_scalar(part[:, 0, :], ps[:, 0, 0:F], 1.0 / N, None, ALU.mult))
            step(nc.vector.tensor_tensor(V, V, over_w(part[:, 0, :], NW), ALU.subtract))
            step(nc.vector.tensor_tensor(big[:, :, :], V, over_f(K["valid"][:, :], NW), ALU.mult))
            step(nc.vector.tensor_tensor(big[:, :, :], big[:, :, :], big[:, :, :], ALU.mult))
            nc.vector.tensor_reduce(part[:, 1, :], big[:, :, :].rearrange("p w f -> p f w"), AX.X, ALU.add)\
                .then_inc(S["mean_parts"].sem, 1)
            v.wait_ge(S["mean_ready"].sem, S["mean_ready"].n + 2)
            nc.vector.tensor_scalar(part[:, 1, :], ps[:, 1, 0:F], 1.0 / N, EPS, ALU.mult, ALU.add)\
                .then_inc(S["var_made"].sem, 1)
            v.wait_ge(S["root_made"].sem, S["root_made"].n + 1)
            step(nc.vector.reciprocal(part[:, 1, :], part[:, 1, :]))
            step(nc.vector.tensor_tensor(part[:, 1, :], part[:, 1, :], gamma, ALU.mult))
            step(nc.vector.tensor_tensor(V, V, over_w(part[:, 1, :], NW), ALU.mult))
            step(nc.vector.tensor_tensor(V, V, over_w(beta, NW), ALU.add))
            step(nc.vector.tensor_tensor(X, X, V, ALU.add))
            layer_norm(nc, v, step, S, X, big[:, :, :], st, 1)
            step.end()

        @block.tensor
        def _(pe):
            for i in range(2):
                pe.wait_ge(S["mean_parts"].sem, S["mean_parts"].n + i + 1)
                nc.tensor.matmul(ps[:, i, 0:F], K["ones"][:, :], part[:, i, :], start=True, stop=True)\
                    .then_inc(S["mean_ready"].sem, 1)

        @block.scalar
        def _(act):
            root(nc, act, S, part[:, 1, :], 0)
            root(nc, act, S, st[:, 1, :], 1)
    passed(S, weights_in=48, mean_parts=2, mean_ready=2, var_made=2, root_made=2)


def stage_rgcn(nc, S, top, d, K):
    L, C = 3, R * F + F
    with Memory(nc) as m:
        W = m.sb("W_relations", [P, L, C])
        bias = m.sb("bias_l2", [P, L, F])
        floor = m.sb("floor", [P, L])
        U, UT = m.sb("U", [P, NWP, F]), m.sb("UT", [P, NWP, F])
        big = m.sb("node_work", [P, NW, F])
        idx = m.sb("rows", [P, 2, B], I32)
        oh = m.sb("onehot", [P, 2, B, P])
        rows = m.sb("Y_rows", [P, 2, B, F])
        st = m.sb("node_stats", [P, 2, NW])
        ps = m.ps("acc", [P, 4096])
        proj = Projection(nc, m, S, "p3", R * F, y_cols=R * F, py="later", pt="later", keep=UT)
        proj.py = ps[:, 0:2048].rearrange("p (k c) -> p k c", k=2)
        proj.pt = ps[:, 3072:4096].rearrange("p (k c) -> p k c", k=2)
        block = m.block()
        gathered = (S["gathered4"], S["gathered5"])
        bodies, n = T1 // BODY, 2 * (T1 // BODY)
        slots, loc, tab = K["slots1"], K["loc1"], K["tab1"]
        outs = [(slice(0, R * F), None, None)]
        table = d["Y"].rearrange("n (r f) -> (n r) f", r=R)
        U25 = U[:, 0:NW, :]

        @block.sync
        def _(sp):
            for l in range(L):
                w, r, b = (d[f"L2_gnn_{x}{l + 1}"] for x in ("W", "root", "b"))
                sp.dma_start(W[:, l, 0:R * F].rearrange("f (r h) -> f r h", r=R), w.rearrange("r f h -> f r h"))\
                    .then_inc(S["weights_in"].sem, 16)
                sp.dma_start(W[:, l, R * F:C], r).then_inc(S["weights_in"].sem, 16)
                sp.dma_start(bias[:, l, :], b.rearrange("(o f) -> o f", o=1).to_broadcast([P, F]))\
                    .then_inc(S["weights_in"].sem, 16)
            with sp.Fori(0, L) as l:
                proj.sync(sp, d["Y"], 1, l)
                sp.sem_inc(S["table_stored"].sem, 1)

        @block.scalar
        def _(act):
            with act.Fori(0, L) as l:
                act.wait_ge(S["nodes_made"].sem, S["nodes_made"].n + l + 1)
                proj.scalar(act, win_of(U), outs, l)
            root(nc, act, S, st[:, 1, :], 0)

        @block.gpsimd
        def _(pool):
            with pool.Fori(0, L) as l:
                pool.wait_ge(S["table_stored"].sem, l + 1)

                def batch(b, h, i):
                    need(pool, S["summed"], b - 1, l * n)
                    need(pool, S["batch_ready"], b + 1, l * n)
                    pool.sem_inc(S["gather_go"].sem, 1)
                    for u in range(B):
                        nc.gpsimd.indirect_dma_start(rows[:, h, u, :], None, table,
                                                     bass.IndirectOffsetOnAxis(ap=idx[:, h, u:u + 1], axis=0))\
                            .then_inc(gathered[h].sem, 16)
                batches(pool, bodies, batch)

        @block.vector
        def _(v):
            step = Chain(v, S["vector_steps"])
            step(nc.vector.memset(floor[:, :], 0.0))
            step(nc.vector.memset(floor[:, L - 1:L], NEG))
            step(nc.vector.tensor_copy(U[:, :, :], K["X"][:, :, :]))
            v.sem_inc(S["nodes_made"].sem, 1)
            v.wait_ge(S["weights_in"].sem, S["weights_in"].n + 48 * L)
            n0, per_layer = step.n, 2
            with v.Fori(0, L) as l:
                def batch(b, h, i):
                    at = ds(b * B, B)
                    need(v, gathered[h], GATHERED * i, l * (GATHERED * bodies))
                    nc.vector.scalar_tensor_tensor(idx[:, h, :], slots[:, at, 0], float(R), slots[:, at, 2],
                                                   ALU.mult, ALU.add).then_inc(S["batch_ready"].sem, 1)
                    need(v, S["summed"], b - 1, l * n)
                    for u in range(B):
                        t = ds(b * B + u, 1)
                        last = nc.vector.tensor_scalar(oh[:, h, u, :], K["col"][:, 0:P], loc[:, t], K["weight"][:, t],
                                                       ALU.is_equal, ALU.mult)
                    last.then_inc(S["onehot_made"].sem, 1)
                batches(v, bodies, batch)
                step.n = n0 + l * per_layer
                v.wait_ge(S["summed"].sem, S["summed"].n + l * n + n)
                accs = ps[:, 0:ACC].rearrange("p (w f) -> p w f", f=F)
                step(nc.vector.tensor_tensor(U25, accs, bias[:, ds(l, 1), :].to_broadcast([P, NW, F]), ALU.add))
                step(nc.vector.tensor_scalar(U25, U25, floor[:, ds(l, 1)], None, ALU.max))
                v.sem_inc(S["nodes_made"].sem, 1)
            step.n = n0 + L * per_layer
            X = K["X"][:, 0:NW, :]
            step(nc.vector.tensor_tensor(X, X, U25, ALU.add))
            layer_norm(nc, v, step, S, X, big[:, :, :], st, 0)
            step.end()

        @block.tensor
        def _(pe):
            pe.wait_ge(S["weights_in"].sem, S["weights_in"].n + 48 * L)
            with pe.Fori(0, L) as l:
                proj.tensor(pe, K["ident"], lambda c, e: W[:, ds(l, 1), c:e].rearrange("p o c -> p (o c)"), 1, l)
                pe.wait_ge(S["p_taken"].sem, S["p_taken"].n + (l + 1) * NWP)
                clear_acc(nc, K, ps)
                for w in range(NW):
                    nc.tensor.matmul(ps[:, w * F:(w + 1) * F], UT[:, w, :],
                                     W[:, ds(l, 1), R * F:C].rearrange("p o c -> p (o c)"), start=False, stop=True,
                                     skip_group_check=True)

                def batch(b, h, i):
                    win = offsets(pe, tab, 1, b, (NW - 1) * P)
                    need(pe, S["onehot_made"], b + 1, l * n)
                    need(pe, gathered[h], GATHERED * (i + 1), l * (GATHERED * bodies))
                    for u in range(B):
                        last = nc.tensor.matmul(ps[:, ds(win[u], F)], oh[:, h, u, :], rows[:, h, u, :], start=False,
                                                stop=True, skip_group_check=True)
                    last.then_inc(S["summed"].sem, 1)
                batches(pe, bodies, batch)
    proj.passed(1, L)
    passed(S, weights_in=48 * L, batch_ready=L * n, onehot_made=L * n, summed=L * n, nodes_made=L + 1, var_made=1,
             root_made=1)


def stage_table3(nc, S, top, d, K):
    with Memory(nc) as m:
        W, Wr = m.sb("W1fb", [P, 2 * F]), m.sb("W1req", [EAD, 2 * F])
        b1, req = m.sb("b1fb", [P, 2 * F]), m.sb("req", [EAD, P])
        const = m.sb("const_fb", [P, 2 * F])
        pc = m.ps("const_psum", [P, 512])
        proj = Projection(nc, m, S, "p4", 2 * F, y_cols=2 * F)
        block = m.block()
        loads = [(W[:, i * F:(i + 1) * F], d[f"L3_gnn_W1{x}"][0:F, :]) for i, x in enumerate("fb")]
        loads += [(Wr[:, i * F:(i + 1) * F], d[f"L3_gnn_W1{x}"][F + EAD:, :]) for i, x in enumerate("fb")]
        loads += [(b1[:, i * F:(i + 1) * F], d[f"L3_gnn_b1{x}"].rearrange("(o f) -> o f", o=1).to_broadcast([P, F]))
                  for i, x in enumerate("fb")]
        loads += [(K["one"][0:EAD, 0:1], d["L3_gnn_req_emb"].rearrange("o c -> c o"))]
        wide = K["w1e_wide"]
        wide_loads = [(wide[EAD * j:EAD * (j + 1), i, j, :], d[f"L3_gnn_W1{x}"][F:F + EAD, :])
                      for i, x in enumerate("fb") for j in range(G0)]

        @block.sync
        def _(sp):
            for dst, src in loads:
                sp.dma_start(dst, src).then_inc(S["weights_in"].sem, 16)
            sp.wait_ge(S["zeroed"].sem, S["zeroed"].n + 1)
            for dst, src in wide_loads:
                sp.dma_start(dst, src).then_inc(S["wide_in"].sem, 16)
            proj.sync(sp, d["T3"], 1)
            sp.wait_ge(S["wide_in"].sem, 16 * len(wide_loads))

        @block.gpsimd
        def _(pool):
            nc.gpsimd.memset(wide[:, :, :, :], 0.0).then_inc(S["zeroed"].sem, 1)

        @block.vector
        def _(v):
            step = Chain(v, S["vector_steps"])
            v.wait_ge(S["weights_in"].sem, S["weights_in"].n + 16 * len(loads))
            nc.vector.tensor_scalar(req[:, :], K["ones"][0:EAD, :], K["one"][0:EAD, 0:1], None, ALU.mult)\
                .then_inc(S["req_made"].sem, 1)
            v.wait_ge(S["const_ready"].sem, 1)
            nc.vector.tensor_tensor(const[:, :], pc[:, 0:2 * F], b1[:, :], ALU.add).then_inc(S["const_made"].sem, 1)
            step.end()
        @block.tensor
        def _(pe):
            pe.wait_ge(S["req_made"].sem, 1)
            nc.tensor.matmul(pc[:, 0:2 * F], req[:, :], Wr[:, :], start=True, stop=True).then_inc(S["const_ready"].sem, 1)
            pe.wait_ge(S["const_made"].sem, 1)
            proj.tensor(pe, K["ident"], lambda c, e: W[:, :], 1, extra=(K["ones"][0:1, :], const[0:1, :]))

        @block.scalar
        def _(act):
            proj.scalar(act, win_of(K["X"]), [(slice(0, 2 * F), None, None)])
    proj.passed(1)
    passed(S, weights_in=16 * len(loads), zeroed=1)


def stage_directional(nc, S, top, d, K):
    with Memory(nc) as m:
        attr = m.sb("attr", [P, 2, B, EAD])
        attrT = m.sb("attrT", [P, 2, 2, P])
        idx = m.sb("rows", [P, 2, B], I32)
        oh = m.sb("onehot", [P, 2, B, P])
        rows = m.sb("T3_rows", [P, 2, B, F])
        msg = m.sb("messages", [P, 2, B, F])
        acc = m.ps("acc", [P, 4096])
        block = m.block()
        attr_in, gathered = (S["slots_in0"], S["slots_in1"]), (S["gathered6"], S["gathered7"])
        bodies, n = TH // BODY, 2 * (TH // BODY)
        slots, loc, tab = K["slots1"], K["loc1"], K["tab1"]
        bank = acc[:, BANK7:BANK7 + 512]
        table = d["T3"].rearrange("n (k f) -> (n k) f", k=2)

        @block.sync
        def _(sp):
            for half in range(2):
                def batch(b, h, i):
                    off = offsets(sp, tab, 0, half * (TH // B) + b, E + GAP)
                    need(sp, S["attr_turned"], b - 1, half * n)
                    for u in range(B):
                        sp.dma_start(attr[:, h, u, :], d["rec1"][ds(off[u], P), REC0:REC1]).then_inc(attr_in[h].sem, 16)
                batches(sp, bodies, batch)

        @block.gpsimd
        def _(pool):
            for half in range(2):
                def batch(b, h, i):
                    need(pool, S["c_made"], NG * (b - 1), half * NG * n)
                    need(pool, S["batch_ready"], b + 1, half * n)
                    pool.sem_inc(S["gather_go"].sem, 1)
                    for u in range(B):
                        nc.gpsimd.indirect_dma_start(rows[:, h, u, :], None, table,
                                                     bass.IndirectOffsetOnAxis(ap=idx[:, h, u:u + 1], axis=0))\
                            .then_inc(gathered[h].sem, 16)
                batches(pool, bodies, batch)

        @block.vector
        def _(v):
            for half in range(2):
                nc.vector.memset(K["STf" if half == 0 else "STb"][:, ACC:], 0.0)

                def add(b, h, i):
                    need(v, gathered[h], GATHERED * (i + 1), half * GATHERED * bodies)
                    need(v, S["summed"], b - 1, half * n)
                    for g, (s, e) in enumerate(GROUPS):
                        need(v, S["h_made"], NG * b + g + 1, half * NG * n)
                        nc.vector.tensor_tensor(msg[:, h, s:e, :].rearrange("p t f -> p (t f)"),
                                                bank[:, 0:(e - s) * F],
                                                rows[:, h, s:e, :].rearrange("p t f -> p (t f)"), ALU.add)\
                            .then_inc(S["c_made"].sem, 1)

                def batch(b, h, i):
                    at = ds(half * TH + b * B, B)
                    need(v, gathered[h], GATHERED * i, half * GATHERED * bodies)
                    nc.vector.tensor_scalar(idx[:, h, :], slots[:, at, 0], 2.0, float(half), ALU.mult, ALU.add)\
                        .then_inc(S["batch_ready"].sem, 1)
                    if h:
                        add(b - 1, 0, i)
                    elif not isinstance(i, int):
                        add(b - 1, 1, i - 1)
                    need(v, S["summed"], b - 1, half * n)
                    for u in range(B):
                        last = nc.vector.tensor_scalar(oh[:, h, u, :], K["col"][:, 0:P],
                                                       loc[:, ds(half * TH + b * B + u, 1)], None, ALU.is_equal)
                    last.then_inc(S["onehot_made"].sem, 1)
                batches(v, bodies, batch)
                add(n - 1, 1, bodies - 1)
                v.wait_ge(S["summed"].sem, S["summed"].n + (half + 1) * n)
                nc.vector.tensor_copy(K["STf" if half == 0 else "STb"][:, 0:ACC], acc[:, 0:ACC])\
                    .then_inc(S["half_out"].sem, 1)

        @block.scalar
        def _(act):
            for half in range(2):
                def batch(b, h, i):
                    need(act, S["attr_turned"], b + 1, half * n)
                    for k, (s, e) in enumerate(PARTS):
                        w = (e - s) * EAD
                        last = nc.scalar.activation(attrT[0:w, h, k, :], bank[0:w, k * P:(k + 1) * P], ACT.Copy)
                    last.then_inc(S["attr_back"].sem, 1)
                    for g, (s, e) in enumerate(GROUPS):
                        need(act, S["c_made"], NG * b + g + 1, half * NG * n)
                        nc.scalar.activation(msg[:, h, s:e, :], msg[:, h, s:e, :], ACT.Relu).then_inc(S["messages_made"].sem, 1)
                batches(act, bodies, batch)

        @block.tensor
        def _(pe):
            for half in range(2):
                if half:
                    pe.wait_ge(S["half_out"].sem, 1)
                clear_acc(nc, K, acc)

                def batch(b, h, i):
                    win = offsets(pe, tab, 1, half * (TH // B) + b, (NW - 1) * P)

                    def add(g):
                        s, e = GROUPS[g]
                        need(pe, S["messages_made"], NG * b + g + 1, half * NG * n)
                        for u in range(s, e):
                            last = nc.tensor.matmul(acc[:, ds(win[u], P)], msg[:, h, u, :], oh[:, h, u, :], start=False,
                                                    stop=True, skip_group_check=True)
                        return last
                    need(pe, attr_in[h], GATHERED * (i + 1), half * GATHERED * bodies)
                    need(pe, S["c_made"], NG * b, half * NG * n)
                    for k, (s, e) in enumerate(PARTS):
                        w = (e - s) * EAD
                        last = nc.tensor.transpose(bank[0:w, k * P:(k + 1) * P],
                                                   attr[:, h, s:e, :].rearrange("p t c -> p (t c)"), K["ident"][:, :])
                    last.then_inc(S["attr_turned"].sem, 1)
                    need(pe, S["attr_back"], b + 1, half * n)
                    for g, (s, e) in enumerate(GROUPS):
                        need(pe, S["c_made"], NG * b + g, half * NG * n)
                        for u in range(s, e):
                            k = u >= G0
                            w = (PARTS[k][1] - PARTS[k][0]) * EAD
                            last = nc.tensor.matmul(bank[:, (u - s) * F:(u - s + 1) * F], attrT[0:w, h, int(k), :],
                                                    K["w1e_wide"][0:w, half, u - PARTS[k][0], :], start=True, stop=True)
                        last.then_inc(S["h_made"].sem, 1)
                        if g == 1:
                            need(pe, S["onehot_made"], b + 1, half * n)
                        if g:
                            add(g - 1)
                    add(NG - 1).then_inc(S["summed"].sem, 1)
                batches(pe, bodies, batch)
    passed(S, summed=2 * n, c_made=2 * NG * n, messages_made=2 * NG * n)


def stage_output(nc, S, top, d, K, out):
    with Memory(nc) as m:
        Wf, Wb, Wu = (m.sb(n, [P, F]) for n in ("W2f", "W2b", "Wu"))
        rows = m.sb("rows_l3", [P, 3, F])
        eps = m.sb("eps", [P, 1])
        hb, Y = m.sb("h_base", [P, NWP, F]), m.sb("Y3", [P, NWP, F])
        degb = m.sb("deg_b", [P, NW])
        st = m.sb("node_stats", [P, 2, NW])
        sf, sb_, hT = (m.sb(n, [P, 2, F]) for n in ("windowf", "windowb", "hT"))
        h = m.sb("h", [P, 2, F])
        ps_h, ps_t, ps_o = (m.ps(n, [P, 2, 512]) for n in ("psum_h", "psum_hT", "psum_out"))
        block = m.block()
        X, Y25, hb25 = K["X"][:, 0:NW, :], Y[:, 0:NW, :], hb[:, 0:NW, :]
        loads = [(Wf[:, :], d["L3_gnn_W2f"]), (Wb[:, :], d["L3_gnn_W2b"]), (Wu[:, :], d["L3_gnn_Wu"]),
                 (eps[:, :], d["L3_gnn_eps"].rearrange("(o f) -> o f", o=1).to_broadcast([P, 1]))]
        loads += [(rows[:, i, :], d[f"L3_gnn_{n}"].rearrange("(o f) -> o f", o=1).to_broadcast([P, F]))
                  for i, n in enumerate(("b2f", "b2b", "bu"))]

        @block.sync
        def _(sp):
            for dst, src in loads:
                sp.dma_start(dst, src).then_inc(S["weights_in"].sem, 16)
            sp.wait_ge(S["output_made"].sem, 1)
            sp.dma_start(out[0:(NW - 1) * P, :].rearrange("(w p) f -> p w f", p=P), Y[:, 0:NW - 1, :])\
                .then_inc(S["output_stored"].sem, 16)
            sp.dma_start(out[(NW - 1) * P:N, :], Y[0:LAST, NW - 1, :]).then_inc(S["output_stored"].sem, 16)
            sp.wait_ge(S["output_stored"].sem, 32)

        @block.scalar
        def _(act):
            def body(i, first):
                for k in range(2):
                    n = 2 * i + k
                    w = ds(n * P, P)
                    if not first:
                        act.wait_ge(S["h_psum"].sem, n - 1)
                    nc.scalar.activation(sf[:, k, :], K["STf"][:, w], ACT.Copy)
                    nc.scalar.activation(sb_[:, k, :], K["STb"][:, w], ACT.Copy).then_inc(S["windows_copied"].sem, 1)
                for k in range(2):
                    n = 2 * i + k
                    act.wait_ge(S["h_turned"].sem, n + 1)
                    if not first:
                        act.wait_ge(S["out_psum"].sem, n - 1)
                    nc.scalar.activation(hT[:, k, :], ps_t[:, k, 0:F], ACT.Copy).then_inc(S["h_back"].sem, 1)
                for k in range(2):
                    n = 2 * i + k
                    act.wait_ge(S["out_psum"].sem, n + 1)
                    nc.scalar.activation(Y[:, ds(n, 1), :], ps_o[:, k, 0:F].unsqueeze(1), ACT.Copy)\
                        .then_inc(S["out_taken"].sem, 1)
            peeled(act, NWP // 2, body)
            root(nc, act, S, st[:, 1, :], 0)

        @block.tensor
        def _(pe):
            pe.wait_ge(S["weights_in"].sem, S["weights_in"].n + 16 * len(loads))

            def body(i, first):
                for k in range(2):
                    n = 2 * i + k
                    pe.wait_ge(S["windows_copied"].sem, n + 1)
                    if not first:
                        pe.wait_ge(S["h_summed"].sem, n - 1)
                    nc.tensor.matmul(ps_h[:, k, 0:F], sf[:, k, :], Wf[:, :], start=True, stop=False)
                    nc.tensor.matmul(ps_h[:, k, 0:F], sb_[:, k, :], Wb[:, :], start=False, stop=True)\
                        .then_inc(S["h_psum"].sem, 1)
                for k in range(2):
                    n = 2 * i + k
                    pe.wait_ge(S["h_summed"].sem, n + 1)
                    if not first:
                        pe.wait_ge(S["h_back"].sem, n - 1)
                    nc.tensor.transpose(ps_t[:, k, 0:F], h[:, k, :], K["ident"][:, :]).then_inc(S["h_turned"].sem, 1)
                for k in range(2):
                    n = 2 * i + k
                    pe.wait_ge(S["h_back"].sem, n + 1)
                    if not first:
                        pe.wait_ge(S["out_taken"].sem, n - 1)
                    nc.tensor.matmul(ps_o[:, k, 0:F], hT[:, k, :], Wu[:, :], start=True, stop=True)\
                        .then_inc(S["out_psum"].sem, 1)
            peeled(pe, NWP // 2, body)

        @block.vector
        def _(v):
            step = Chain(v, S["vector_steps"])
            v.wait_ge(S["weights_in"].sem, S["weights_in"].n + 16 * len(loads))
            step(nc.vector.memset(hb[:, NW:NWP, :], 0.0))
            step(nc.vector.tensor_scalar(eps[:, :], eps[:, :], 1.0, None, ALU.add))
            step(nc.vector.tensor_tensor(degb[:, :], K["deg"][:, :], K["deg_f"][:, :], ALU.subtract))
            step(nc.vector.tensor_tensor(hb25, over_f(K["deg_f"][:, :], NW), over_w(rows[:, 0, :], NW), ALU.mult))
            step(nc.vector.tensor_tensor(Y25, over_f(degb[:, :], NW), over_w(rows[:, 1, :], NW), ALU.mult))
            step(nc.vector.tensor_tensor(hb25, hb25, Y25, ALU.add))
            step(nc.vector.scalar_tensor_tensor(hb25, X, eps[:, 0:1], hb25, ALU.mult, ALU.add))

            def body(i, first):
                for k in range(2):
                    n = 2 * i + k
                    v.wait_ge(S["h_psum"].sem, n + 1)
                    if not first:
                        v.wait_ge(S["h_turned"].sem, n - 1)
                    nc.vector.tensor_tensor(h[:, k, :].unsqueeze(1), ps_h[:, k, 0:F].unsqueeze(1), hb[:, ds(n, 1), :], ALU.add)\
                        .then_inc(S["h_summed"].sem, 1)
            peeled(v, NWP // 2, body)
            v.wait_ge(S["out_taken"].sem, NWP)
            step(nc.vector.tensor_tensor(Y25, Y25, over_w(rows[:, 2, :], NW), ALU.add))
            step(nc.vector.scalar_tensor_tensor(Y25, Y25, 0.0, X, ALU.max, ALU.add))
            layer_norm(nc, v, step, S, Y25, hb25, st, 0)
            v.sem_inc(S["output_made"].sem, 1)
            step.end()


def build(nc, d, out):
    scratch = {
        "Q": [NWP * P, F],
        "rec0": [E + GAP, REC0], "rec1": [E + 2 * GAP, REC1], "rec1_given": [E, REC1],
        "tab0w": [1, T0], "tab1w": [1, T1],
        "c": [T0 // B, P, B * F],
        "H": [NWP * P, F], "Y": [NWP * P, R * F], "T3": [NWP * P, 2 * F],
    }
    for name, shape in scratch.items():
        d[name] = nc.dram_tensor(f"scratch_{name}", shape, F32).ap()
    for g, T in ((0, T0), (1, T1)):
        d[f"tab{g}"] = nc.dram_tensor(f"scratch_tab{g}", [3, T], I32).ap()
    with Memory(nc) as top:
        S = signals(nc, top.ctx)
        K = {name: top.sb(name, shape, dt) for name, shape, dt in [
            ("X", [P, NWP, F], F32),
            ("col", [P, NKEY], F32), ("row", [P, 1], F32), ("tile_no", [P, BODY], F32),
            ("col_b", [P, NKEY], BF16), ("ident_b", [P, P], BF16), ("ones", [P, P], F32), ("zeros", [P, 512], BF16), ("ident", [P, P], F32), ("before", [P, P], F32),
            ("before_half", [P, P], F32), ("half0", [P, 1], F32), ("half1", [P, 1], F32),
            ("in_half0", [P, P], F32), ("in_half1", [P, P], F32), ("valid", [P, NW], F32),
            ("W_l1T", [P, F], F32), ("gamma0", [P, F], F32), ("beta0", [P, F], F32), ("scale", [P, F], F32),
            ("stat", [P, 1, F], F32), ("one", [P, 1], F32), ("dinv", [P, NWP], F32),
            ("tab0", [3, T0 // B * BP], I32), ("tab1", [3, T1 // B * BP], I32), ("loc0", [P, T0], F32), ("loc1", [P, T1], F32),
            ("inv_count", [P, NKEY], F32), ("deg", [P, NW], F32), ("deg_f", [P, NW], F32), ("out_deg", [P, NW], F32),
        ]}
        with Memory(nc) as layer0:
            K["PN"] = layer0.sb("PN", [P, NWP, F])
            K["w1c_wide"] = layer0.sb("w1c_wide", [KA, G0, F], BF16)
            with Memory(nc) as front:
                stage_setup(nc, S, top, front, d, K)
                stage_sort(nc, S, top, front, d, K)
            K["PNf"] = K["PN"][:, :, :].rearrange("p w f -> p (w f)")
            stage_edge_mlp(nc, S, top, d, K)
        K["slots1"], K["weight"] = top.sb("slots1", [P, T1, REC0]), top.sb("edge_weight", [P, T1])
        with Memory(nc) as gcn:
            K["H"] = gcn.sb("H", [P, NWP, F])
            with Memory(nc) as sums:
                K["STf"] = K["ST"] = sums.sb("ST", [P, NWP * P])
                stage_edge_sum(nc, S, top, d, K)
                stage_nodes0(nc, S, top, d, K)
            K["ACC"] = gcn.sb("ACC", [P, ACC])
            stage_gcn(nc, S, top, d, K)
            K["ACC"] = K["ACC"][:, :]
            stage_nodes1(nc, S, top, d, K)
        stage_rgcn(nc, S, top, d, K)
        K["STf"], K["STb"] = top.sb("STf", [P, NWP * P]), top.sb("STb", [P, NWP * P])
        with Memory(nc) as directional:
            K["w1e_wide"] = directional.sb("w1e_wide", [G0 * EAD, 2, G0, F])
            stage_table3(nc, S, top, d, K)
            stage_directional(nc, S, top, d, K)
        stage_output(nc, S, top, d, K, out)


_OUT = (N, F)


def kernel(**inputs):
    import numpy as _np
    import concourse.bacc as _bacc
    from concourse.bass_utils import run_bass_kernel_spmd as _run

    nc = _bacc.Bacc("TRN2", target_bir_lowering=False, num_devices=1)
    arrays, d = {}, {}
    for name, value in inputs.items():
        a = _np.ascontiguousarray(value)
        arrays[f"in_{name}"] = a
        d[name] = nc.dram_tensor(f"in_{name}", a.shape, mybir.dt.from_np(a.dtype), kind="ExternalInput").ap()
    out = nc.dram_tensor("out_nodes", _OUT, F32, kind="ExternalOutput").ap()
    build(nc, d, out)
    r = _run(nc, [arrays], core_ids=[0])
    return r.results[0]["out_nodes"]
```
